# Optimizing a Trainium2 kernel written in Bass

```python
import numpy as np
import jax
import jax.numpy as jnp

def _softmax(x, axis=-1):
    return jax.nn.softmax(x, axis=axis)
def _gelu(x):
    return jax.nn.gelu(x, approximate=True)
def _silu(x):
    return jax.nn.silu(x)
def _sigmoid(x):
    return jax.nn.sigmoid(x)
def _layernorm(x, axis=-1, eps=1e-5):
    m = jnp.mean(x, axis=axis, keepdims=True)
    v = jnp.var(x, axis=axis, keepdims=True)
    return (x - m) / jnp.sqrt(v + eps)
def _scatter_add(tgt, idx, src, axis=0):
    return tgt.at[idx].add(src)
def _segment_sum(src, seg, n):
    return jax.ops.segment_sum(src, seg, n)

kernel_name = 'mk_adj_resnorm_d4_adj_128_a2f505'

def setup_inputs(seed: int = 0):
    np.random.seed(seed)
    _w = jnp.asarray
    def _rec_inputs():
        import jax
        import jax.numpy as jnp
        _gk = jax.random.key(seed)
        x = -0.000929 + 1 * jax.random.normal(jax.random.fold_in(_gk, 1), (4096, 128), jnp.float32)
        _a = jax.random.bernoulli(jax.random.fold_in(_gk, 2), 0.0078125, (4096, 4096))
        _af = _a.astype(jnp.float32)
        adj = _af
        return x, adj
    x, adj = _rec_inputs()
    def _L0_gnn_setup():
        import jax, jax.numpy as jnp
        import numpy as np
        N, D = (8192, 128)
        key = jax.random.key(seed)
        k1, k2, k3 = jax.random.split(key, 3)
        x = jax.random.normal(k1, (N, D), dtype=jnp.float32)
        adj = jax.random.randint(k2, (N, N), 0, 2).astype(jnp.float32)
        beta = jax.random.uniform(k3, (1,), dtype=jnp.float32)
        return {'x': x, 'adj': adj, 'beta': beta}
    _L0_gnn_all = _L0_gnn_setup()
    _L0_gnn_in = {k: v for k, v in _L0_gnn_all.items() if k in ('beta', )}
    del _L0_gnn_all

    def _L1_gnn_setup():
        import jax, jax.numpy as jnp
        import numpy as np
        N, D_IN, F1, F2, D_OUT = (10000, 128, 20, 20, 128)

        def _gcn(h, adj, W, b):
            return adj @ (h @ W) + b
        key = jax.random.key(seed)
        ks = jax.random.split(key, 8)
        x = jax.random.normal(ks[0], (N, D_IN), dtype=jnp.float32)
        adj = jax.random.uniform(ks[1], (N, N), dtype=jnp.float32)

        def glorot(k, fi, fo):
            s = 1.0 / np.sqrt(fi)
            return jax.random.uniform(k, (fi, fo), dtype=jnp.float32, minval=-s, maxval=s)
        W1 = glorot(ks[2], D_IN, F1)
        b1 = jnp.zeros((F1,), jnp.float32)
        W2 = glorot(ks[3], F1, F2)
        b2 = jnp.zeros((F2,), jnp.float32)
        W3 = glorot(ks[4], F2, D_OUT)
        b3 = jnp.zeros((D_OUT,), jnp.float32)
        return {'x': x, 'adj': adj, 'W1': W1, 'b1': b1, 'W2': W2, 'b2': b2, 'W3': W3, 'b3': b3}
    _L1_gnn_all = _L1_gnn_setup()
    _L1_gnn_in = {k: v for k, v in _L1_gnn_all.items() if k in ('W1', 'b1', 'W2', 'b2', 'W3', 'b3', )}
    del _L1_gnn_all

    def _L2_gnn_setup():
        import jax, jax.numpy as jnp
        import numpy as np
        C = 1.0
        EPS = 1e-15
        PROJ_EPS = 0.001
        ATANH_CLIP = 1e-05

        def _norm(x):
            return jnp.clip(jnp.linalg.norm(x, axis=-1, keepdims=True), EPS, None)

        def artanh(x):
            return jnp.arctanh(jnp.clip(x, -1.0 + ATANH_CLIP, 1.0 - ATANH_CLIP))

        def proj(x):
            n = _norm(x)
            maxnorm = (1.0 - PROJ_EPS) / jnp.sqrt(C)
            return jnp.where(n > maxnorm, x / n * maxnorm, x)

        def expmap0(u):
            sc = jnp.sqrt(C)
            n = _norm(u)
            return jnp.tanh(sc * n) * u / (sc * n)

        def logmap0(p):
            sc = jnp.sqrt(C)
            n = _norm(p)
            return artanh(sc * n) * p / (sc * n)

        def mobius_add(x, y):
            x2 = jnp.sum(x * x, -1, keepdims=True)
            y2 = jnp.sum(y * y, -1, keepdims=True)
            xy = jnp.sum(x * y, -1, keepdims=True)
            num = (1 + 2 * C * xy + C * y2) * x + (1 - C * x2) * y
            den = 1 + 2 * C * xy + C * C * x2 * y2
            return num / jnp.clip(den, EPS, None)

        def mobius_matvec(M, x):
            sc = jnp.sqrt(C)
            xn = _norm(x)
            mx = x @ M.T
            mxn = _norm(mx)
            res = jnp.tanh(mxn / xn * artanh(sc * xn)) * mx / (mxn * sc)
            return jnp.where(jnp.all(mx == 0, -1, keepdims=True), jnp.zeros_like(res), res)

        def lambda_x(x):
            return 2.0 / jnp.clip(1.0 - C * jnp.sum(x * x, -1, keepdims=True), EPS, None)

        def expmap(u, p):
            sc = jnp.sqrt(C)
            un = _norm(u)
            second = jnp.tanh(sc * lambda_x(p) * un / 2.0) * u / (sc * un)
            return mobius_add(p, second)

        def logmap(p1, p2):
            sc = jnp.sqrt(C)
            sub = mobius_add(-p1, p2)
            sn = _norm(sub)
            return 2.0 / (sc * lambda_x(p1)) * artanh(sc * sn) * sub / sn
        key = jax.random.key(seed)
        ks = jax.random.split(key, 7)
        N, D = (1024, 128)
        x = jax.random.normal(ks[0], (N, D), jnp.float32) * 0.01
        adj = jax.random.uniform(ks[1], (N, N), jnp.float32)
        W = jax.random.normal(ks[2], (D, D), jnp.float32) * 0.1
        b = jax.random.normal(ks[3], (D,), jnp.float32) * 0.01
        att_wl = jax.random.normal(ks[4], (D,), jnp.float32)
        att_wr = jax.random.normal(ks[5], (D,), jnp.float32)
        att_b = jax.random.normal(ks[6], (1,), jnp.float32)
        return {'x': x, 'adj': adj, 'W': W, 'b': b, 'att_wl': att_wl, 'att_wr': att_wr, 'att_b': att_b}
    _L2_gnn_all = _L2_gnn_setup()
    _L2_gnn_in = {k: v for k, v in _L2_gnn_all.items() if k in ('W', 'b', 'att_wl', 'att_wr', 'att_b', )}
    del _L2_gnn_all

    def _L3_gnn_setup():
        import jax, jax.numpy as jnp
        import numpy as np
        CUTOFF = 0.5
        key = jax.random.key(seed)
        k_z, k_d, k_w, k_mu, k_sg = jax.random.split(key, 5)
        N, D_IN, D_OUT = (8192, 128, 128)
        z = jax.random.normal(k_z, (N, D_IN), dtype=jnp.float32)
        dist_matrix = jax.random.uniform(k_d, (N, N), dtype=jnp.float32)
        W = jax.random.normal(k_w, (D_IN, D_OUT), dtype=jnp.float32)
        B = jnp.zeros((D_OUT,), dtype=jnp.float32)
        mu = jax.random.normal(k_mu, (1,), dtype=jnp.float32)
        sigma = jax.random.normal(k_sg, (1,), dtype=jnp.float32)
        return {'z': z, 'dist_matrix': dist_matrix, 'W': W, 'B': B, 'mu': mu, 'sigma': sigma}
    _L3_gnn_all = _L3_gnn_setup()
    _L3_gnn_in = {k: v for k, v in _L3_gnn_all.items() if k in ('W', 'B', 'mu', 'sigma', )}
    del _L3_gnn_all

    return {
        "x": x,
        "adj": adj,
        "L0_gnn_beta": _L0_gnn_in["beta"],
        "L1_gnn_W1": _L1_gnn_in["W1"],
        "L1_gnn_b1": _L1_gnn_in["b1"],
        "L1_gnn_W2": _L1_gnn_in["W2"],
        "L1_gnn_b2": _L1_gnn_in["b2"],
        "L1_gnn_W3": _L1_gnn_in["W3"],
        "L1_gnn_b3": _L1_gnn_in["b3"],
        "L2_gnn_W": _L2_gnn_in["W"],
        "L2_gnn_b": _L2_gnn_in["b"],
        "L2_gnn_att_wl": _L2_gnn_in["att_wl"],
        "L2_gnn_att_wr": _L2_gnn_in["att_wr"],
        "L2_gnn_att_b": _L2_gnn_in["att_b"],
        "L3_gnn_W": _L3_gnn_in["W"],
        "L3_gnn_B": _L3_gnn_in["B"],
        "L3_gnn_mu": _L3_gnn_in["mu"],
        "L3_gnn_sigma": _L3_gnn_in["sigma"],
    }

def reference(x, adj, L0_gnn_beta, L1_gnn_W1, L1_gnn_b1, L1_gnn_W2, L1_gnn_b2, L1_gnn_W3, L1_gnn_b3, L2_gnn_W, L2_gnn_b, L2_gnn_att_wl, L2_gnn_att_wr, L2_gnn_att_b, L3_gnn_W, L3_gnn_B, L3_gnn_mu, L3_gnn_sigma):
    import jax
    import jax.numpy as jnp
    def _L0_gnn_ref(x, adj, beta):
        import jax, jax.numpy as jnp
        import numpy as np
        N, D = (8192, 128)
        norm2 = jnp.linalg.norm(x, axis=1, keepdims=True)
        cos = beta * (x @ x.T) / (norm2 @ norm2.T + 1e-07)
        masked = cos + (1.0 - adj) * -1000000000.0
        P = jax.nn.softmax(masked, axis=1)
        return P @ x

    def _L1_gnn_ref(x, adj, W1, b1, W2, b2, W3, b3):
        import jax, jax.numpy as jnp
        import numpy as np
        N, D_IN, F1, F2, D_OUT = (10000, 128, 20, 20, 128)

        def _gcn(h, adj, W, b):
            return adj @ (h @ W) + b
        h = jax.nn.relu(_gcn(x, adj, W1, b1))
        h = jax.nn.relu(_gcn(h, adj, W2, b2))
        h = jax.nn.relu(_gcn(h, adj, W3, b3))
        return jax.nn.relu(h + x)

    def _L2_gnn_ref(x, adj, W, b, att_wl, att_wr, att_b):
        import jax, jax.numpy as jnp
        import numpy as np
        C = 1.0
        EPS = 1e-15
        PROJ_EPS = 0.001
        ATANH_CLIP = 1e-05

        def _norm(x):
            return jnp.clip(jnp.linalg.norm(x, axis=-1, keepdims=True), EPS, None)

        def artanh(x):
            return jnp.arctanh(jnp.clip(x, -1.0 + ATANH_CLIP, 1.0 - ATANH_CLIP))

        def proj(x):
            n = _norm(x)
            maxnorm = (1.0 - PROJ_EPS) / jnp.sqrt(C)
            return jnp.where(n > maxnorm, x / n * maxnorm, x)

        def expmap0(u):
            sc = jnp.sqrt(C)
            n = _norm(u)
            return jnp.tanh(sc * n) * u / (sc * n)

        def logmap0(p):
            sc = jnp.sqrt(C)
            n = _norm(p)
            return artanh(sc * n) * p / (sc * n)

        def mobius_add(x, y):
            x2 = jnp.sum(x * x, -1, keepdims=True)
            y2 = jnp.sum(y * y, -1, keepdims=True)
            xy = jnp.sum(x * y, -1, keepdims=True)
            num = (1 + 2 * C * xy + C * y2) * x + (1 - C * x2) * y
            den = 1 + 2 * C * xy + C * C * x2 * y2
            return num / jnp.clip(den, EPS, None)

        def mobius_matvec(M, x):
            sc = jnp.sqrt(C)
            xn = _norm(x)
            mx = x @ M.T
            mxn = _norm(mx)
            res = jnp.tanh(mxn / xn * artanh(sc * xn)) * mx / (mxn * sc)
            return jnp.where(jnp.all(mx == 0, -1, keepdims=True), jnp.zeros_like(res), res)

        def lambda_x(x):
            return 2.0 / jnp.clip(1.0 - C * jnp.sum(x * x, -1, keepdims=True), EPS, None)

        def expmap(u, p):
            sc = jnp.sqrt(C)
            un = _norm(u)
            second = jnp.tanh(sc * lambda_x(p) * un / 2.0) * u / (sc * un)
            return mobius_add(p, second)

        def logmap(p1, p2):
            sc = jnp.sqrt(C)
            sub = mobius_add(-p1, p2)
            sn = _norm(sub)
            return 2.0 / (sc * lambda_x(p1)) * artanh(sc * sn) * sub / sn
        x = proj(x)
        h = proj(mobius_matvec(W, x))
        h = proj(mobius_add(h, proj(expmap0(b[None, :]))))
        h_t = logmap0(h)
        local_t = logmap(h[:, None, :], h[None, :, :])
        scores = h_t @ att_wl
        scores = scores[:, None] + (h_t @ att_wr)[None, :] + att_b[0]
        adj_att = jax.nn.sigmoid(scores) * adj
        support_t = jnp.einsum('ij,ijd->id', adj_att, local_t)
        h = proj(expmap(support_t, h))
        h = jax.nn.relu(logmap0(h))
        return proj(expmap0(h))

    def _L3_gnn_ref(z, dist_matrix, W, B, mu, sigma):
        import jax, jax.numpy as jnp
        import numpy as np
        CUTOFF = 0.5
        N = dist_matrix.shape[0]
        h = z @ W + B
        mask = (dist_matrix < CUTOFF) & ~jnp.eye(N, dtype=bool)
        r = jnp.where(mask, dist_matrix, 1.0)
        sens = jnp.exp(-(1.0 / r - 1.0 / mu[0]) ** 2 / (2.0 * sigma[0] ** 2))
        S = jnp.where(mask, sens, 0.0)
        return S @ h

    x = _layernorm(x + _L0_gnn_ref(x, adj, L0_gnn_beta), axis=-1)
    x = _layernorm(x + _L1_gnn_ref(x, adj, L1_gnn_W1, L1_gnn_b1, L1_gnn_W2, L1_gnn_b2, L1_gnn_W3, L1_gnn_b3), axis=-1)
    x = _layernorm(x + _L2_gnn_ref(x, adj, L2_gnn_W, L2_gnn_b, L2_gnn_att_wl, L2_gnn_att_wr, L2_gnn_att_b), axis=-1)
    x = _layernorm(x + _L3_gnn_ref(x, adj, L3_gnn_W, L3_gnn_B, L3_gnn_mu, L3_gnn_sigma), axis=-1)
    return x


_drawn_inputs = setup_inputs


def setup_inputs(seed=0):
    import zlib

    import numpy as np

    out = dict(_drawn_inputs(seed))
    spreads = {'L1_gnn_b1': (0.0, 0.1),
     'L1_gnn_b2': (0.0, 2.0),
     'L1_gnn_b3': (0.0, 2.0),
     'L3_gnn_B': (0.0, 0.1)}
    factors = {'L2_gnn_b': 64.0, 'L2_gnn_att_wl': 64.0, 'L2_gnn_att_wr': 8.0}
    for name, (base, spread) in spreads.items():
        noise = np.random.default_rng([zlib.crc32(name.encode()), seed]).standard_normal(out[name].shape)
        drawn = base * np.exp(spread * noise) if base else spread * noise
        out[name] = jnp.asarray(drawn.astype(out[name].dtype))
    for name, factor in factors.items():
        out[name] = (out[name] * factor).astype(out[name].dtype)
    return out
```

```python
from contextlib import ExitStack

import concourse.bass as bass
from concourse import mybir

F32 = mybir.dt.float32
BF16 = mybir.dt.bfloat16
FP8 = mybir.dt.float8e4
U8 = mybir.dt.uint8
ALU = mybir.AluOpType
ACT = mybir.ActivationFunctionType
AX = mybir.AxisListType

P = 128
CH = 512
COS_EPS = 1e-7
NO_NEIGHBOUR = 1e-30
TINY_NORM = 1e-13
LN_EPS = 1e-5
EPS = 1e-15
MAXNORM = 0.999
R_FLOOR = 1e-15
ATANH_MAX = 0.99999
V_MIN = 1.0 - ATANH_MAX * ATANH_MAX
LNW_MAX = -0.0
SCORE_MIN = -43.0
EDGE8 = 64.0
EDGE_PE = 2.0
CREDIT = 2


class Chain:

    def __init__(self, eng, sem):
        self.eng, self.sem, self.n = eng, sem, 0

    def mark(self, ins):
        ins.then_inc(self.sem, 1)
        self.n = self.n + 1
        return self.n

    def wait(self, n):
        self.eng.wait_ge(self.sem, n)

    def link(self, ins):
        self.wait(self.mark(ins))


def loop(eng, start, end, chains, body):
    at = [ch.n for ch, _ in chains]
    with eng.Fori(start, end) as i:
        for (ch, steps), n0 in zip(chains, at):
            ch.n = n0 + (i - start) * steps
        want = [ch.n for ch, _ in chains]
        body(i)
    for (ch, steps), n0 in zip(chains, at):
        ch.n = n0 + (end - start) * steps


def gnn_stack(nc, x, adj, beta, W1, b1, W2, b2, W3, b3, hW, hb, att_wl, att_wr, att_b,
              W, B, mu, sigma, out, LAYERS=4):
    import math

    N, D = x.shape
    F1 = W1.shape[1]
    NT = N // P
    NCH = N // CH
    KT = CH // P
    NP = NT // 2
    STG = 4
    NPC = NT // STG
    AUG = 12
    LNW_MAX = -math.log(V_MIN)
    LNW_MIN = 2.0 ** -23
    assert D == P and F1 == W2.shape[1] and W3.shape[0] == F1

    ctx = ExitStack()
    with ctx:
        def sb(name, shape, dt=F32):
            return ctx.enter_context(nc.sbuf_tensor(name, shape, dt))

        def sem(name):
            return ctx.enter_context(nc.semaphore(name))

        def dram(name, shape, dt=F32):
            return nc.dram_tensor(name, shape, dt, kind="Internal").ap()

        adjT = sb("adjT", [P, NT, N], FP8)
        adjU = adjT[:, :, :].bitcast(U8)
        A = sb("A", [P, NT, D])
        T = sb("T", [P, N])
        arena = sb("arena", [P, 42 * 256])
        ident = sb("ident", [P, P])
        identb = sb("identb", [P, P], BF16)
        not_i = sb("not_i", [P, P], BF16)
        ones = sb("ones", [P, P])
        NS = 30
        scal = sb("scal", [P, NS, NT])
        par = sb("par", [P, 16])
        PS = ctx.enter_context(nc.psum_tensor("PS", [P, 8, 512], F32))
        PSrow = PS[:, :, :].rearrange("p b (k f) -> p (b k) f", f=P)

        used = {}

        def S(name):
            if name not in used:
                used[name] = len(used)
                assert len(used) <= NS, name
            return scal[:, used[name], :]

        def area(start, size, dt=F32):
            return arena[:, start:start + size] if dt == F32 else arena[:, start:start + size].bitcast(dt)

        KW = 256
        R = area(0, 16 * KW).rearrange("p (t f) -> p t f", f=D)
        TMP = area(16 * KW, 16 * KW).rearrange("p (t f) -> p t f", f=D)
        X2 = area(32 * KW, 10 * KW)
        stage = [area(8 * KW * b, 8 * KW) for b in range(2)]
        stage4 = [s.rearrange("p (k x) -> p k x", k=KT) for s in stage]
        stage_hi = [s.bitcast(BF16).rearrange("p (k x two) -> p k x two", k=KT, two=2) for s in stage]
        rbuf = [area((16 + 4 * b) * KW, 4 * KW) for b in range(2)]
        ebuf = [area((24 + 4 * b) * KW, 4 * KW) for b in range(2)]
        acc0 = area(32 * KW, 4 * KW)
        rho_b = area(36 * KW, 2 * KW)
        osb = area(38 * KW, 2 * KW)
        mid = area(40 * KW, 2 * KW)
        hs1 = [area(KW * 4 * b, KW * 4, BF16)[:, 0:NT * 3 * F1].rearrange("p (t f) -> p t f", f=3 * F1)
               for b in range(2)]
        agg_sb = [area((8 + 2 * b) * KW, 2 * KW) for b in range(2)]
        h_sb = [area((12 + 2 * b) * KW, 2 * KW) for b in range(2)]
        stack = area(32 * KW, 2 * KW)
        w_small = area(34 * KW, 2 * KW)
        a2 = [area((16 + 4 * b) * KW, 4 * KW) for b in range(2)]
        b2b = [area((24 + 4 * b) * KW, 4 * KW) for b in range(2)]
        e2 = area(32 * KW, 4 * KW)
        sbrow = area(36 * KW, 2 * KW)
        augS = A[:, 0:16, :].rearrange("p t f -> p (t f)").bitcast(BF16)
        augM = A[:, 16:32, :].rearrange("p t f -> p (t f)").bitcast(BF16)
        augrows = [area((32 + k) * KW, NT * AUG // 2, BF16).rearrange("p (t a) -> p t a", a=AUG) for k in range(2)]
        uRow = X2[0:1, 8 * KW:8 * KW + CH]
        hs3 = [area(8 * KW * s, 8 * KW, BF16).rearrange("p (t f) -> p t f", f=D) for s in range(3)]

        numT_d = dram("numT", [P, N])
        row_d = dram("row_scalar", [NT, P])
        x_d = dram("x_spill", [P, NT * D])

        s = {n: sem(n) for n in (
            "x_loaded", "par_loaded", "const_ready", "const_done",
            "act_asked", "act_answered", "dve_step", "act_step", "pe_step",
            "pe_asked", "pe_answered", "copy_answered", "dma_asked", "dma_answered",
            "piece_in0", "piece_in1", "tp_ready", "tp_free",
            "cos_sum_ready", "cos_free", "guard_ready", "exp_ready", "masked_ready", "masked_used",
            "masked_added", "z_ready", "z_free", "out_bank_free", "osb_ready", "osb_stored",
            "rho_in", "rho_used", "z_loaded",
            "agg_ready", "agg_copied", "mixed_ready", "mixed_copied", "t20_ready", "split_ready", "mix_free",
            "dist_ready", "lnw_ready", "clip_ready", "score_ready", "soft_ready", "half_ready",
            "ln1p_ready", "artanh_ready", "expo_ready", "weight_exp_ready", "c_ready", "c_used", "u_bank_free",
            "uT_ready", "uT_copied", "srow_in", "srow_used", "o2_stored", "o2_copied",
            "mask_ready", "agg3_ready", "agg3_free", "out_stored", "spilled")}

        xv = x.rearrange("(t p) f -> p t f", p=P)
        adj_v = adj.rearrange("(c k i) (q x) -> c q i k x", k=KT, i=P, x=STG * P)

        def row(v):
            return v.rearrange("(a n) -> a n", a=1)

        BETA, NABS, ATTB, MU, SIG, Y2, GY, S0, T0, T1, B1C, B2C, B3C, T2 = range(14)

        block = ctx.enter_context(nc.Block())

        @block.sync
        def _(sp):
            asked = [0]

            def serve(fn, n=1):
                asked[0] += 1
                sp.wait_ge(s["dma_asked"], asked[0])
                fn().then_inc(s["dma_answered"], 16)

            sp.dma_start(A[:, :, :], xv).then_inc(s["x_loaded"], 16)
            for col, v in ((BETA, beta), (ATTB, att_b), (MU, mu), (SIG, sigma)):
                sp.dma_start(par[:, col:col + 1], v.partition_broadcast(P)).then_inc(s["par_loaded"], 16)
            for col, v, n in ((B1C, b1, F1), (B2C, b2, F1), (B3C, b3, D)):
                sp.dma_start(par[0:n, col:col + 1], v.rearrange("(n a) -> n a", a=1)).then_inc(s["par_loaded"], 16)

            serve(lambda: sp.dma_start(row_d, mid[0:NT, 0:P]))
            rows_flat = row_d.rearrange("t p -> (t p)")

            def pieces(cc, first):
                for q in range(NPC):
                    g = cc * NPC + q
                    sp.wait_ge(s["tp_ready"], 2 * g + 2)
                    sp.dma_start(stage4[q % 2], adj_v[bass.ds(cc, 1), q].rearrange("a i k x -> (a i) k x")
                                 if not first else adj_v[0, q]).then_inc(s[f"piece_in{q % 2}"], 16)

            def rho_load(c):
                sp.wait_ge(s["rho_used"], c + 1)
                sp.dma_start(rho_b, rows_flat[bass.ds(c * CH, CH)].partition_broadcast(P)).then_inc(s["rho_in"], 16)

            def store_out(c):
                sp.wait_ge(s["osb_ready"], c + 1)
                sp.dma_start(numT_d[:, bass.ds(c * CH, CH)], osb).then_inc(s["osb_stored"], 16)

            sp.wait_ge(s["dma_answered"], 16)
            sp.wait_ge(s["copy_answered"], 2)
            pieces(0, True)
            rho_load(0)
            with sp.Fori(0, NCH - 1) as c:
                pieces(c + 1, False)
                rho_load(c + 1)
                store_out(c)
            store_out(NCH - 1)
            sp.wait_ge(s["osb_stored"], 16 * NCH + 16)
            sp.dma_start(T[:, :], numT_d).then_inc(s["z_loaded"], 16)
            if LAYERS > 1:
                serve(lambda: sp.dma_start(w_small[:, 0:F1], W1))
                for l, (w, f) in enumerate(((W2, F1), (W3, D))):
                    for part in range(3):
                        serve(lambda: sp.dma_start(stack[part * F1:(part + 1) * F1, 64 + l * 64:64 + l * 64 + f], w))
            if LAYERS > 2:
                serve(lambda: sp.dma_start(x_d, A[:, :, :].rearrange("p t f -> p (t f)")))
                serve(lambda: sp.dma_start(X2[:, 0:P], hW))
                serve(lambda: sp.dma_start(X2[:, P:2 * P], hb.partition_broadcast(P)))
                serve(lambda: sp.dma_start(X2[:, 2 * P:3 * P], att_wl.partition_broadcast(P)))
                serve(lambda: sp.dma_start(X2[:, 3 * P:4 * P], att_wr.partition_broadcast(P)))
                serve(lambda: sp.dma_start(row_d, X2[0:NT, 4 * P:5 * P]))
                sp.wait_ge(s["dma_answered"], 16 * asked[0])

                def srow_load(c):
                    sp.wait_ge(s["srow_used"], c + 1)
                    sp.dma_start(sbrow, rows_flat[bass.ds(c * CH, CH)].partition_broadcast(P))\
                        .then_inc(s["srow_in"], 16)

                def store2(c):
                    sp.wait_ge(s["o2_copied"], c + 1)
                    sp.dma_start(numT_d[:, bass.ds(c * CH, CH)], osb).then_inc(s["o2_stored"], 16)

                srow_load(0)
                with sp.Fori(0, NCH - 1) as c:
                    srow_load(c + 1)
                    store2(c)
                store2(NCH - 1)
                sp.wait_ge(s["o2_stored"], 16 * NCH + 16)
                sp.dma_start(T[:, :], numT_d).then_inc(s["z_loaded"], 16)
                serve(lambda: sp.dma_start(T[:, :], x_d))
            if LAYERS > 3:
                serve(lambda: sp.dma_start(X2[:, 0:P], W))
                serve(lambda: sp.dma_start(X2[:, P:2 * P], B.partition_broadcast(P)))
            asked[0] += 1
            sp.wait_ge(s["dma_asked"], asked[0])
            sp.dma_start(out.rearrange("(t p) f -> p t f", p=P), A[:, :, :]).then_inc(s["out_stored"], 16)
            sp.wait_ge(s["out_stored"], 16)

        @block.gpsimd
        def _(pool):
            def step(n, ins):
                ins.then_inc(s["const_ready"], 1)
                pool.wait_ge(s["const_ready"], n)

            step(1, pool.memset(ident[:, :], 0.0))
            step(2, pool.memset(not_i[:, :], 1.0))
            step(3, pool.memset(ones[:, :], 1.0))
            step(4, pool.affine_select(out=ident[:, :], in_=ident[:, :], compare_op=ALU.not_equal, fill=1.0,
                                       base=0, pattern=[[-1, P]], channel_multiplier=1))
            step(5, pool.affine_select(out=not_i[:, :], in_=not_i[:, :], compare_op=ALU.not_equal, fill=0.0,
                                       base=0, pattern=[[-1, P]], channel_multiplier=1))
            pool.tensor_copy(identb[:, :], ident[:, :]).then_inc(s["const_done"], 1)

            def add(n, buf):
                pool.wait_ge(s["masked_ready"], n + 1)
                pool.wait_ge(s["masked_added"], n + CREDIT)
                pool.tensor_tensor(acc0, acc0, ebuf[buf], ALU.add).then_inc(s["masked_added"], 1)

            def chunk(c):
                pool.wait_ge(s["z_ready"], c + 1)
                pool.wait_ge(s["masked_ready"], c * NP + 1)
                pool.tensor_tensor(acc0, ebuf[0], ones[:, 0:1].to_broadcast([P, 2 * CH]), ALU.mult).then_inc(s["masked_added"], 1)
                add(c * NP + 1, 1)

                def pairs(m):
                    add(c * NP + 2 * m, 0)
                    add(c * NP + 2 * m + 1, 1)
                loop(pool, 1, NP // 2, [], pairs)

            pool.sem_inc(s["masked_added"], CREDIT)
            loop(pool, 0, NCH, [], chunk)

        @block.tensor
        def _(pe):
            asked = [0]
            copies = [0]

            def ask_wait():
                asked[0] += 1
                pe.wait_ge(s["pe_asked"], asked[0])

            def transposes(src, dst=None):
                for t in range(NT):
                    last = nc.tensor.transpose(PSrow[:, t, :], src(t), ident[:, :])
                return last

            def tile_T(t):
                return T[:, t * P:(t + 1) * P]

            pe.sem_inc(s["tp_ready"], 2 * CREDIT)
            pe.sem_inc(s["masked_used"], CREDIT)
            pe.sem_inc(s["z_ready"], 1)
            pe.wait_ge(s["const_done"], 1)
            ask_wait()
            nc.tensor.transpose(PS[0:NT, 7, 0:P], S("rho"), ident[:, :]).then_inc(s["pe_answered"], 1)
            ask_wait()
            pe.wait_ge(s["copy_answered"], 1)
            transposes(lambda t: R[:, t, :]).then_inc(s["pe_answered"], 1)
            pe.wait_ge(s["copy_answered"], 2)

            def build(c, jp):
                tp = PS[:, 4 + jp % 2, :].bitcast(BF16).rearrange("p (j x) -> p j x", j=2)
                q = jp // 2
                if jp % 2 == 0:
                    pe.wait_ge(s[f"piece_in{q % 2}"], 16 * (c * (NPC // 2) + q // 2 + 1))
                pe.wait_ge(s["tp_free"], c * NP + jp + 1)
                for jj in range(2):
                    J = 2 * jp + jj
                    for k in range(KT):
                        last = nc.tensor.transpose(tp[:, jj, k * P:(k + 1) * P],
                                                   stage_hi[q % 2][:, k, (J % STG) * P:(J % STG + 1) * P, 1],
                                                   identb[:, :])
                last.then_inc(s["tp_ready"], 1)

            def cosines(c, jp):
                n = c * NP + jp
                pe.wait_ge(s["cos_free"], n + 1)
                for jj in range(2):
                    J = 2 * jp + jj
                    last = nc.tensor.matmul(PS[:, 2 * (jp % 2) + jj, :], T[:, J * P:(J + 1) * P],
                                            T[:, bass.ds(c * CH, CH)], start=True, stop=True)
                last.then_inc(s["cos_sum_ready"], 1)

            def chunk0(c, more):
                cosines(c, 0)
                cosines(c, 1)
                for jp in range(NP):
                    if more:
                        build(c + 1, jp)
                    if jp == 0:
                        pe.wait_ge(s["out_bank_free"], c + 1)
                    pe.wait_ge(s["masked_ready"], c * NP + jp + 1)
                    for jj in range(2):
                        J = 2 * jp + jj
                        last = nc.tensor.matmul(PS[:, 6, :], A[:, J, :], ebuf[jp % 2][:, jj * CH:(jj + 1) * CH],
                                                start=(J == 0), stop=(J == NT - 1))
                    last.then_inc(s["masked_used"], 1)
                    if jp + 2 < NP:
                        cosines(c, jp + 2)
                pe.wait_ge(s["masked_added"], (c + 1) * NP + CREDIT)
                pe.wait_ge(s["z_free"], c + 1)
                for k in range(KT):
                    for half in range(2):
                        last = nc.tensor.matmul(PS[:, 7, k:k + 1], acc0[:, half * CH + k * P:half * CH + (k + 1) * P],
                                                ones[:, 0:1], start=(half == 0), stop=(half == 1))
                last.then_inc(s["z_ready"], 1)

            for jp in range(NP):
                build(0, jp)
            with pe.Fori(0, NCH - 1) as c:
                chunk0(c, True)
            chunk0(NCH - 1, False)

            ask_wait()
            for t in range(NT):
                last = nc.tensor.matmul(PS[:, 0, 0:P], ones[:, :], A[:, t, :], start=(t == 0), stop=(t == NT - 1))
            last.then_inc(s["pe_answered"], 1)
            ask_wait()
            pe.wait_ge(s["z_loaded"], 16)
            transposes(tile_T).then_inc(s["pe_answered"], 1)

            if LAYERS > 1:
                ask_wait()
                transposes(lambda t: A[:, t, :]).then_inc(s["pe_answered"], 1)
                ask_wait()
                pe.wait_ge(s["copy_answered"], 3)
                for t in range(NT):
                    last = nc.tensor.matmul(PS[:, t // 4, (t % 4) * F1:(t % 4 + 1) * F1], tile_T(t), w_small[:, 0:F1],
                                            start=True, stop=True)
                last.then_inc(s["pe_answered"], 1)
                pe.sem_inc(s["t20_ready"], CREDIT)
                for l in range(3):
                    F = D if l == 2 else F1
                    wl = stack[0:3 * F1, (0, 64, 128)[l]:(0, 64, 128)[l] + F]
                    hs = hs1[l % 2]

                    def agg(c, half):
                        pe.wait_ge(s["agg_copied"], l * NCH + c + 1)
                        for J in range(NT):
                            last = nc.tensor.matmul(PS[0:3 * F1, half, :], hs[:, J, :],
                                                    adjT[:, J, c * CH:(c + 1) * CH],
                                                    start=(J == 0), stop=(J == NT - 1))
                        last.then_inc(s["agg_ready"], 1)

                    def mix(c, half):
                        pe.wait_ge(s["agg_copied"], l * NCH + c + 1 + CREDIT)
                        pe.wait_ge(s["mixed_copied"], l * NCH + c + 1)
                        nc.tensor.matmul(PS[0:F, 2 + half, :], wl, agg_sb[half][0:3 * F1, :],
                                         start=True, stop=True).then_inc(s["mixed_ready"], 1)
                        if l < 2:
                            pe.wait_ge(s["mixed_copied"], l * NCH + c + 1 + CREDIT)
                            pe.wait_ge(s["split_ready"], l * NCH + c + 1)
                            for k in range(KT):
                                last = nc.tensor.transpose(PS[:, 4 + half, k * F1:(k + 1) * F1],
                                                           h_sb[half][0:F1, k * P:(k + 1) * P], ident[0:F1, 0:F1])
                            last.then_inc(s["t20_ready"], 1)

                    pe.wait_ge(s["split_ready"], CREDIT + l * NCH)
                    agg(0, 0)
                    for c in range(1, NCH):
                        agg(c, c % 2)
                        mix(c - 1, (c - 1) % 2)
                    mix(NCH - 1, 1)
                ask_wait()
                transposes(tile_T).then_inc(s["pe_answered"], 1)

            if LAYERS > 2:
                ask_wait()
                nc.tensor.transpose(PS[:, 0, 0:P], X2[:, 0:P], ident[:, :]).then_inc(s["pe_answered"], 1)
                ask_wait()
                transposes(lambda t: R[:, t, :]).then_inc(s["pe_answered"], 1)
                ask_wait()
                pe.wait_ge(s["copy_answered"], 4)
                for t in range(NT):
                    last = nc.tensor.matmul(PSrow[:, t, :], tile_T(t), X2[:, 5 * P:6 * P], start=True, stop=True)
                last.then_inc(s["pe_answered"], 1)
                ask_wait()
                transposes(lambda t: R[:, t, :]).then_inc(s["pe_answered"], 1)
                ask_wait()
                pe.wait_ge(s["copy_answered"], 5)
                nc.tensor.transpose(PS[0:NT, 7, 0:P], S("sc_i"), ident[:, :]).then_inc(s["pe_answered"], 1)
                for aug in range(2):
                    ask_wait()
                    for t in range(NT):
                        last = nc.tensor.transpose(PS[:, :, :].bitcast(BF16).rearrange("p b f -> p (b f)")
                                                   [0:AUG, t * P:(t + 1) * P],
                                                   augrows[aug][:, t, :], identb[:, :])
                    last.then_inc(s["pe_answered"], 1)
                ask_wait()
                pe.sem_inc(s["pe_answered"], 1)
                pe.sem_inc(s["c_used"], CREDIT)

                def dist(c, jp):
                    n = c * NP + jp
                    pe.wait_ge(s["weight_exp_ready"], n + 1)
                    for jj in range(2):
                        J = 2 * jp + jj
                        o = PS[:, 2 * (jp % 2) + jj, :]
                        nc.tensor.matmul(o, T[:, J * P:(J + 1) * P], T[:, bass.ds(c * CH, CH)],
                                         start=True, stop=False)
                        last = nc.tensor.matmul(o, augS[:, J * P:(J + 1) * P], augM[:, bass.ds(c * CH, CH)],
                                                start=False, stop=True)
                    last.then_inc(s["dist_ready"], 1)

                with pe.Fori(0, NCH) as c:
                    dist(c, 0)
                    dist(c, 1)
                    for jp in range(NP):
                        if jp == 0:
                            pe.wait_ge(s["uT_copied"], c + 1)
                        pe.wait_ge(s["c_ready"], c * NP + jp + 1 + CREDIT)
                        for jj in range(2):
                            J = 2 * jp + jj
                            cm = b2b[jp % 2][:, jj * CH:(jj + 1) * CH]
                            nc.tensor.matmul(PS[:, 6, :], R[:, J, :], cm, start=(J == 0), stop=(J == NT - 1))
                            last = nc.tensor.matmul(PS[0:1, 7, :], S("ub")[:, J:J + 1], cm,
                                                    start=(J == 0), stop=(J == NT - 1))
                        last.then_inc(s["c_used"], 1)
                        if jp + 2 < NP:
                            dist(c, jp + 2)
                    pe.wait_ge(s["u_bank_free"], c + 1)
                    for k in range(KT):
                        last = nc.tensor.matmul(PS[:, 6, k:k + 1], uRow[:, k * P:(k + 1) * P], ones[0:1, 0:1],
                                                start=True, stop=True)
                    last.then_inc(s["uT_ready"], 1)
                ask_wait()
                pe.wait_ge(s["z_loaded"], 32)
                transposes(tile_T).then_inc(s["pe_answered"], 1)

            if LAYERS > 3:
                ask_wait()
                transposes(lambda t: A[:, t, :]).then_inc(s["pe_answered"], 1)
                ask_wait()
                pe.wait_ge(s["copy_answered"], 9)
                for t in range(NT):
                    last = nc.tensor.matmul(PSrow[:, t, :], tile_T(t), X2[:, 0:P], start=True, stop=True)
                last.then_inc(s["pe_answered"], 1)
                ask_wait()
                pe.sem_inc(s["pe_answered"], 1)

                def agg3(c, half):
                    pe.wait_ge(s["agg3_free"], c + 1)
                    pe.wait_ge(s["mask_ready"], c + 1)
                    for part in range(3):
                        for J in range(NT):
                            last = nc.tensor.matmul(PS[:, half, :], hs3[part][:, J, :],
                                                    adjT[:, J, c * CH:(c + 1) * CH],
                                                    start=(J == 0 and part == 0), stop=(J == NT - 1 and part == 2))
                    last.then_inc(s["agg3_ready"], 1)

                for c in range(NCH):
                    agg3(c, c % 2)
                ask_wait()
                transposes(tile_T).then_inc(s["pe_answered"], 1)

        @block.scalar
        def _(act):
            asked = [0]
            steps = Chain(act, s["act_step"])

            def fn(out_, in_, func, **kw):
                asked[0] += 1
                act.wait_ge(s["act_asked"], asked[0])
                nc.scalar.activation(out_, in_, func, **kw).then_inc(s["act_answered"], 1)

            pes = [0]

            def pe_copy(n, dst, src):
                act.wait_ge(s["pe_answered"], n)
                nc.scalar.copy(dst, src).then_inc(s["copy_answered"], 1)

            def sqrt(name):
                fn(S("y0"), S(name), ACT.Sqrt)

            sqrt("ss")
            pe_copy(1, mid[0:NT, 0:P], PS[0:NT, 7, 0:P])
            pe_copy(2, T[:, :], PS[:, :, :].rearrange("p b f -> p (b f)"))

            def guard(c, jp, par_, tile):
                n = c * NP + jp
                act.wait_ge(s["cos_free"], n + 1)
                for jj in range(2):
                    steps.mark(nc.scalar.activation(rbuf[par_][:, jj * CH:(jj + 1) * CH], rho_b, ACT.Ln,
                                                    scale=S("erho")[:, bass.ds(2 * jp + jj, 1)], bias=1.0))
                steps.wait(steps.n)
                nc.scalar.activation(rbuf[par_], rbuf[par_], ACT.Exp, scale=-1.0).then_inc(s["guard_ready"], 1)

            def exps(c, jp, par_):
                act.wait_ge(s["cos_free"], c * NP + jp + 1 + CREDIT)
                nc.scalar.activation(ebuf[par_], ebuf[par_], ACT.Exp, scale=par[:, BETA:BETA + 1],
                                     bias=par[:, NABS:NABS + 1]).then_inc(s["exp_ready"], 1)

            def chunk0(c):
                act.wait_ge(s["rho_in"], 16 * (c + 1))
                guard(c, 0, 0, 0)
                guard(c, 1, 1, 1)

                def pairs(m):
                    for h in range(2):
                        exps(c, 2 * m + h, h)
                        guard(c, 2 * m + 2 + h, h, 0)
                loop(act, 0, NP // 2 - 1, [(steps, 4)], pairs)
                act.wait_ge(s["guard_ready"], (c + 1) * NP)
                act.sem_inc(s["rho_used"], 1)
                for h in range(2):
                    exps(c, NP - 2 + h, h)
                act.wait_ge(s["masked_used"], (c + 1) * NP + CREDIT)
                act.wait_ge(s["osb_stored"], 16 * c + 16)
                nc.scalar.copy(osb, PS[:, 6, :]).then_inc(s["osb_ready"], 1)
                act.wait_ge(s["osb_ready"], c + 1)
                act.sem_inc(s["out_bank_free"], 1)

            act.sem_inc(s["rho_used"], 1)
            act.sem_inc(s["out_bank_free"], 1)
            act.sem_inc(s["osb_stored"], 16)
            act.wait_ge(s["const_done"], 1)
            nc.scalar.preload_act_table_set("natural_log_exp_and_others")
            loop(act, 0, NCH, [(steps, 2 * NP)], chunk0)
            sqrt("var")
            if LAYERS > 1:
                pe_copy(5, T[:, :], PS[:, :, :].rearrange("p b f -> p (b f)"))
                act.sem_inc(s["agg_copied"], CREDIT)
                act.sem_inc(s["mixed_copied"], CREDIT)
                for l in range(3):
                    F = D if l == 2 else F1
                    bias = par[0:F, (B1C, B2C, B3C)[l]:(B1C, B2C, B3C)[l] + 1]

                    def agg_copy(c, half):
                        act.wait_ge(s["agg_ready"], l * NCH + c + 1)
                        nc.scalar.copy(agg_sb[half][0:3 * F1, :], PS[0:3 * F1, half, :])\
                            .then_inc(s["agg_copied"], 1)

                    def relu(c, half):
                        act.wait_ge(s["mixed_ready"], l * NCH + c + 1)
                        if l < 2:
                            act.wait_ge(s["t20_ready"], l * NCH + c + 1)
                            dst = h_sb[half][0:F, :]
                        else:
                            dst = T[:, bass.ds(c * CH, CH)]
                        nc.scalar.activation(dst, PS[0:F, 2 + half, :], ACT.Relu, bias=bias)\
                            .then_inc(s["mixed_copied"], 1)

                    agg_copy(0, 0)
                    with act.Fori(0, NCH // 2 - 1) as m:
                        agg_copy(2 * m + 1, 1)
                        relu(2 * m, 0)
                        agg_copy(2 * m + 2, 0)
                        relu(2 * m + 1, 1)
                    agg_copy(NCH - 1, 1)
                    relu(NCH - 2, 0)
                    relu(NCH - 1, 1)
                sqrt("var")
            if LAYERS > 2:
                sqrt("ss")
                pe_copy(9, T[:, :], PS[:, :, :].rearrange("p b f -> p (b f)"))
                sqrt("ss")
                sqrt("ss")
                fn(S("y1"), S("y0"), ACT.Ln, bias=1.0)
                fn(S("y2"), S("y0"), ACT.Ln, scale=-1.0, bias=1.0)
                fn(S("y0"), S("y1"), ACT.Tanh)
                fn(S("y2"), S("y1"), ACT.Tanh)
                sqrt("ss")
                fn(S("y1"), S("y0"), ACT.Ln, bias=1.0)
                fn(S("y2"), S("y0"), ACT.Ln, scale=-1.0, bias=1.0)
                pe_copy(11, T[:, :], PS[:, :, :].rearrange("p b f -> p (b f)"))
                pe_copy(12, X2[0:NT, 4 * P:5 * P], PS[0:NT, 7, 0:P])
                for k, dst in enumerate((augS, augM)):
                    pe_copy(13 + k, dst[0:AUG, :],
                            PS[:, :, :].bitcast(BF16).rearrange("p b f -> p (b f)")[0:AUG, 0:N])

                def lnw(c, jp, par_):
                    act.wait_ge(s["dist_ready"], c * NP + jp + 1)
                    act.wait_ge(s["c_ready"], c * NP + jp + 1)
                    nc.scalar.activation(a2[par_], PS[:, 2 * par_:2 * par_ + 2, :].rearrange("p b f -> p (b f)"),
                                         ACT.Ln, scale=-2.0).then_inc(s["lnw_ready"], 1)

                f = PS[:, 4:6, :].rearrange("p b f -> p (b f)")

                def soft_exp(c, jp):
                    act.wait_ge(s["score_ready"], c * NP + jp + 1)
                    return steps.mark(nc.scalar.activation(f, f, ACT.Exp, scale=-1.0))

                def soft_ln(c, jp, after):
                    steps.wait(after)
                    nc.scalar.activation(f, f, ACT.Ln, bias=1.0).then_inc(s["soft_ready"], 1)

                def pair(c, jp, par_, more):
                    n = c * NP + jp
                    w = PS[:, 2 * par_:2 * par_ + 2, :].rearrange("p b f -> p (b f)")
                    act.wait_ge(s["clip_ready"], n + 1)
                    k = steps.mark(nc.scalar.activation(w, b2b[par_], ACT.Exp, scale=-1.0))
                    steps.wait(k)
                    k = steps.mark(nc.scalar.activation(w, w, ACT.Ln, scale=-1.0, bias=1.0))
                    steps.wait(k)
                    act.wait_ge(s["artanh_ready"], n + 1)
                    nc.scalar.activation(e2, w, ACT.Exp, scale=0.5).then_inc(s["half_ready"], 1)
                    if more:
                        k2 = soft_exp(c, jp + 1)
                    act.wait_ge(s["half_ready"], n + 1)
                    nc.scalar.activation(e2, e2, ACT.Ln, bias=1.0).then_inc(s["ln1p_ready"], 1)
                    if more:
                        soft_ln(c, jp + 1, k2)
                        lnw(c, jp + 1, 1 - par_)
                    act.wait_ge(s["expo_ready"], n + 1)
                    nc.scalar.activation(a2[par_], a2[par_], ACT.Exp, scale=-1.0).then_inc(s["weight_exp_ready"], 1)

                def chunk2(c):
                    k = soft_exp(c, 0)
                    soft_ln(c, 0, k)
                    lnw(c, 0, 0)

                    def pairs(m):
                        for h in range(2):
                            pair(c, 2 * m + h, h, True)
                    loop(act, 0, NP // 2 - 1, [(steps, 6)], pairs)
                    pair(c, NP - 2, 0, True)
                    pair(c, NP - 1, 1, False)
                    act.wait_ge(s["c_used"], (c + 1) * NP + CREDIT)
                    act.wait_ge(s["o2_stored"], 16 * c + 16)
                    nc.scalar.copy(osb, PS[:, 6, :]).then_inc(s["o2_copied"], 1)
                    act.wait_ge(s["o2_copied"], c + 1)
                    nc.scalar.copy(uRow, PS[0:1, 7, :]).then_inc(s["u_bank_free"], 1)

                act.sem_inc(s["weight_exp_ready"], CREDIT)
                act.sem_inc(s["o2_stored"], 16)
                act.sem_inc(s["srow_used"], 1)
                nc.scalar.preload_act_table_set("natural_log_exp_and_others")
                loop(act, 0, NCH, [(steps, 3 * NP)], chunk2)
                sqrt("ss")
                fn(S("y0"), S("y1"), ACT.Tanh)
                sqrt("ss")
                fn(S("y1"), S("y0"), ACT.Ln, bias=1.0)
                fn(S("y2"), S("y0"), ACT.Ln, scale=-1.0, bias=1.0)
                sqrt("ss")
                fn(S("y0"), S("y1"), ACT.Tanh)
                sqrt("var")
            if LAYERS > 3:
                pe_copy(17, T[:, :], PS[:, :, :].rearrange("p b f -> p (b f)"))
                fn(par[:, T1:T1 + 1], par[:, T0:T0 + 1], ACT.Square)
                fn(par[:, S0:S0 + 1], par[:, T2:T2 + 1], ACT.Exp)

                def out3(c, half):
                    act.wait_ge(s["agg3_ready"], c + 1)
                    nc.scalar.copy(T[:, bass.ds(c * CH, CH)], PS[:, half, :]).then_inc(s["agg3_free"], 1)

                act.sem_inc(s["agg3_free"], CREDIT)
                with act.Fori(0, NCH // 2) as m:
                    out3(2 * m, 0)
                    out3(2 * m + 1, 1)
                sqrt("var")

        @block.vector
        def _(dve):
            steps = Chain(dve, s["dve_step"])
            link = steps.link
            V = nc.vector
            n_act, n_pe, n_dma = [0], [0], [0]

            def bc(sc):
                return sc.unsqueeze(2).to_broadcast([P, NT, D])

            def bf(v):
                return v.unsqueeze(1).to_broadcast([P, NT, D])

            def act_do():
                n_act[0] += 1
                dve.sem_inc(s["act_asked"], 1)
                dve.wait_ge(s["act_answered"], n_act[0])

            def pe_do(wait=True):
                n_pe[0] += 1
                dve.sem_inc(s["pe_asked"], 1)
                if wait:
                    dve.wait_ge(s["pe_answered"], n_pe[0])

            def dma_do(wait=True):
                n_dma[0] += 1
                dve.sem_inc(s["dma_asked"], 1)
                if wait:
                    dve.wait_ge(s["dma_answered"], 16 * n_dma[0])

            def tt(o, a, b, op):
                link(V.tensor_tensor(o, a, b, op))

            def ts(o, a, s1, op0, s2=None, op1=ALU.bypass):
                link(V.tensor_scalar(o, a, s1, s2, op0, op1))

            def stt(o, a, sc, b, op0, op1):
                link(V.scalar_tensor_tensor(out=o, in0=a, scalar=sc, in1=b, op0=op0, op1=op1))

            def rec(o, a):
                link(V.reciprocal(o, a))

            def sum_of_products(name, a, b, tmp):
                tt(tmp, a, b, ALU.mult)
                link(V.tensor_reduce(S(name), tmp, AX.X, ALU.add))

            def sqrt(dst, name):
                act_do()
                rec(S("y1"), S("y0"))
                tt(S("y1"), S("y1"), S(name), ALU.mult)
                tt(S("y0"), S("y0"), S("y1"), ALU.add)
                ts(dst, S("y0"), 0.5, ALU.mult)

            def layer_norm(src, tmp):
                link(V.tensor_reduce(S("mean"), src, AX.X, ALU.add))
                ts(S("mean"), S("mean"), 1.0 / D, ALU.mult)
                tt(src, src, bc(S("mean")), ALU.subtract)
                sum_of_products("var", src, src, tmp)
                ts(S("var"), S("var"), 1.0 / D, ALU.mult, LN_EPS, ALU.add)
                sqrt(S("rstd"), "var")
                rec(S("rstd"), S("rstd"))
                tt(A[:, :, :], src, bc(S("rstd")), ALU.mult)

            def split3(dst, src, rest):
                link(V.tensor_copy(dst[0], src))
                tt(rest, src, dst[0], ALU.subtract)
                link(V.tensor_copy(dst[1], rest))
                tt(rest, rest, dst[1], ALU.subtract)
                link(V.tensor_copy(dst[2], rest))

            dve.wait_ge(s["x_loaded"], 16)
            sum_of_products("ss", A[:, :, :], A[:, :, :], R)
            ts(S("ss"), S("ss"), TINY_NORM ** 2, ALU.max)
            sqrt(S("rho"), "ss")
            rec(S("rho"), S("rho"))
            ts(S("erho"), S("rho"), COS_EPS, ALU.mult)
            tt(R, A[:, :, :], bc(S("rho")), ALU.mult)
            dve.wait_ge(s["par_loaded"], 16 * 7)
            ts(par[:, T0:T0 + 1], par[:, BETA:BETA + 1], -1.0, ALU.mult)
            tt(par[:, NABS:NABS + 1], par[:, T0:T0 + 1], par[:, BETA:BETA + 1], ALU.min)
            dve.wait_ge(s["const_done"], 1)
            pe_do()
            dve.wait_ge(s["copy_answered"], 1)
            dma_do(False)
            pe_do()

            def evacuate(c, jp, par_):
                n = c * NP + jp
                dve.wait_ge(s["tp_ready"], n + 1 + 2 * CREDIT)
                V.tensor_scalar(adjU[:, bass.ds(2 * jp, 2), bass.ds(c * CH, CH)],
                                PS[:, 4 + par_, :].bitcast(BF16).rearrange("p (j x) -> p j x", j=2),
                                EDGE8, None, ALU.mult).then_inc(s["tp_free"], 1)

            def product(c, jp, par_):
                n = c * NP + jp
                dve.wait_ge(s["cos_sum_ready"], n + 1)
                dve.wait_ge(s["guard_ready"], n + 1)
                dve.wait_ge(s["masked_used"], n + 1)
                dve.wait_ge(s["masked_added"], n + 1)
                V.tensor_tensor(ebuf[par_], PS[:, 2 * par_:2 * par_ + 2, :].rearrange("p b f -> p (b f)"),
                                rbuf[par_], ALU.mult).then_inc(s["cos_free"], 1)

            def mask(c, jp, par_):
                dve.wait_ge(s["exp_ready"], c * NP + jp + 1)
                e = ebuf[par_].rearrange("p (j x) -> p j x", j=2)
                V.tensor_tensor(e, e, adjU[:, bass.ds(2 * jp, 2), bass.ds(c * CH, CH)], ALU.mult)\
                    .then_inc(s["masked_ready"], 1)

            def chunk0(c, more):
                dve.wait_ge(s["tp_free"], (c + 1) * NP + CREDIT)
                product(c, 0, 0)

                def pairs(m):
                    for h in range(2):
                        product(c, 2 * m + h + 1, 1 - h)
                        if more:
                            evacuate(c + 1, 2 * m + h, h)
                        mask(c, 2 * m + h, h)
                loop(dve, 0, NP // 2 - 1, [], pairs)
                product(c, NP - 1, 1)
                for h in range(2):
                    if more:
                        evacuate(c + 1, NP - 2 + h, h)
                    mask(c, NP - 2 + h, h)
                dve.wait_ge(s["z_ready"], c + 2)
                V.tensor_copy(S("z")[:, bass.ds(c * KT, KT)], PS[:, 7, 0:KT]).then_inc(s["z_free"], 1)

            dve.sem_inc(s["tp_free"], CREDIT)
            dve.sem_inc(s["cos_free"], CREDIT)
            dve.sem_inc(s["z_free"], 1)
            with dve.Fori(0, NP // 2) as m:
                for h in range(2):
                    evacuate(0, 2 * m + h, h)
            with dve.Fori(0, NCH - 1) as c:
                chunk0(c, True)
            chunk0(NCH - 1, False)
            dve.wait_ge(s["z_free"], NCH + 1)
            pe_do()
            csum = X2[:, 0:P]
            ts(csum, PS[:, 0, 0:P], EDGE8 * NO_NEIGHBOUR, ALU.mult)
            pe_do()
            ts(S("z"), S("z"), EDGE8 * NO_NEIGHBOUR * N, ALU.add)
            rec(S("z"), S("z"))
            tt(R, PSrow, bf(csum), ALU.add)
            tt(R, R, bc(S("z")), ALU.mult)
            tt(R, R, A[:, :, :], ALU.add)
            layer_norm(R, TMP)

            if LAYERS > 1:
                for _ in range(7):
                    dma_do()
                pe_do()
                dve.wait_ge(s["copy_answered"], 3)
                pe_do()
                v = PS[:, :, 0:4 * F1].rearrange("p b (k f) -> p b k f", f=F1)
                rest = TMP.rearrange("p t f -> p (t f)")[:, 0:NT * F1].rearrange("p (b k f) -> p b k f", k=4, f=F1)
                hv = hs1[0].rearrange("p (b k) f -> p b k f", k=4)
                split3([hv[:, :, :, q * F1:(q + 1) * F1] for q in range(3)], v, rest)
                tt(stack[0:3 * F1, 0:F1], ident[0:3 * F1, 0:F1], ident[0:3 * F1, F1:2 * F1], ALU.add)
                tt(stack[0:3 * F1, 0:F1], stack[0:3 * F1, 0:F1], ident[0:3 * F1, 2 * F1:3 * F1], ALU.add)
                ts(stack[0:3 * F1, 0:2 * P], stack[0:3 * F1, 0:2 * P], 1.0 / EDGE_PE, ALU.mult)
                dve.sem_inc(s["split_ready"], CREDIT)
                restc = [area((16 + b) * KW, KT * F1).rearrange("p (k f) -> p k f", f=F1) for b in range(2)]
                for l in range(2):
                    nxt = hs1[(l + 1) % 2]

                    def split(c, half):
                        dve.wait_ge(s["t20_ready"], l * NCH + c + 1 + CREDIT)
                        v = PS[:, 4 + half, 0:KT * F1].rearrange("p (k f) -> p k f", f=F1)
                        split3([nxt[:, bass.ds(c * KT, KT), q * F1:(q + 1) * F1] for q in range(3)], v, restc[half])
                        dve.sem_inc(s["split_ready"], 1)

                    def two(m):
                        split(2 * m, 0)
                        split(2 * m + 1, 1)
                    loop(dve, 0, NCH // 2, [(steps, 10)], two)
                dve.wait_ge(s["mixed_copied"], 3 * NCH + CREDIT)
                pe_do()
                tt(R, PSrow, A[:, :, :], ALU.add)
                ts(R, R, 0.0, ALU.max)
                tt(R, R, A[:, :, :], ALU.add)
                layer_norm(R, TMP)

            def clip_norm(dst, name):
                ts(S(name), S(name), EPS * EPS, ALU.max)
                sqrt(dst, name)

            def radius(dst, n):
                rec(dst, n)
                ts(dst, dst, MAXNORM, ALU.mult, 1.0, ALU.min)

            def artanh(dst, n):
                ts(S("y0"), n, ATANH_MAX, ALU.min)
                act_do()
                act_do()
                tt(S("y1"), S("y1"), S("y2"), ALU.subtract)
                ts(dst, S("y1"), 0.5, ALU.mult)

            def add_weights(x2, xy, y2, c1, c2):
                tt(S("y1"), x2, y2, ALU.mult)
                stt(S("y1"), xy, 2.0, S("y1"), ALU.mult, ALU.add)
                ts(S("y1"), S("y1"), 1.0, ALU.add, EPS, ALU.max)
                rec(S("y1"), S("y1"))
                stt(S("y2"), xy, 2.0, y2, ALU.mult, ALU.add)
                stt(c1, S("y2"), 1.0, S("y1"), ALU.add, ALU.mult)
                ts(S("y2"), x2, -1.0, ALU.mult, 1.0, ALU.add)
                tt(c2, S("y2"), S("y1"), ALU.mult)

            if LAYERS > 2:
                Wb, hbB, wlB, wrB = (X2[:, k * P:(k + 1) * P] for k in range(4))
                WT = X2[:, 5 * P:6 * P]
                for _ in range(5):
                    dma_do()
                pe_do()
                link(V.tensor_copy(WT, PS[:, 0, 0:P]))
                sum_of_products("ss", A[:, :, :], A[:, :, :], TMP)
                clip_norm(S("n"), "ss")
                radius(S("f"), S("n"))
                tt(R, A[:, :, :], bc(S("f")), ALU.mult)
                tt(S("n"), S("n"), S("f"), ALU.mult)
                pe_do()
                dve.wait_ge(s["copy_answered"], 4)
                pe_do()
                link(V.tensor_copy(A[:, :, :], PSrow))
                sum_of_products("x2", A[:, :, :], A[:, :, :], TMP)
                link(V.tensor_copy(S("ss"), S("x2")))
                clip_norm(S("m"), "ss")
                tt(TMP[:, 0, :], hbB, hbB, ALU.mult)
                link(V.tensor_reduce(par[:, T0:T0 + 1], TMP[:, 0, :], AX.X, ALU.add))
                tt(S("ss"), par[:, T0:T0 + 1].to_broadcast([P, NT]), par[:, T0:T0 + 1].to_broadcast([P, NT]), ALU.max)
                clip_norm(S("nb"), "ss")
                artanh(S("at"), S("n"))
                rec(S("y1"), S("n"))
                tt(S("y1"), S("y1"), S("m"), ALU.mult)
                tt(S("y1"), S("y1"), S("at"), ALU.mult)
                act_do()
                rec(S("g"), S("m"))
                tt(S("g"), S("g"), S("y0"), ALU.mult)
                ts(S("n"), S("y0"), EPS, ALU.max)
                radius(S("f"), S("n"))
                tt(S("g"), S("g"), S("f"), ALU.mult)
                tt(S("x2"), S("x2"), S("g"), ALU.mult)
                tt(S("x2"), S("x2"), S("g"), ALU.mult)
                link(V.tensor_copy(S("y1"), S("nb")))
                act_do()
                ts(S("n"), S("y2"), EPS, ALU.max)
                radius(S("f"), S("n"))
                tt(S("n"), S("n"), S("f"), ALU.mult)
                rec(S("gb"), S("nb"))
                tt(S("gb"), S("gb"), S("n"), ALU.mult)
                tt(S("yy"), S("n"), S("n"), ALU.mult)
                sum_of_products("xy", A[:, :, :], bf(hbB), TMP)
                tt(S("xy"), S("xy"), S("g"), ALU.mult)
                tt(S("xy"), S("xy"), S("gb"), ALU.mult)
                add_weights(S("x2"), S("xy"), S("yy"), S("c1"), S("c2"))
                tt(S("c1"), S("c1"), S("g"), ALU.mult)
                tt(S("c2"), S("c2"), S("gb"), ALU.mult)
                tt(A[:, :, :], A[:, :, :], bc(S("c1")), ALU.mult)
                tt(TMP, bf(hbB), bc(S("c2")), ALU.mult)
                tt(A[:, :, :], A[:, :, :], TMP, ALU.add)
                sum_of_products("ss", A[:, :, :], A[:, :, :], TMP)
                clip_norm(S("n"), "ss")
                radius(S("f"), S("n"))
                tt(A[:, :, :], A[:, :, :], bc(S("f")), ALU.mult)
                sum_of_products("x2", A[:, :, :], A[:, :, :], TMP)
                tt(S("n"), S("n"), S("f"), ALU.mult)
                artanh(S("at"), S("n"))
                rec(S("g"), S("n"))
                tt(S("g"), S("g"), S("at"), ALU.mult)
                sum_of_products("sc_i", A[:, :, :], bf(wlB), TMP)
                tt(S("sc_i"), S("sc_i"), S("g"), ALU.mult)
                sum_of_products("sc_j", A[:, :, :], bf(wrB), TMP)
                tt(S("sc_j"), S("sc_j"), S("g"), ALU.mult)
                ts(S("sc_j"), S("sc_j"), par[:, ATTB:ATTB + 1], ALU.add)
                ts(S("b"), S("x2"), -1.0, ALU.mult, 1.0, ALU.add)
                rec(S("ib"), S("b"))
                tt(S("kap"), S("x2"), S("ib"), ALU.mult)
                ts(S("ub"), S("x2"), 1.0, ALU.add)
                tt(S("ub"), S("ub"), S("ib"), ALU.mult)
                tt(R, A[:, :, :], bc(S("ib")), ALU.mult)
                pe_do()
                dve.wait_ge(s["copy_answered"], 5)
                pe_do()
                dve.wait_ge(s["copy_answered"], 6)
                dma_do()
                tS, tM = augrows
                for k, name in enumerate(("ib", "kap")):
                    pb = [area(16 * KW + 512 + 16 * q, 16, BF16) for q in range(3)]
                    split3(pb, S(name), TMP[:, 8, 0:NT])
                    for col, (i, j) in enumerate(((0, 0), (0, 1), (1, 0), (0, 2), (2, 0), (1, 1))):
                        link(V.tensor_copy(tS[:, :, 6 * k + col], pb[i]))
                        ts(tM[:, :, 6 * k + col], pb[j], -0.5, ALU.mult)
                link(V.memset(A[:, :, :], 0.0))
                pe_do()
                dve.wait_ge(s["copy_answered"], 7)
                pe_do()
                dve.wait_ge(s["copy_answered"], 8)
                pe_do(False)

                f2 = PS[:, 4:6, :].rearrange("p b f -> p (b f)")

                def scores(c, jp):
                    for jj in range(2):
                        ins = V.tensor_scalar(f2[:, jj * CH:(jj + 1) * CH], sbrow,
                                              S("sc_j")[:, bass.ds(2 * jp + jj, 1)], SCORE_MIN, ALU.add, ALU.max)
                    ins.then_inc(s["score_ready"], 1)

                def clip(c, jp, par_):
                    n = c * NP + jp
                    dve.wait_ge(s["lnw_ready"], n + 1)
                    dve.wait_ge(s["c_used"], n + 1)
                    V.tensor_scalar(b2b[par_], a2[par_], LNW_MIN, LNW_MAX, ALU.max, ALU.min)\
                        .then_inc(s["clip_ready"], 1)

                def pair2(c, jp, par_, more):
                    n = c * NP + jp
                    w = PS[:, 2 * par_:2 * par_ + 2, :].rearrange("p b f -> p (b f)")
                    dve.wait_ge(s["soft_ready"], n + 1)
                    dve.wait_ge(s["clip_ready"], n + 1)
                    k = steps.mark(V.tensor_tensor(a2[par_], f2, a2[par_], ALU.add))
                    steps.wait(k)
                    if more:
                        scores(c, jp + 1)
                    dve.wait_ge(s["half_ready"], n + 1)
                    V.scalar_tensor_tensor(out=a2[par_], in0=w, scalar=0.5, in1=a2[par_],
                                           op0=ALU.mult, op1=ALU.add).then_inc(s["expo_ready"], 1)
                    if more:
                        clip(c, jp + 1, 1 - par_)
                    dve.wait_ge(s["ln1p_ready"], n + 1)
                    V.scalar_tensor_tensor(out=b2b[par_], in0=e2, scalar=2.0, in1=b2b[par_],
                                           op0=ALU.mult, op1=ALU.add).then_inc(s["artanh_ready"], 1)
                    dve.wait_ge(s["artanh_ready"], n + 2)
                    dve.wait_ge(s["weight_exp_ready"], n + 1 + CREDIT)
                    stt(b2b[par_], b2b[par_], 0.5 / EDGE8, a2[par_], ALU.mult, ALU.mult)
                    cm = b2b[par_].rearrange("p (j x) -> p j x", j=2)
                    V.tensor_tensor(cm, cm, adjU[:, bass.ds(2 * jp, 2), bass.ds(c * CH, CH)], ALU.mult)\
                        .then_inc(s["c_ready"], 1)

                def chunk2(c):
                    dve.wait_ge(s["srow_in"], 16 * (c + 1))
                    scores(c, 0)
                    clip(c, 0, 0)

                    def pairs(m):
                        for h in range(2):
                            pair2(c, 2 * m + h, h, True)
                    loop(dve, 0, NP // 2 - 1, [(steps, 4)], pairs)
                    pair2(c, NP - 2, 0, True)
                    dve.wait_ge(s["score_ready"], (c + 1) * NP)
                    dve.sem_inc(s["srow_used"], 1)
                    pair2(c, NP - 1, 1, False)
                    dve.wait_ge(s["uT_ready"], c + 1)
                    V.tensor_copy(S("u")[:, bass.ds(c * KT, KT)], PS[:, 6, 0:KT]).then_inc(s["uT_copied"], 1)

                dve.sem_inc(s["c_ready"], CREDIT)
                dve.sem_inc(s["artanh_ready"], 1)
                dve.sem_inc(s["uT_copied"], 1)
                loop(dve, 0, NCH, [(steps, 2 * NP)], chunk2)
                dve.wait_ge(s["uT_copied"], NCH + 1)
                pe_do()
                link(V.tensor_copy(A[:, :, :], PSrow))
                tt(R, R, bc(S("b")), ALU.mult)
                sum_of_products("xy", R, A[:, :, :], TMP)
                stt(S("g"), S("xy"), 2.0, S("u"), ALU.mult, ALU.subtract)
                tt(A[:, :, :], A[:, :, :], bc(S("b")), ALU.mult)
                tt(TMP, R, bc(S("g")), ALU.mult)
                tt(A[:, :, :], A[:, :, :], TMP, ALU.add)
                dma_do(False)
                sum_of_products("ss", A[:, :, :], A[:, :, :], TMP)
                link(V.tensor_copy(S("at"), S("ss")))
                clip_norm(S("n"), "ss")
                ts(S("y2"), S("b"), EPS, ALU.max)
                rec(S("y2"), S("y2"))
                tt(S("y1"), S("y2"), S("n"), ALU.mult)
                act_do()
                rec(S("gb"), S("n"))
                tt(S("gb"), S("gb"), S("y0"), ALU.mult)
                tt(S("yy"), S("gb"), S("gb"), ALU.mult)
                tt(S("yy"), S("yy"), S("at"), ALU.mult)
                sum_of_products("xy", R, A[:, :, :], TMP)
                tt(S("xy"), S("xy"), S("gb"), ALU.mult)
                add_weights(S("x2"), S("xy"), S("yy"), S("c1"), S("c2"))
                tt(S("c2"), S("c2"), S("gb"), ALU.mult)
                tt(R, R, bc(S("c1")), ALU.mult)
                tt(A[:, :, :], A[:, :, :], bc(S("c2")), ALU.mult)
                tt(R, R, A[:, :, :], ALU.add)
                sum_of_products("ss", R, R, TMP)
                clip_norm(S("n"), "ss")
                radius(S("f"), S("n"))
                tt(S("m"), S("n"), S("f"), ALU.mult)
                ts(S("m"), S("m"), EPS, ALU.max)
                artanh(S("at"), S("m"))
                rec(S("g"), S("m"))
                tt(S("g"), S("g"), S("at"), ALU.mult)
                tt(S("g"), S("g"), S("f"), ALU.mult)
                tt(R, R, bc(S("g")), ALU.mult)
                ts(R, R, 0.0, ALU.max)
                sum_of_products("ss", R, R, TMP)
                clip_norm(S("n"), "ss")
                link(V.tensor_copy(S("y1"), S("n")))
                act_do()
                rec(S("g"), S("n"))
                tt(S("g"), S("g"), S("y0"), ALU.mult)
                ts(S("n"), S("y0"), EPS, ALU.max)
                radius(S("f"), S("n"))
                tt(S("g"), S("g"), S("f"), ALU.mult)
                tt(R, R, bc(S("g")), ALU.mult)
                dve.wait_ge(s["dma_answered"], 16 * n_dma[0])
                tt(R, R, T[:, :].rearrange("p (t f) -> p t f", f=D), ALU.add)
                layer_norm(R, TMP)

            if LAYERS > 3:
                for _ in range(2):
                    dma_do()
                pe_do()
                dve.wait_ge(s["copy_answered"], 9)
                pe_do()
                restf = X2[:, 2 * P:2 * P + 4 * P].rearrange("p (k f) -> p k f", f=P)
                Bb = X2[:, P:2 * P].unsqueeze(1).to_broadcast([P, KT, D])

                def split_h(g):
                    v = PSrow[:, g * KT:(g + 1) * KT, :]
                    tt(restf, v, Bb, ALU.add)
                    parts = [hs3[q][:, g * KT:(g + 1) * KT, :] for q in range(3)]
                    link(V.tensor_copy(parts[0], restf))
                    tt(restf, restf, parts[0], ALU.subtract)
                    link(V.tensor_copy(parts[1], restf))
                    tt(restf, restf, parts[1], ALU.subtract)
                    link(V.tensor_copy(parts[2], restf))
                for g in range(NCH):
                    split_h(g)
                pe_do(False)

                link(V.memset(par[:, T2:T2 + 1], R_FLOOR))
                rec(par[:, T2:T2 + 1], par[:, T2:T2 + 1])
                rec(par[:, T1:T1 + 1], par[:, MU:MU + 1])
                tt(par[:, T0:T0 + 1], par[:, T2:T2 + 1], par[:, T1:T1 + 1], ALU.subtract)
                act_do()
                tt(par[:, T2:T2 + 1], par[:, SIG:SIG + 1], par[:, SIG:SIG + 1], ALU.mult)
                ts(par[:, T2:T2 + 1], par[:, T2:T2 + 1], -2.0, ALU.mult)
                rec(par[:, T2:T2 + 1], par[:, T2:T2 + 1])
                tt(par[:, T2:T2 + 1], par[:, T2:T2 + 1], par[:, T1:T1 + 1], ALU.mult)
                act_do()

                def masks(c):
                    m = adjU[:, :, bass.ds(c * CH, CH)]
                    link(V.tensor_scalar(m, m, 0.5 * EDGE8, EDGE8, ALU.is_lt, ALU.mult))
                    for k in range(KT):
                        d = adjU[:, bass.ds(c * KT + k, 1), bass.ds(c * CH + k * P, P)]
                        ins = V.tensor_tensor(d, d, not_i[:, :].unsqueeze(1), ALU.mult)
                    ins.then_inc(s["mask_ready"], 1)
                loop(dve, 0, NCH, [(steps, 1)], masks)
                dve.wait_ge(s["agg3_free"], NCH + CREDIT)
                pe_do()
                ts(par[:, S0:S0 + 1], par[:, S0:S0 + 1], 1.0 / EDGE_PE, ALU.mult)
                stt(R, PSrow, par[:, S0:S0 + 1], A[:, :, :], ALU.mult, ALU.add)
                layer_norm(R, TMP)
            dma_do(False)


_INS = ["x", "adj", "L0_gnn_beta", "L1_gnn_W1", "L1_gnn_b1", "L1_gnn_W2", "L1_gnn_b2", "L1_gnn_W3", "L1_gnn_b3",
        "L2_gnn_W", "L2_gnn_b", "L2_gnn_att_wl", "L2_gnn_att_wr", "L2_gnn_att_b",
        "L3_gnn_W", "L3_gnn_B", "L3_gnn_mu", "L3_gnn_sigma"]
_OUTS = [((4096, 128), "float32")]


def kernel(**inputs):
    import numpy as _np
    import concourse.bacc as _bacc
    from concourse import mybir as _mybir
    from concourse.bass_utils import run_bass_kernel_spmd as _run

    nc = _bacc.Bacc("TRN2", target_bir_lowering=False, num_devices=1)
    arrays, args = {}, []
    for name in _INS:
        a = _np.ascontiguousarray(inputs[name])
        arrays[f"in_{name}_dram"] = a
        args.append(nc.dram_tensor(f"in_{name}_dram", a.shape, _mybir.dt.from_np(a.dtype), kind="ExternalInput").ap())
    for i, (shape, dtype) in enumerate(_OUTS):
        dt = _mybir.dt.from_np(_np.dtype(dtype))
        args.append(nc.dram_tensor(f"out_{i}_dram", shape, dt, kind="ExternalOutput").ap())
    gnn_stack(nc, *args)
    r = _run(nc, [arrays], core_ids=[0])
    return r.results[0]["out_0_dram"]
```

```python
from contextlib import ExitStack

import concourse.bass as bass
from concourse import mybir

F32 = mybir.dt.float32
BF16 = mybir.dt.bfloat16
FP8 = mybir.dt.float8e4
U8 = mybir.dt.uint8
ALU = mybir.AluOpType
ACT = mybir.ActivationFunctionType
AX = mybir.AxisListType

P = 128
CH = 512
COS_EPS = 1e-7
NO_NEIGHBOUR = 1e-30
TINY_NORM = 1e-13
LN_EPS = 1e-5
EPS = 1e-15
MAXNORM = 0.999
R_FLOOR = 1e-15
ATANH_MAX = 0.99999
V_MIN = 1.0 - ATANH_MAX * ATANH_MAX
EDGE8 = 64.0
EDGE_PE = 2.0
CREDIT = 2


class Chain:

    def __init__(self, eng, sem):
        self.eng, self.sem, self.n = eng, sem, 0

    def mark(self, ins):
        ins.then_inc(self.sem, 1)
        self.n = self.n + 1
        return self.n

    def wait(self, n):
        self.eng.wait_ge(self.sem, n)

    def link(self, ins):
        self.wait(self.mark(ins))


def loop(eng, start, end, chains, body):
    at = [ch.n for ch, _ in chains]
    with eng.Fori(start, end) as i:
        for (ch, steps), n0 in zip(chains, at):
            ch.n = n0 + (i - start) * steps
        want = [ch.n for ch, _ in chains]
        body(i)
    for (ch, steps), n0 in zip(chains, at):
        ch.n = n0 + (end - start) * steps


def gnn_stack(nc, x, adj, beta, W1, b1, W2, b2, W3, b3, hW, hb, att_wl, att_wr, att_b,
              W, B, mu, sigma, out, LAYERS=4):
    import math

    N, D = x.shape
    F1 = W1.shape[1]
    NT = N // P
    NCH = N // CH
    KT = CH // P
    NP = NT // 2
    STG = 4
    NPC = NT // STG
    AUG = 12
    LNW_MAX = -math.log(V_MIN)
    LNW_MIN = 2.0 ** -23
    assert D == P and F1 == W2.shape[1] and W3.shape[0] == F1

    ctx = ExitStack()
    with ctx:
        def sb(name, shape, dt=F32):
            return ctx.enter_context(nc.sbuf_tensor(name, shape, dt))

        def sem(name):
            return ctx.enter_context(nc.semaphore(name))

        def dram(name, shape, dt=F32):
            return nc.dram_tensor(name, shape, dt, kind="Internal").ap()

        adjT = sb("adjT", [P, NT, N], FP8)
        adjU = adjT[:, :, :].bitcast(U8)
        A = sb("A", [P, NT, D])
        T = sb("T", [P, N])
        arena = sb("arena", [P, 42 * 256])
        ident = sb("ident", [P, P])
        identb = sb("identb", [P, P], BF16)
        not_i = sb("not_i", [P, P], BF16)
        ones = sb("ones", [P, P])
        NS = 30
        scal = sb("scal", [P, NS, NT])
        par = sb("par", [P, 16])
        PS = ctx.enter_context(nc.psum_tensor("PS", [P, 8, 512], F32))
        PSrow = PS[:, :, :].rearrange("p b (k f) -> p (b k) f", f=P)

        used = {}

        def S(name):
            if name not in used:
                used[name] = len(used)
                assert len(used) <= NS, name
            return scal[:, used[name], :]

        def area(start, size, dt=F32):
            return arena[:, start:start + size] if dt == F32 else arena[:, start:start + size].bitcast(dt)

        KW = 256
        R = area(0, 16 * KW).rearrange("p (t f) -> p t f", f=D)
        TMP = area(16 * KW, 16 * KW).rearrange("p (t f) -> p t f", f=D)
        X2 = area(32 * KW, 10 * KW)
        stage = [area(8 * KW * b, 8 * KW) for b in range(2)]
        stage4 = [s.rearrange("p (k x) -> p k x", k=KT) for s in stage]
        stage_hi = [s.bitcast(BF16).rearrange("p (k x two) -> p k x two", k=KT, two=2) for s in stage]
        rbuf = [area((16 + 4 * b) * KW, 4 * KW) for b in range(2)]
        ebuf = [area((24 + 4 * b) * KW, 4 * KW) for b in range(2)]
        acc0 = area(32 * KW, 4 * KW)
        rho_b = area(36 * KW, 2 * KW)
        osb = area(38 * KW, 2 * KW)
        mid = area(40 * KW, 2 * KW)
        hs1 = [area(KW * 4 * b, KW * 4, BF16)[:, 0:NT * 3 * F1].rearrange("p (t f) -> p t f", f=3 * F1)
               for b in range(2)]
        agg_sb = [area((8 + 2 * b) * KW, 2 * KW) for b in range(2)]
        h_sb = [area((12 + 2 * b) * KW, 2 * KW) for b in range(2)]
        stack = area(32 * KW, 2 * KW)
        w_small = area(34 * KW, 2 * KW)
        Q4 = 4 * CH
        a2 = [area(8 * b * KW, 8 * KW) for b in range(2)]
        b2b = [area((16 + 8 * b) * KW, 8 * KW) for b in range(2)]
        e2 = area(32 * KW, 8 * KW)
        augS = A[:, 0:16, :].rearrange("p t f -> p (t f)").bitcast(BF16)
        augM = A[:, 16:32, :].rearrange("p t f -> p (t f)").bitcast(BF16)
        augrows = [area((32 + k) * KW, NT * AUG // 2, BF16).rearrange("p (t a) -> p t a", a=AUG) for k in range(2)]
        sbrow = area(0, 16 * KW)
        sig = [area((16 + 2 * b) * KW, 2 * KW) for b in range(2)]
        NW = 4
        wbuf = [area((20 + 4 * b) * KW, 4 * KW) for b in range(NW)]
        acc2 = area(36 * KW, 4 * KW)
        osb2 = area(40 * KW, 2 * KW)
        Trow = T[:, :].rearrange("p (t f) -> p t f", f=D)
        fin = [A[:, 16 * b:16 * (b + 1), :].rearrange("p t f -> p (t f)") for b in range(2)]
        hs3 = [area(8 * KW * s, 8 * KW, BF16).rearrange("p (t f) -> p t f", f=D) for s in range(3)]

        numT_d = dram("numT", [P, N])
        row_d = dram("row_scalar", [NT, P])
        x_d = dram("x_spill", [P, NT * D])
        h_d = dram("h_spill", [P, NT * D])
        f_d = dram("factor", [N, N])
        f_tiles = f_d.rearrange("(g j p) (c x) -> g c p j x", j=4, p=P, x=CH)

        s = {n: sem(n) for n in (
            "x_loaded", "par_loaded", "const_ready", "const_done",
            "act_asked", "act_answered", "dve_step", "act_step", "pe_step",
            "pe_asked", "pe_answered", "copy_answered", "dma_asked", "dma_answered",
            "piece_in0", "piece_in1", "tp_ready", "tp_free",
            "cos_sum_ready", "cos_free", "guard_ready", "exp_ready", "masked_ready", "masked_used",
            "masked_added", "z_ready", "z_free", "out_bank_free", "osb_ready", "osb_stored",
            "rho_in", "rho_used", "z_loaded",
            "agg_ready", "agg_copied", "mixed_ready", "mixed_copied", "t20_ready", "split_ready", "mix_free",
            "dist_ready", "guard2_ready", "lnw_ready", "clip_ready", "half_ready", "ln1p_ready", "artanh_ready", "expo_ready",
            "weight_exp_ready", "factor_ready", "factor_stored0", "factor_stored1",
            "rows_in", "srow_in", "factor_in0", "factor_in1", "fin_used_dve",
            "sig_ready", "sig_used", "tf_ready", "tf_free", "c_ready", "c_used", "c_added",
            "u_ready", "u_free", "h_read", "o2_copied", "o2_stored", "o2_bank_free",
            "mask_ready", "agg3_ready", "agg3_free", "out_stored", "spilled")}

        xv = x.rearrange("(t p) f -> p t f", p=P)
        adj_v = adj.rearrange("(c k i) (q x) -> c q i k x", k=KT, i=P, x=STG * P)

        def row(v):
            return v.rearrange("(a n) -> a n", a=1)

        NQ = NT // 4
        NF = NCH * (NCH + 1) // 2

        def fin_reader(c, q, back):
            k = c * NQ + q - back
            uppers = sum(1 for i in range(k + 1) if i % NQ <= i // NQ)
            if k % NQ <= k // NQ:
                return "fin_used_dve", uppers
            return "tf_ready", 2 * (k + 1 - uppers)

        BETA, NABS, ATTB, MU, SIG, Y2, GY, S0, T0, T1, B1C, B2C, B3C, T2 = range(14)

        block = ctx.enter_context(nc.Block())

        @block.sync
        def _(sp):
            asked = [0]

            def serve(fn, n=1):
                asked[0] += 1
                sp.wait_ge(s["dma_asked"], asked[0])
                fn().then_inc(s["dma_answered"], 16)

            sp.dma_start(A[:, :, :], xv).then_inc(s["x_loaded"], 16)
            for col, v in ((BETA, beta), (ATTB, att_b), (MU, mu), (SIG, sigma)):
                sp.dma_start(par[:, col:col + 1], v.partition_broadcast(P)).then_inc(s["par_loaded"], 16)
            for col, v, n in ((B1C, b1, F1), (B2C, b2, F1), (B3C, b3, D)):
                sp.dma_start(par[0:n, col:col + 1], v.rearrange("(n a) -> n a", a=1)).then_inc(s["par_loaded"], 16)

            serve(lambda: sp.dma_start(row_d, mid[0:NT, 0:P]))
            rows_flat = row_d.rearrange("t p -> (t p)")

            def pieces(cc, first):
                for q in range(NPC):
                    g = cc * NPC + q
                    sp.wait_ge(s["tp_ready"], 2 * g + 2)
                    sp.dma_start(stage4[q % 2], adj_v[bass.ds(cc, 1), q].rearrange("a i k x -> (a i) k x")
                                 if not first else adj_v[0, q]).then_inc(s[f"piece_in{q % 2}"], 16)

            def rho_load(c):
                sp.wait_ge(s["rho_used"], c + 1)
                sp.dma_start(rho_b, rows_flat[bass.ds(c * CH, CH)].partition_broadcast(P)).then_inc(s["rho_in"], 16)

            def store_out(c):
                sp.wait_ge(s["osb_ready"], c + 1)
                sp.dma_start(numT_d[:, bass.ds(c * CH, CH)], osb).then_inc(s["osb_stored"], 16)

            sp.wait_ge(s["dma_answered"], 16)
            sp.wait_ge(s["copy_answered"], 2)
            pieces(0, True)
            rho_load(0)
            with sp.Fori(0, NCH - 1) as c:
                pieces(c + 1, False)
                rho_load(c + 1)
                store_out(c)
            store_out(NCH - 1)
            sp.wait_ge(s["osb_stored"], 16 * NCH + 16)
            sp.dma_start(T[:, :], numT_d).then_inc(s["z_loaded"], 16)
            if LAYERS > 1:
                serve(lambda: sp.dma_start(w_small[:, 0:F1], W1))
                for l, (w, f) in enumerate(((W2, F1), (W3, D))):
                    for part in range(3):
                        serve(lambda: sp.dma_start(stack[part * F1:(part + 1) * F1, 64 + l * 64:64 + l * 64 + f], w))
            if LAYERS > 2:
                serve(lambda: sp.dma_start(x_d, A[:, :, :].rearrange("p t f -> p (t f)")))
                serve(lambda: sp.dma_start(X2[:, 0:P], hW))
                serve(lambda: sp.dma_start(X2[:, P:2 * P], hb.partition_broadcast(P)))
                serve(lambda: sp.dma_start(X2[:, 2 * P:3 * P], att_wl.partition_broadcast(P)))
                serve(lambda: sp.dma_start(X2[:, 3 * P:4 * P], att_wr.partition_broadcast(P)))
                serve(lambda: sp.dma_start(h_d, R.rearrange("p t f -> p (t f)")))
                serve(lambda: sp.dma_start(row_d, X2[0:NT, 4 * P:5 * P]))
                sp.wait_ge(s["dma_answered"], 16 * asked[0])

                def store2(c):
                    sp.wait_ge(s["o2_copied"], c + 1)
                    sp.dma_start(numT_d[:, bass.ds(c * CH, CH)], osb2).then_inc(s["o2_stored"], 16)

                n = 0
                for c in range(NCH):
                    for g in range(c + 1):
                        sp.wait_ge(s["factor_ready"], n + 1 + CREDIT)
                        sp.dma_start(f_tiles[g, c], b2b[n % 2].rearrange("p (j x) -> p j x", x=CH))\
                            .then_inc(s[f"factor_stored{n % 2}"], 16)
                        n += 1
                for b in range(2):
                    sp.wait_ge(s[f"factor_stored{b}"], 16 * (n // 2) + 16)
                sp.dma_start(T[:, :], h_d).then_inc(s["rows_in"], 16)
                sp.dma_start(sbrow, rows_flat.partition_broadcast(P)).then_inc(s["srow_in"], 16)
                for c in range(NCH):
                    for q in range(NQ):
                        if (c, q) >= (0, 2):
                            who, count = fin_reader(c, q, 2)
                            sp.wait_ge(s[who], count)
                        if q <= c:
                            src = f_tiles[q, c]
                            dst = fin[q % 2].rearrange("p (j x) -> p j x", x=CH)
                        else:
                            src = f_tiles[c, q]
                            dst = fin[q % 2].rearrange("p (j x) -> p j x", x=CH)
                        sp.dma_start(dst, src).then_inc(s[f"factor_in{q % 2}"], 16)
                    if c >= 1:
                        store2(c - 1)
                store2(NCH - 1)
                sp.wait_ge(s["o2_stored"], 16 * NCH + 16)
                sp.wait_ge(s["h_read"], 1)
                sp.dma_start(T[:, :], numT_d).then_inc(s["z_loaded"], 16)
                serve(lambda: sp.dma_start(T[:, :], x_d))
            if LAYERS > 3:
                serve(lambda: sp.dma_start(X2[:, 0:P], W))
                serve(lambda: sp.dma_start(X2[:, P:2 * P], B.partition_broadcast(P)))
            asked[0] += 1
            sp.wait_ge(s["dma_asked"], asked[0])
            sp.dma_start(out.rearrange("(t p) f -> p t f", p=P), A[:, :, :]).then_inc(s["out_stored"], 16)
            sp.wait_ge(s["out_stored"], 16)

        @block.gpsimd
        def _(pool):
            def step(n, ins):
                ins.then_inc(s["const_ready"], 1)
                pool.wait_ge(s["const_ready"], n)

            step(1, pool.memset(ident[:, :], 0.0))
            step(2, pool.memset(not_i[:, :], 1.0))
            step(3, pool.memset(ones[:, :], 1.0))
            step(4, pool.affine_select(out=ident[:, :], in_=ident[:, :], compare_op=ALU.not_equal, fill=1.0,
                                       base=0, pattern=[[-1, P]], channel_multiplier=1))
            step(5, pool.affine_select(out=not_i[:, :], in_=not_i[:, :], compare_op=ALU.not_equal, fill=0.0,
                                       base=0, pattern=[[-1, P]], channel_multiplier=1))
            pool.tensor_copy(identb[:, :], ident[:, :]).then_inc(s["const_done"], 1)

            def add(n, buf):
                pool.wait_ge(s["masked_ready"], n + 1)
                pool.wait_ge(s["masked_added"], n + CREDIT)
                pool.tensor_tensor(acc0, acc0, ebuf[buf], ALU.add).then_inc(s["masked_added"], 1)

            def chunk(c):
                pool.wait_ge(s["z_ready"], c + 1)
                pool.wait_ge(s["masked_ready"], c * NP + 1)
                pool.tensor_tensor(acc0, ebuf[0], ones[:, 0:1].to_broadcast([P, 2 * CH]), ALU.mult).then_inc(s["masked_added"], 1)
                add(c * NP + 1, 1)

                def pairs(m):
                    add(c * NP + 2 * m, 0)
                    add(c * NP + 2 * m + 1, 1)
                loop(pool, 1, NP // 2, [], pairs)

            pool.sem_inc(s["masked_added"], CREDIT)
            loop(pool, 0, NCH, [], chunk)

            if LAYERS > 2:
                pool.sem_inc(s["factor_ready"], CREDIT)

                def product(n, b):
                    pool.wait_ge(s["weight_exp_ready"], n + 1)
                    pool.wait_ge(s["artanh_ready"], n + 2)
                    pool.tensor_tensor(b2b[b], b2b[b], a2[b], ALU.mult).then_inc(s["factor_ready"], 1)

                def products(m):
                    product(2 * m, 0)
                    product(2 * m + 1, 1)
                loop(pool, 0, NF // 2, [], products)

                def add2(n, buf):
                    pool.wait_ge(s["c_ready"], n + 1)
                    pool.wait_ge(s["c_added"], n + NW)
                    pool.tensor_tensor(acc2, acc2, wbuf[buf], ALU.add).then_inc(s["c_added"], 1)

                def chunk2(c):
                    pool.wait_ge(s["u_ready"], c + 1)
                    pool.wait_ge(s["c_ready"], c * NP + 1)
                    pool.tensor_tensor(acc2, wbuf[0], ones[:, 0:1].to_broadcast([P, 2 * CH]), ALU.mult)\
                        .then_inc(s["c_added"], 1)
                    for b in range(1, NW):
                        add2(c * NP + b, b)

                    def pairs(m):
                        for b in range(NW):
                            add2(c * NP + NW * m + b, b)
                    loop(pool, 1, NP // NW, [], pairs)

                pool.sem_inc(s["c_added"], NW)
                loop(pool, 0, NCH, [], chunk2)

        @block.tensor
        def _(pe):
            asked = [0]
            copies = [0]

            def ask_wait():
                asked[0] += 1
                pe.wait_ge(s["pe_asked"], asked[0])

            def transposes(src, dst=None):
                for t in range(NT):
                    last = nc.tensor.transpose(PSrow[:, t, :], src(t), ident[:, :])
                return last

            def tile_T(t):
                return T[:, t * P:(t + 1) * P]

            pe.sem_inc(s["tp_ready"], 2 * CREDIT)
            pe.sem_inc(s["masked_used"], CREDIT)
            pe.sem_inc(s["z_ready"], 1)
            pe.wait_ge(s["const_done"], 1)
            ask_wait()
            nc.tensor.transpose(PS[0:NT, 7, 0:P], S("rho"), ident[:, :]).then_inc(s["pe_answered"], 1)
            ask_wait()
            pe.wait_ge(s["copy_answered"], 1)
            transposes(lambda t: R[:, t, :]).then_inc(s["pe_answered"], 1)
            pe.wait_ge(s["copy_answered"], 2)

            def build(c, jp):
                tp = PS[:, 4 + jp % 2, :].bitcast(BF16).rearrange("p (j x) -> p j x", j=2)
                q = jp // 2
                if jp % 2 == 0:
                    pe.wait_ge(s[f"piece_in{q % 2}"], 16 * (c * (NPC // 2) + q // 2 + 1))
                pe.wait_ge(s["tp_free"], c * NP + jp + 1)
                for jj in range(2):
                    J = 2 * jp + jj
                    for k in range(KT):
                        last = nc.tensor.transpose(tp[:, jj, k * P:(k + 1) * P],
                                                   stage_hi[q % 2][:, k, (J % STG) * P:(J % STG + 1) * P, 1],
                                                   identb[:, :])
                last.then_inc(s["tp_ready"], 1)

            def cosines(c, jp):
                n = c * NP + jp
                pe.wait_ge(s["cos_free"], n + 1)
                for jj in range(2):
                    J = 2 * jp + jj
                    last = nc.tensor.matmul(PS[:, 2 * (jp % 2) + jj, :], T[:, J * P:(J + 1) * P],
                                            T[:, bass.ds(c * CH, CH)], start=True, stop=True)
                last.then_inc(s["cos_sum_ready"], 1)

            def chunk0(c, more):
                cosines(c, 0)
                cosines(c, 1)
                for jp in range(NP):
                    if jp + 2 < NP:
                        cosines(c, jp + 2)
                    if jp == 0:
                        pe.wait_ge(s["out_bank_free"], c + 1)
                    pe.wait_ge(s["masked_ready"], c * NP + jp + 1)
                    for jj in range(2):
                        J = 2 * jp + jj
                        last = nc.tensor.matmul(PS[:, 6, :], A[:, J, :], ebuf[jp % 2][:, jj * CH:(jj + 1) * CH],
                                                start=(J == 0), stop=(J == NT - 1))
                    last.then_inc(s["masked_used"], 1)
                    if more:
                        build(c + 1, jp)
                pe.wait_ge(s["masked_added"], (c + 1) * NP + CREDIT)
                pe.wait_ge(s["z_free"], c + 1)
                for k in range(KT):
                    for half in range(2):
                        last = nc.tensor.matmul(PS[:, 7, k:k + 1], acc0[:, half * CH + k * P:half * CH + (k + 1) * P],
                                                ones[:, 0:1], start=(half == 0), stop=(half == 1))
                last.then_inc(s["z_ready"], 1)

            for jp in range(NP):
                build(0, jp)
            with pe.Fori(0, NCH - 1) as c:
                chunk0(c, True)
            chunk0(NCH - 1, False)

            ask_wait()
            for t in range(NT):
                last = nc.tensor.matmul(PS[:, 0, 0:P], ones[:, :], A[:, t, :], start=(t == 0), stop=(t == NT - 1))
            last.then_inc(s["pe_answered"], 1)
            ask_wait()
            pe.wait_ge(s["z_loaded"], 16)
            transposes(tile_T).then_inc(s["pe_answered"], 1)

            if LAYERS > 1:
                ask_wait()
                transposes(lambda t: A[:, t, :]).then_inc(s["pe_answered"], 1)
                ask_wait()
                pe.wait_ge(s["copy_answered"], 3)
                for t in range(NT):
                    last = nc.tensor.matmul(PS[:, t // 4, (t % 4) * F1:(t % 4 + 1) * F1], tile_T(t), w_small[:, 0:F1],
                                            start=True, stop=True)
                last.then_inc(s["pe_answered"], 1)
                pe.sem_inc(s["t20_ready"], CREDIT)
                for l in range(3):
                    F = D if l == 2 else F1
                    wl = stack[0:3 * F1, (0, 64, 128)[l]:(0, 64, 128)[l] + F]
                    hs = hs1[l % 2]

                    def agg(c, half):
                        pe.wait_ge(s["agg_copied"], l * NCH + c + 1)
                        for J in range(NT):
                            last = nc.tensor.matmul(PS[0:3 * F1, half, :], hs[:, J, :],
                                                    adjT[:, J, c * CH:(c + 1) * CH],
                                                    start=(J == 0), stop=(J == NT - 1))
                        last.then_inc(s["agg_ready"], 1)

                    def mix(c, half):
                        pe.wait_ge(s["agg_copied"], l * NCH + c + 1 + CREDIT)
                        pe.wait_ge(s["mixed_copied"], l * NCH + c + 1)
                        nc.tensor.matmul(PS[0:F, 2 + half, :], wl, agg_sb[half][0:3 * F1, :],
                                         start=True, stop=True).then_inc(s["mixed_ready"], 1)
                        if l < 2:
                            pe.wait_ge(s["mixed_copied"], l * NCH + c + 1 + CREDIT)
                            pe.wait_ge(s["split_ready"], l * NCH + c + 1)
                            for k in range(KT):
                                last = nc.tensor.transpose(PS[:, 4 + half, k * F1:(k + 1) * F1],
                                                           h_sb[half][0:F1, k * P:(k + 1) * P], ident[0:F1, 0:F1])
                            last.then_inc(s["t20_ready"], 1)

                    pe.wait_ge(s["split_ready"], CREDIT + l * NCH)
                    agg(0, 0)
                    for c in range(1, NCH):
                        agg(c, c % 2)
                        mix(c - 1, (c - 1) % 2)
                    mix(NCH - 1, 1)
                ask_wait()
                transposes(tile_T).then_inc(s["pe_answered"], 1)

            if LAYERS > 2:
                ask_wait()
                nc.tensor.transpose(PS[:, 0, 0:P], X2[:, 0:P], ident[:, :]).then_inc(s["pe_answered"], 1)
                ask_wait()
                transposes(lambda t: R[:, t, :]).then_inc(s["pe_answered"], 1)
                ask_wait()
                pe.wait_ge(s["copy_answered"], 4)
                for t in range(NT):
                    last = nc.tensor.matmul(PSrow[:, t, :], tile_T(t), X2[:, 5 * P:6 * P], start=True, stop=True)
                last.then_inc(s["pe_answered"], 1)
                ask_wait()
                transposes(lambda t: R[:, t, :]).then_inc(s["pe_answered"], 1)
                ask_wait()
                pe.wait_ge(s["copy_answered"], 5)
                nc.tensor.transpose(PS[0:NT, 7, 0:P], S("sc_i"), ident[:, :]).then_inc(s["pe_answered"], 1)
                for aug in range(2):
                    ask_wait()
                    for t in range(NT):
                        last = nc.tensor.transpose(PS[:, :, :].bitcast(BF16).rearrange("p b f -> p (b f)")
                                                   [0:AUG, t * P:(t + 1) * P],
                                                   augrows[aug][:, t, :], identb[:, :])
                    last.then_inc(s["pe_answered"], 1)
                ask_wait()
                pe.sem_inc(s["pe_answered"], 1)
                n = 0
                for c in range(NCH):
                    for g in range(c + 1):
                        if n > 0:
                            pe.wait_ge(s["guard2_ready"], n)
                        for j in range(4):
                            J = 4 * g + j
                            o = PS[:, j, :]
                            nc.tensor.matmul(o, T[:, J * P:(J + 1) * P], T[:, c * CH:(c + 1) * CH],
                                             start=True, stop=False)
                            last = nc.tensor.matmul(o, augS[:, J * P:(J + 1) * P], augM[:, c * CH:(c + 1) * CH],
                                                    start=False, stop=True)
                        last.then_inc(s["dist_ready"], 1)
                        n += 1

                pe.sem_inc(s["c_used"], NW)
                pe.sem_inc(s["u_ready"], 1)
                low = [0]

                def mirror(c, jp):
                    q, half = jp // 2, jp % 2
                    if half == 0:
                        pe.wait_ge(s[f"factor_in{q % 2}"], 16 * (c * NQ // 2 + q // 2 + 1))
                    pe.wait_ge(s["tf_free"], low[0] + 1)
                    for jj in range(2):
                        for k in range(KT):
                            last = nc.tensor.transpose(
                                PS[:, 2 * (jp % 2) + jj, k * P:(k + 1) * P],
                                fin[q % 2][:, k * CH + (2 * half + jj) * P:k * CH + (2 * half + jj + 1) * P],
                                ident[:, :])
                    last.then_inc(s["tf_ready"], 1)
                    low[0] += 1

                pe.wait_ge(s["rows_in"], 16)
                pe.wait_ge(s["weight_exp_ready"], NF)
                pe.wait_ge(s["artanh_ready"], NF + 1)
                for c in range(NCH):
                    for jp in range(NP):
                        if jp + 1 < NP and (jp + 1) // 2 > c:
                            mirror(c, jp + 1)
                        if jp == 0:
                            pe.wait_ge(s["o2_bank_free"], c + 1)
                        pe.wait_ge(s["c_ready"], c * NP + jp + 1)
                        for jj in range(2):
                            J = 2 * jp + jj
                            last = nc.tensor.matmul(PS[:, 6, :], Trow[:, J, :], wbuf[jp % NW][:, jj * CH:(jj + 1) * CH],
                                                    start=(J == 0), stop=(J == NT - 1))
                        last.then_inc(s["c_used"], 1)
                    pe.wait_ge(s["c_added"], (c + 1) * NP + NW)
                    pe.wait_ge(s["u_free"], c + 1)
                    for k in range(KT):
                        for half in range(2):
                            last = nc.tensor.matmul(PS[:, 7, k:k + 1],
                                                    acc2[:, half * CH + k * P:half * CH + (k + 1) * P],
                                                    ones[:, 0:1], start=(half == 0), stop=(half == 1))
                    last.then_inc(s["u_ready"], 1)
                ask_wait()
                pe.wait_ge(s["z_loaded"], 32)
                transposes(tile_T).then_inc(s["pe_answered"], 1)

            if LAYERS > 3:
                ask_wait()
                transposes(lambda t: A[:, t, :]).then_inc(s["pe_answered"], 1)
                ask_wait()
                pe.wait_ge(s["copy_answered"], 9)
                for t in range(NT):
                    last = nc.tensor.matmul(PSrow[:, t, :], tile_T(t), X2[:, 0:P], start=True, stop=True)
                last.then_inc(s["pe_answered"], 1)
                ask_wait()
                pe.sem_inc(s["pe_answered"], 1)

                def agg3(c, half):
                    pe.wait_ge(s["agg3_free"], c + 1)
                    pe.wait_ge(s["mask_ready"], c + 1)
                    for part in range(3):
                        for J in range(NT):
                            last = nc.tensor.matmul(PS[:, half, :], hs3[part][:, J, :],
                                                    adjT[:, J, c * CH:(c + 1) * CH],
                                                    start=(J == 0 and part == 0), stop=(J == NT - 1 and part == 2))
                    last.then_inc(s["agg3_ready"], 1)

                for c in range(NCH):
                    agg3(c, c % 2)
                ask_wait()
                transposes(tile_T).then_inc(s["pe_answered"], 1)

        @block.scalar
        def _(act):
            asked = [0]
            steps = Chain(act, s["act_step"])

            def fn(out_, in_, func, **kw):
                asked[0] += 1
                act.wait_ge(s["act_asked"], asked[0])
                nc.scalar.activation(out_, in_, func, **kw).then_inc(s["act_answered"], 1)

            pes = [0]

            def pe_copy(n, dst, src):
                act.wait_ge(s["pe_answered"], n)
                nc.scalar.copy(dst, src).then_inc(s["copy_answered"], 1)

            def sqrt(name):
                fn(S("y0"), S(name), ACT.Sqrt)

            sqrt("ss")
            pe_copy(1, mid[0:NT, 0:P], PS[0:NT, 7, 0:P])
            pe_copy(2, T[:, :], PS[:, :, :].rearrange("p b f -> p (b f)"))

            def guard(c, jp, par_, tile):
                n = c * NP + jp
                act.wait_ge(s["exp_ready"], n + 1)
                for jj in range(2):
                    steps.mark(nc.scalar.activation(rbuf[par_][:, jj * CH:(jj + 1) * CH], rho_b, ACT.Ln,
                                                    scale=S("erho")[:, bass.ds(2 * jp + jj, 1)], bias=1.0))
                steps.wait(steps.n)
                nc.scalar.activation(rbuf[par_], rbuf[par_], ACT.Exp, scale=-1.0).then_inc(s["guard_ready"], 1)

            def exps(c, jp, par_):
                n = c * NP + jp
                act.wait_ge(s["cos_free"], n + 1 + CREDIT)
                act.wait_ge(s["masked_used"], n + 1)
                act.wait_ge(s["masked_added"], n + 1)
                nc.scalar.activation(ebuf[par_], rbuf[par_], ACT.Exp, scale=par[:, BETA:BETA + 1],
                                     bias=par[:, NABS:NABS + 1]).then_inc(s["exp_ready"], 1)

            def chunk0(c):
                act.wait_ge(s["rho_in"], 16 * (c + 1))
                guard(c, 0, 0, 0)
                guard(c, 1, 1, 1)

                def pairs(m):
                    for h in range(2):
                        exps(c, 2 * m + h, h)
                        guard(c, 2 * m + 2 + h, h, 0)
                loop(act, 0, NP // 2 - 1, [(steps, 4)], pairs)
                act.wait_ge(s["guard_ready"], (c + 1) * NP)
                act.sem_inc(s["rho_used"], 1)
                for h in range(2):
                    exps(c, NP - 2 + h, h)
                act.wait_ge(s["masked_used"], (c + 1) * NP + CREDIT)
                act.wait_ge(s["osb_stored"], 16 * c + 16)
                nc.scalar.copy(osb, PS[:, 6, :]).then_inc(s["osb_ready"], 1)
                act.wait_ge(s["osb_ready"], c + 1)
                act.sem_inc(s["out_bank_free"], 1)

            act.sem_inc(s["rho_used"], 1)
            act.sem_inc(s["out_bank_free"], 1)
            act.sem_inc(s["osb_stored"], 16)
            act.sem_inc(s["exp_ready"], CREDIT)
            act.wait_ge(s["const_done"], 1)
            nc.scalar.preload_act_table_set("natural_log_exp_and_others")
            loop(act, 0, NCH, [(steps, 2 * NP)], chunk0)
            sqrt("var")
            if LAYERS > 1:
                pe_copy(5, T[:, :], PS[:, :, :].rearrange("p b f -> p (b f)"))
                act.sem_inc(s["agg_copied"], CREDIT)
                act.sem_inc(s["mixed_copied"], CREDIT)
                for l in range(3):
                    F = D if l == 2 else F1
                    bias = par[0:F, (B1C, B2C, B3C)[l]:(B1C, B2C, B3C)[l] + 1]

                    def agg_copy(c, half):
                        act.wait_ge(s["agg_ready"], l * NCH + c + 1)
                        nc.scalar.copy(agg_sb[half][0:3 * F1, :], PS[0:3 * F1, half, :])\
                            .then_inc(s["agg_copied"], 1)

                    def relu(c, half):
                        act.wait_ge(s["mixed_ready"], l * NCH + c + 1)
                        if l < 2:
                            act.wait_ge(s["t20_ready"], l * NCH + c + 1)
                            dst = h_sb[half][0:F, :]
                        else:
                            dst = T[:, bass.ds(c * CH, CH)]
                        nc.scalar.activation(dst, PS[0:F, 2 + half, :], ACT.Relu, bias=bias)\
                            .then_inc(s["mixed_copied"], 1)

                    agg_copy(0, 0)
                    with act.Fori(0, NCH // 2 - 1) as m:
                        agg_copy(2 * m + 1, 1)
                        relu(2 * m, 0)
                        agg_copy(2 * m + 2, 0)
                        relu(2 * m + 1, 1)
                    agg_copy(NCH - 1, 1)
                    relu(NCH - 2, 0)
                    relu(NCH - 1, 1)
                sqrt("var")
            if LAYERS > 2:
                sqrt("ss")
                pe_copy(9, T[:, :], PS[:, :, :].rearrange("p b f -> p (b f)"))
                sqrt("ss")
                sqrt("ss")
                fn(S("y1"), S("y0"), ACT.Ln, bias=1.0)
                fn(S("y2"), S("y0"), ACT.Ln, scale=-1.0, bias=1.0)
                fn(S("y0"), S("y1"), ACT.Tanh)
                fn(S("y2"), S("y1"), ACT.Tanh)
                sqrt("ss")
                fn(S("y1"), S("y0"), ACT.Ln, bias=1.0)
                fn(S("y2"), S("y0"), ACT.Ln, scale=-1.0, bias=1.0)
                pe_copy(11, T[:, :], PS[:, :, :].rearrange("p b f -> p (b f)"))
                pe_copy(12, X2[0:NT, 4 * P:5 * P], PS[0:NT, 7, 0:P])
                for k, dst in enumerate((augS, augM)):
                    pe_copy(13 + k, dst[0:AUG, :],
                            PS[:, :, :].bitcast(BF16).rearrange("p b f -> p (b f)")[0:AUG, 0:N])

                w = PS[:, 4:8, :].rearrange("p b f -> p (b f)")

                def lnw(n, par_):
                    act.wait_ge(s["guard2_ready"], n + 1)
                    nc.scalar.activation(a2[par_], a2[par_], ACT.Ln, scale=-2.0).then_inc(s["lnw_ready"], 1)

                def factor(n, par_, more):
                    act.wait_ge(s["clip_ready"], n + 1)
                    steps.link(nc.scalar.activation(w, b2b[par_], ACT.Exp, scale=-1.0))
                    steps.link(nc.scalar.activation(w, w, ACT.Ln, scale=-1.0, bias=1.0))
                    act.wait_ge(s["artanh_ready"], n + 1)
                    nc.scalar.activation(e2, w, ACT.Exp, scale=0.5).then_inc(s["half_ready"], 1)
                    act.wait_ge(s["half_ready"], n + 1)
                    nc.scalar.activation(e2, e2, ACT.Ln, bias=1.0).then_inc(s["ln1p_ready"], 1)
                    if more:
                        lnw(n + 1, 1 - par_)
                    act.wait_ge(s["expo_ready"], n + 1)
                    nc.scalar.activation(a2[par_], a2[par_], ACT.Exp, scale=-1.0).then_inc(s["weight_exp_ready"], 1)

                act.sem_inc(s["o2_stored"], 16)
                act.sem_inc(s["o2_bank_free"], 1)
                nc.scalar.preload_act_table_set("natural_log_exp_and_others")
                lnw(0, 0)

                def quads(m):
                    factor(2 * m, 0, True)
                    factor(2 * m + 1, 1, True)
                loop(act, 0, NF // 2 - 1, [(steps, 4)], quads)
                factor(NF - 2, 0, True)
                factor(NF - 1, 1, False)

                def sigmoid(c, J, b):
                    act.wait_ge(s["sig_used"], c * NT + J + 1)
                    nc.scalar.activation(sig[b], sbrow[:, bass.ds(c * CH, CH)], ACT.Sigmoid,
                                         bias=S("sc_j")[:, bass.ds(J, 1)]).then_inc(s["sig_ready"], 1)

                nc.scalar.preload_act_table_set("sigmoid_and_others")
                act.wait_ge(s["srow_in"], 16)
                with act.Fori(0, NCH) as c:
                    with act.Fori(0, NT // 2) as m:
                        sigmoid(c, 2 * m, 0)
                        sigmoid(c, 2 * m + 1, 1)
                    act.wait_ge(s["c_used"], (c + 1) * NP + NW)
                    act.wait_ge(s["o2_stored"], 16 * c + 16)
                    nc.scalar.copy(osb2, PS[:, 6, :]).then_inc(s["o2_copied"], 1)
                    act.wait_ge(s["o2_copied"], c + 1)
                    act.sem_inc(s["o2_bank_free"], 1)
                sqrt("ss")
                fn(S("y0"), S("y1"), ACT.Tanh)
                sqrt("ss")
                fn(S("y1"), S("y0"), ACT.Ln, bias=1.0)
                fn(S("y2"), S("y0"), ACT.Ln, scale=-1.0, bias=1.0)
                sqrt("ss")
                fn(S("y0"), S("y1"), ACT.Tanh)
                sqrt("var")
            if LAYERS > 3:
                pe_copy(17, T[:, :], PS[:, :, :].rearrange("p b f -> p (b f)"))
                fn(par[:, T1:T1 + 1], par[:, T0:T0 + 1], ACT.Square)
                fn(par[:, S0:S0 + 1], par[:, T2:T2 + 1], ACT.Exp)

                def out3(c, half):
                    act.wait_ge(s["agg3_ready"], c + 1)
                    nc.scalar.copy(T[:, bass.ds(c * CH, CH)], PS[:, half, :]).then_inc(s["agg3_free"], 1)

                act.sem_inc(s["agg3_free"], CREDIT)
                with act.Fori(0, NCH // 2) as m:
                    out3(2 * m, 0)
                    out3(2 * m + 1, 1)
                sqrt("var")

        @block.vector
        def _(dve):
            steps = Chain(dve, s["dve_step"])
            link = steps.link
            V = nc.vector
            n_act, n_pe, n_dma = [0], [0], [0]

            def bc(sc):
                return sc.unsqueeze(2).to_broadcast([P, NT, D])

            def bf(v):
                return v.unsqueeze(1).to_broadcast([P, NT, D])

            def act_do():
                n_act[0] += 1
                dve.sem_inc(s["act_asked"], 1)
                dve.wait_ge(s["act_answered"], n_act[0])

            def pe_do(wait=True):
                n_pe[0] += 1
                dve.sem_inc(s["pe_asked"], 1)
                if wait:
                    dve.wait_ge(s["pe_answered"], n_pe[0])

            def dma_do(wait=True):
                n_dma[0] += 1
                dve.sem_inc(s["dma_asked"], 1)
                if wait:
                    dve.wait_ge(s["dma_answered"], 16 * n_dma[0])

            def tt(o, a, b, op):
                link(V.tensor_tensor(o, a, b, op))

            def ts(o, a, s1, op0, s2=None, op1=ALU.bypass):
                link(V.tensor_scalar(o, a, s1, s2, op0, op1))

            def stt(o, a, sc, b, op0, op1):
                link(V.scalar_tensor_tensor(out=o, in0=a, scalar=sc, in1=b, op0=op0, op1=op1))

            def rec(o, a):
                link(V.reciprocal(o, a))

            def sum_of_products(name, a, b, tmp):
                tt(tmp, a, b, ALU.mult)
                link(V.tensor_reduce(S(name), tmp, AX.X, ALU.add))

            def sqrt(dst, name):
                act_do()
                rec(S("y1"), S("y0"))
                tt(S("y1"), S("y1"), S(name), ALU.mult)
                tt(S("y0"), S("y0"), S("y1"), ALU.add)
                ts(dst, S("y0"), 0.5, ALU.mult)

            def layer_norm(src, tmp):
                link(V.tensor_reduce(S("mean"), src, AX.X, ALU.add))
                ts(S("mean"), S("mean"), 1.0 / D, ALU.mult)
                tt(src, src, bc(S("mean")), ALU.subtract)
                sum_of_products("var", src, src, tmp)
                ts(S("var"), S("var"), 1.0 / D, ALU.mult, LN_EPS, ALU.add)
                sqrt(S("rstd"), "var")
                rec(S("rstd"), S("rstd"))
                tt(A[:, :, :], src, bc(S("rstd")), ALU.mult)

            def split3(dst, src, rest):
                link(V.tensor_copy(dst[0], src))
                tt(rest, src, dst[0], ALU.subtract)
                link(V.tensor_copy(dst[1], rest))
                tt(rest, rest, dst[1], ALU.subtract)
                link(V.tensor_copy(dst[2], rest))

            dve.wait_ge(s["x_loaded"], 16)
            sum_of_products("ss", A[:, :, :], A[:, :, :], R)
            ts(S("ss"), S("ss"), TINY_NORM ** 2, ALU.max)
            sqrt(S("rho"), "ss")
            rec(S("rho"), S("rho"))
            ts(S("erho"), S("rho"), COS_EPS, ALU.mult)
            tt(R, A[:, :, :], bc(S("rho")), ALU.mult)
            dve.wait_ge(s["par_loaded"], 16 * 7)
            ts(par[:, T0:T0 + 1], par[:, BETA:BETA + 1], -1.0, ALU.mult)
            tt(par[:, NABS:NABS + 1], par[:, T0:T0 + 1], par[:, BETA:BETA + 1], ALU.min)
            dve.wait_ge(s["const_done"], 1)
            pe_do()
            dve.wait_ge(s["copy_answered"], 1)
            dma_do(False)
            pe_do()

            def evacuate(c, jp, par_):
                n = c * NP + jp
                dve.wait_ge(s["tp_ready"], n + 1 + 2 * CREDIT)
                V.tensor_scalar(adjU[:, bass.ds(2 * jp, 2), bass.ds(c * CH, CH)],
                                PS[:, 4 + par_, :].bitcast(BF16).rearrange("p (j x) -> p j x", j=2),
                                EDGE8, None, ALU.mult).then_inc(s["tp_free"], 1)

            def product(c, jp, par_):
                n = c * NP + jp
                dve.wait_ge(s["cos_sum_ready"], n + 1)
                dve.wait_ge(s["guard_ready"], n + 1)
                V.tensor_tensor(rbuf[par_], PS[:, 2 * par_:2 * par_ + 2, :].rearrange("p b f -> p (b f)"),
                                rbuf[par_], ALU.mult).then_inc(s["cos_free"], 1)

            def mask(c, jp, par_):
                dve.wait_ge(s["exp_ready"], c * NP + jp + 1 + CREDIT)
                e = ebuf[par_].rearrange("p (j x) -> p j x", j=2)
                V.tensor_tensor(e, e, adjU[:, bass.ds(2 * jp, 2), bass.ds(c * CH, CH)], ALU.mult)\
                    .then_inc(s["masked_ready"], 1)

            def chunk0(c, more):
                dve.wait_ge(s["tp_free"], (c + 1) * NP + CREDIT)
                product(c, 0, 0)

                def turn(jp, h, evac=True):
                    product(c, jp + 1, 1 - h)
                    mask(c, jp, h)
                    if more and evac:
                        evacuate(c + 1, jp - 1, 1 - h)

                turn(0, 0, False)
                turn(1, 1)

                def pairs(m):
                    turn(2 * m, 0)
                    turn(2 * m + 1, 1)
                loop(dve, 1, NP // 2 - 1, [], pairs)
                turn(NP - 2, 0)
                mask(c, NP - 1, 1)
                if more:
                    evacuate(c + 1, NP - 2, 0)
                    evacuate(c + 1, NP - 1, 1)
                dve.wait_ge(s["z_ready"], c + 2)
                V.tensor_copy(S("z")[:, bass.ds(c * KT, KT)], PS[:, 7, 0:KT]).then_inc(s["z_free"], 1)

            dve.sem_inc(s["tp_free"], CREDIT)
            dve.sem_inc(s["cos_free"], CREDIT)
            dve.sem_inc(s["z_free"], 1)
            with dve.Fori(0, NP // 2) as m:
                for h in range(2):
                    evacuate(0, 2 * m + h, h)
            with dve.Fori(0, NCH - 1) as c:
                chunk0(c, True)
            chunk0(NCH - 1, False)
            dve.wait_ge(s["z_free"], NCH + 1)
            pe_do()
            csum = X2[:, 0:P]
            ts(csum, PS[:, 0, 0:P], EDGE8 * NO_NEIGHBOUR, ALU.mult)
            pe_do()
            ts(S("z"), S("z"), EDGE8 * NO_NEIGHBOUR * N, ALU.add)
            rec(S("z"), S("z"))
            tt(R, PSrow, bf(csum), ALU.add)
            tt(R, R, bc(S("z")), ALU.mult)
            tt(R, R, A[:, :, :], ALU.add)
            layer_norm(R, TMP)

            if LAYERS > 1:
                for _ in range(7):
                    dma_do()
                pe_do()
                dve.wait_ge(s["copy_answered"], 3)
                pe_do()
                v = PS[:, :, 0:4 * F1].rearrange("p b (k f) -> p b k f", f=F1)
                rest = TMP.rearrange("p t f -> p (t f)")[:, 0:NT * F1].rearrange("p (b k f) -> p b k f", k=4, f=F1)
                hv = hs1[0].rearrange("p (b k) f -> p b k f", k=4)
                split3([hv[:, :, :, q * F1:(q + 1) * F1] for q in range(3)], v, rest)
                tt(stack[0:3 * F1, 0:F1], ident[0:3 * F1, 0:F1], ident[0:3 * F1, F1:2 * F1], ALU.add)
                tt(stack[0:3 * F1, 0:F1], stack[0:3 * F1, 0:F1], ident[0:3 * F1, 2 * F1:3 * F1], ALU.add)
                ts(stack[0:3 * F1, 0:2 * P], stack[0:3 * F1, 0:2 * P], 1.0 / EDGE_PE, ALU.mult)
                dve.sem_inc(s["split_ready"], CREDIT)
                restc = [area((16 + b) * KW, KT * F1).rearrange("p (k f) -> p k f", f=F1) for b in range(2)]
                for l in range(2):
                    nxt = hs1[(l + 1) % 2]

                    def split(c, half):
                        dve.wait_ge(s["t20_ready"], l * NCH + c + 1 + CREDIT)
                        v = PS[:, 4 + half, 0:KT * F1].rearrange("p (k f) -> p k f", f=F1)
                        split3([nxt[:, bass.ds(c * KT, KT), q * F1:(q + 1) * F1] for q in range(3)], v, restc[half])
                        dve.sem_inc(s["split_ready"], 1)

                    def two(m):
                        split(2 * m, 0)
                        split(2 * m + 1, 1)
                    loop(dve, 0, NCH // 2, [(steps, 10)], two)
                dve.wait_ge(s["mixed_copied"], 3 * NCH + CREDIT)
                pe_do()
                tt(R, PSrow, A[:, :, :], ALU.add)
                ts(R, R, 0.0, ALU.max)
                tt(R, R, A[:, :, :], ALU.add)
                layer_norm(R, TMP)

            def clip_norm(dst, name):
                ts(S(name), S(name), EPS * EPS, ALU.max)
                sqrt(dst, name)

            def radius(dst, n):
                rec(dst, n)
                ts(dst, dst, MAXNORM, ALU.mult, 1.0, ALU.min)

            def artanh(dst, n):
                ts(S("y0"), n, ATANH_MAX, ALU.min)
                act_do()
                act_do()
                tt(S("y1"), S("y1"), S("y2"), ALU.subtract)
                ts(dst, S("y1"), 0.5, ALU.mult)

            def add_weights(x2, xy, y2, c1, c2):
                tt(S("y1"), x2, y2, ALU.mult)
                stt(S("y1"), xy, 2.0, S("y1"), ALU.mult, ALU.add)
                ts(S("y1"), S("y1"), 1.0, ALU.add, EPS, ALU.max)
                rec(S("y1"), S("y1"))
                stt(S("y2"), xy, 2.0, y2, ALU.mult, ALU.add)
                stt(c1, S("y2"), 1.0, S("y1"), ALU.add, ALU.mult)
                ts(S("y2"), x2, -1.0, ALU.mult, 1.0, ALU.add)
                tt(c2, S("y2"), S("y1"), ALU.mult)

            if LAYERS > 2:
                Wb, hbB, wlB, wrB = (X2[:, k * P:(k + 1) * P] for k in range(4))
                WT = X2[:, 5 * P:6 * P]
                for _ in range(5):
                    dma_do()
                pe_do()
                link(V.tensor_copy(WT, PS[:, 0, 0:P]))
                sum_of_products("ss", A[:, :, :], A[:, :, :], TMP)
                clip_norm(S("n"), "ss")
                radius(S("f"), S("n"))
                tt(R, A[:, :, :], bc(S("f")), ALU.mult)
                tt(S("n"), S("n"), S("f"), ALU.mult)
                pe_do()
                dve.wait_ge(s["copy_answered"], 4)
                pe_do()
                link(V.tensor_copy(A[:, :, :], PSrow))
                sum_of_products("x2", A[:, :, :], A[:, :, :], TMP)
                link(V.tensor_copy(S("ss"), S("x2")))
                clip_norm(S("m"), "ss")
                tt(TMP[:, 0, :], hbB, hbB, ALU.mult)
                link(V.tensor_reduce(par[:, T0:T0 + 1], TMP[:, 0, :], AX.X, ALU.add))
                tt(S("ss"), par[:, T0:T0 + 1].to_broadcast([P, NT]), par[:, T0:T0 + 1].to_broadcast([P, NT]), ALU.max)
                clip_norm(S("nb"), "ss")
                artanh(S("at"), S("n"))
                rec(S("y1"), S("n"))
                tt(S("y1"), S("y1"), S("m"), ALU.mult)
                tt(S("y1"), S("y1"), S("at"), ALU.mult)
                act_do()
                rec(S("g"), S("m"))
                tt(S("g"), S("g"), S("y0"), ALU.mult)
                ts(S("n"), S("y0"), EPS, ALU.max)
                radius(S("f"), S("n"))
                tt(S("g"), S("g"), S("f"), ALU.mult)
                tt(S("x2"), S("x2"), S("g"), ALU.mult)
                tt(S("x2"), S("x2"), S("g"), ALU.mult)
                link(V.tensor_copy(S("y1"), S("nb")))
                act_do()
                ts(S("n"), S("y2"), EPS, ALU.max)
                radius(S("f"), S("n"))
                tt(S("n"), S("n"), S("f"), ALU.mult)
                rec(S("gb"), S("nb"))
                tt(S("gb"), S("gb"), S("n"), ALU.mult)
                tt(S("yy"), S("n"), S("n"), ALU.mult)
                sum_of_products("xy", A[:, :, :], bf(hbB), TMP)
                tt(S("xy"), S("xy"), S("g"), ALU.mult)
                tt(S("xy"), S("xy"), S("gb"), ALU.mult)
                add_weights(S("x2"), S("xy"), S("yy"), S("c1"), S("c2"))
                tt(S("c1"), S("c1"), S("g"), ALU.mult)
                tt(S("c2"), S("c2"), S("gb"), ALU.mult)
                tt(A[:, :, :], A[:, :, :], bc(S("c1")), ALU.mult)
                tt(TMP, bf(hbB), bc(S("c2")), ALU.mult)
                tt(A[:, :, :], A[:, :, :], TMP, ALU.add)
                sum_of_products("ss", A[:, :, :], A[:, :, :], TMP)
                clip_norm(S("n"), "ss")
                radius(S("f"), S("n"))
                tt(A[:, :, :], A[:, :, :], bc(S("f")), ALU.mult)
                sum_of_products("x2", A[:, :, :], A[:, :, :], TMP)
                tt(S("n"), S("n"), S("f"), ALU.mult)
                artanh(S("at"), S("n"))
                rec(S("g"), S("n"))
                tt(S("g"), S("g"), S("at"), ALU.mult)
                sum_of_products("sc_i", A[:, :, :], bf(wlB), TMP)
                tt(S("sc_i"), S("sc_i"), S("g"), ALU.mult)
                sum_of_products("sc_j", A[:, :, :], bf(wrB), TMP)
                tt(S("sc_j"), S("sc_j"), S("g"), ALU.mult)
                ts(S("sc_j"), S("sc_j"), par[:, ATTB:ATTB + 1], ALU.add)
                ts(S("b"), S("x2"), -1.0, ALU.mult, 1.0, ALU.add)
                rec(S("ib"), S("b"))
                tt(S("kap"), S("x2"), S("ib"), ALU.mult)
                ts(S("ub"), S("x2"), 1.0, ALU.add)
                tt(S("ub"), S("ub"), S("ib"), ALU.mult)
                ts(S("ub"), S("ub"), 0.5 / EDGE8, ALU.mult)
                tt(R, A[:, :, :], bc(S("ib")), ALU.mult)
                pe_do()
                dve.wait_ge(s["copy_answered"], 5)
                ts(S("y1"), S("x2"), 1.0, ALU.add)
                rec(S("y1"), S("y1"))
                tt(R, A[:, :, :], bc(S("y1")), ALU.mult)
                dma_do()
                pe_do()
                dve.wait_ge(s["copy_answered"], 6)
                dma_do()
                tS, tM = augrows
                for k, name in enumerate(("ib", "kap")):
                    pb = [area(16 * KW + 512 + 16 * q, 16, BF16) for q in range(3)]
                    split3(pb, S(name), TMP[:, 8, 0:NT])
                    for col, (i, j) in enumerate(((0, 0), (0, 1), (1, 0), (0, 2), (2, 0), (1, 1))):
                        link(V.tensor_copy(tS[:, :, 6 * k + col], pb[i]))
                        ts(tM[:, :, 6 * k + col], pb[j], -0.5, ALU.mult)
                link(V.memset(A[:, :, :], 0.0))
                pe_do()
                dve.wait_ge(s["copy_answered"], 7)
                pe_do()
                dve.wait_ge(s["copy_answered"], 8)
                pe_do(False)

                w_in = PS[:, 0:4, :].rearrange("p b f -> p (b f)")
                w = PS[:, 4:8, :].rearrange("p b f -> p (b f)")

                def guard(n, b):
                    dve.wait_ge(s["dist_ready"], n + 1)
                    dve.wait_ge(s["factor_ready"], n + 1)
                    V.tensor_scalar(a2[b], w_in, -0.5, None, ALU.min).then_inc(s["guard2_ready"], 1)

                def clip(m, n, b):
                    dve.wait_ge(s["lnw_ready"], n + 1)
                    dve.wait_ge(s[f"factor_stored{b}"], 16 * m + 16)
                    V.tensor_scalar(b2b[b], a2[b], LNW_MIN, LNW_MAX, ALU.max, ALU.min)\
                        .then_inc(s["clip_ready"], 1)

                def factor(m, b, left):
                    n = 2 * m + b
                    dve.wait_ge(s["half_ready"], n + 1)
                    V.scalar_tensor_tensor(out=a2[b], in0=w, scalar=0.5, in1=a2[b],
                                           op0=ALU.mult, op1=ALU.add).then_inc(s["expo_ready"], 1)
                    dve.wait_ge(s["ln1p_ready"], n + 1)
                    V.scalar_tensor_tensor(out=b2b[b], in0=e2, scalar=2.0, in1=b2b[b],
                                           op0=ALU.mult, op1=ALU.add).then_inc(s["artanh_ready"], 1)
                    if left >= 1:
                        clip(m + b, n + 1, 1 - b)
                    if left >= 2:
                        guard(n + 2, b)

                dve.sem_inc(s["artanh_ready"], 1)
                for b in range(2):
                    dve.sem_inc(s[f"factor_stored{b}"], 16)
                guard(0, 0)
                guard(1, 1)
                clip(0, 0, 0)

                def quads(m):
                    factor(m, 0, 2)
                    factor(m, 1, 2)
                loop(dve, 0, NF // 2 - 1, [], quads)
                factor(NF // 2 - 1, 0, 1)
                factor(NF // 2 - 1, 1, 0)

                dve.sem_inc(s["sig_used"], CREDIT)
                dve.sem_inc(s["tf_free"], CREDIT)
                dve.sem_inc(s["u_free"], 1)

                def weigh(c, jp, b, factor_of, used):
                    n = c * NP + jp
                    dve.wait_ge(s["c_used"], n + 1)
                    dve.wait_ge(s["c_added"], n + 1)
                    for jj in range(2):
                        dve.wait_ge(s["sig_ready"], 2 * n + jj + 1)
                        V.scalar_tensor_tensor(out=wbuf[b][:, jj * CH:(jj + 1) * CH], in0=sig[jj],
                                               scalar=S("ub")[:, bass.ds(2 * jp + jj, 1)],
                                               in1=factor_of(jj), op0=ALU.mult, op1=ALU.mult)\
                            .then_inc(s["sig_used"], 1)
                    dve.wait_ge(s["sig_used"], 2 * n + 2 + CREDIT)
                    if used:
                        dve.sem_inc(s[used], 1)
                    w = wbuf[b].rearrange("p (j x) -> p j x", j=2)
                    V.tensor_tensor(w, w, adjU[:, bass.ds(2 * jp, 2), c * CH:(c + 1) * CH], ALU.mult)\
                        .then_inc(s["c_ready"], 1)

                for c in range(NCH):
                    def upper(q, b):
                        dve.wait_ge(s[f"factor_in{b}"], 16 * (c * NQ // 2 + 1) + 8 * (q - b))
                        for h in range(2):
                            weigh(c, 2 * q + h, 2 * b + h, lambda jj: fin[b][:, (2 * h + jj) * CH:(2 * h + jj + 1) * CH],
                                  "fin_used_dve" if h else None)

                    def two(m):
                        upper(2 * m, 0)
                        upper(2 * m + 1, 1)
                    if c >= 1:
                        loop(dve, 0, (c + 1) // 2, [], two)
                    if c % 2 == 0:
                        upper(c, 0)
                    before = sum(2 * (NQ - 1 - k) for k in range(c))

                    def lower(q, b):
                        for h in range(2):
                            dve.wait_ge(s["tf_ready"], before + 2 * (q - c - 1) + h + 1)
                            weigh(c, 2 * q + h, 2 * b + h, lambda jj: PS[:, 2 * h + jj, :], "tf_free")

                    def two_lower(m):
                        lower(2 * m, 0)
                        lower(2 * m + 1, 1)
                    if c % 2 == 0:
                        lower(c + 1, 1)
                    if c // 2 + 1 < NQ // 2:
                        loop(dve, c // 2 + 1, NQ // 2, [], two_lower)
                    dve.wait_ge(s["u_ready"], c + 2)
                    V.tensor_copy(S("u")[:, c * KT:(c + 1) * KT], PS[:, 7, 0:KT]).then_inc(s["u_free"], 1)
                dve.wait_ge(s["u_free"], NCH + 1)
                ts(S("ib"), S("x2"), 1.0, ALU.add)
                tt(R, Trow, bc(S("ib")), ALU.mult)
                dve.sem_inc(s["h_read"], 1)
                pe_do()
                link(V.tensor_copy(A[:, :, :], PSrow))
                sum_of_products("xy", R, A[:, :, :], TMP)
                stt(S("g"), S("xy"), 2.0, S("u"), ALU.mult, ALU.subtract)
                tt(A[:, :, :], A[:, :, :], bc(S("b")), ALU.mult)
                tt(TMP, R, bc(S("g")), ALU.mult)
                tt(A[:, :, :], A[:, :, :], TMP, ALU.add)
                dma_do(False)
                sum_of_products("ss", A[:, :, :], A[:, :, :], TMP)
                link(V.tensor_copy(S("at"), S("ss")))
                clip_norm(S("n"), "ss")
                ts(S("y2"), S("b"), EPS, ALU.max)
                rec(S("y2"), S("y2"))
                tt(S("y1"), S("y2"), S("n"), ALU.mult)
                act_do()
                rec(S("gb"), S("n"))
                tt(S("gb"), S("gb"), S("y0"), ALU.mult)
                tt(S("yy"), S("gb"), S("gb"), ALU.mult)
                tt(S("yy"), S("yy"), S("at"), ALU.mult)
                sum_of_products("xy", R, A[:, :, :], TMP)
                tt(S("xy"), S("xy"), S("gb"), ALU.mult)
                add_weights(S("x2"), S("xy"), S("yy"), S("c1"), S("c2"))
                tt(S("c2"), S("c2"), S("gb"), ALU.mult)
                tt(R, R, bc(S("c1")), ALU.mult)
                tt(A[:, :, :], A[:, :, :], bc(S("c2")), ALU.mult)
                tt(R, R, A[:, :, :], ALU.add)
                sum_of_products("ss", R, R, TMP)
                clip_norm(S("n"), "ss")
                radius(S("f"), S("n"))
                tt(S("m"), S("n"), S("f"), ALU.mult)
                ts(S("m"), S("m"), EPS, ALU.max)
                artanh(S("at"), S("m"))
                rec(S("g"), S("m"))
                tt(S("g"), S("g"), S("at"), ALU.mult)
                tt(S("g"), S("g"), S("f"), ALU.mult)
                tt(R, R, bc(S("g")), ALU.mult)
                ts(R, R, 0.0, ALU.max)
                sum_of_products("ss", R, R, TMP)
                clip_norm(S("n"), "ss")
                link(V.tensor_copy(S("y1"), S("n")))
                act_do()
                rec(S("g"), S("n"))
                tt(S("g"), S("g"), S("y0"), ALU.mult)
                ts(S("n"), S("y0"), EPS, ALU.max)
                radius(S("f"), S("n"))
                tt(S("g"), S("g"), S("f"), ALU.mult)
                tt(R, R, bc(S("g")), ALU.mult)
                dve.wait_ge(s["dma_answered"], 16 * n_dma[0])
                tt(R, R, T[:, :].rearrange("p (t f) -> p t f", f=D), ALU.add)
                layer_norm(R, TMP)

            if LAYERS > 3:
                for _ in range(2):
                    dma_do()
                pe_do()
                dve.wait_ge(s["copy_answered"], 9)
                pe_do()
                restf = X2[:, 2 * P:2 * P + 4 * P].rearrange("p (k f) -> p k f", f=P)
                Bb = X2[:, P:2 * P].unsqueeze(1).to_broadcast([P, KT, D])

                def split_h(g):
                    v = PSrow[:, g * KT:(g + 1) * KT, :]
                    tt(restf, v, Bb, ALU.add)
                    parts = [hs3[q][:, g * KT:(g + 1) * KT, :] for q in range(3)]
                    link(V.tensor_copy(parts[0], restf))
                    tt(restf, restf, parts[0], ALU.subtract)
                    link(V.tensor_copy(parts[1], restf))
                    tt(restf, restf, parts[1], ALU.subtract)
                    link(V.tensor_copy(parts[2], restf))
                for g in range(NCH):
                    split_h(g)
                pe_do(False)

                link(V.memset(par[:, T2:T2 + 1], R_FLOOR))
                rec(par[:, T2:T2 + 1], par[:, T2:T2 + 1])
                rec(par[:, T1:T1 + 1], par[:, MU:MU + 1])
                tt(par[:, T0:T0 + 1], par[:, T2:T2 + 1], par[:, T1:T1 + 1], ALU.subtract)
                act_do()
                tt(par[:, T2:T2 + 1], par[:, SIG:SIG + 1], par[:, SIG:SIG + 1], ALU.mult)
                ts(par[:, T2:T2 + 1], par[:, T2:T2 + 1], -2.0, ALU.mult)
                rec(par[:, T2:T2 + 1], par[:, T2:T2 + 1])
                tt(par[:, T2:T2 + 1], par[:, T2:T2 + 1], par[:, T1:T1 + 1], ALU.mult)
                act_do()

                def masks(c):
                    m = adjU[:, :, bass.ds(c * CH, CH)]
                    link(V.tensor_scalar(m, m, 0.5 * EDGE8, EDGE8, ALU.is_lt, ALU.mult))
                    for k in range(KT):
                        d = adjU[:, bass.ds(c * KT + k, 1), bass.ds(c * CH + k * P, P)]
                        ins = V.tensor_tensor(d, d, not_i[:, :].unsqueeze(1), ALU.mult)
                    ins.then_inc(s["mask_ready"], 1)
                loop(dve, 0, NCH, [(steps, 1)], masks)
                dve.wait_ge(s["agg3_free"], NCH + CREDIT)
                pe_do()
                ts(par[:, S0:S0 + 1], par[:, S0:S0 + 1], 1.0 / EDGE_PE, ALU.mult)
                stt(R, PSrow, par[:, S0:S0 + 1], A[:, :, :], ALU.mult, ALU.add)
                layer_norm(R, TMP)
            dma_do(False)


_INS = ["x", "adj", "L0_gnn_beta", "L1_gnn_W1", "L1_gnn_b1", "L1_gnn_W2", "L1_gnn_b2", "L1_gnn_W3", "L1_gnn_b3",
        "L2_gnn_W", "L2_gnn_b", "L2_gnn_att_wl", "L2_gnn_att_wr", "L2_gnn_att_b",
        "L3_gnn_W", "L3_gnn_B", "L3_gnn_mu", "L3_gnn_sigma"]
_OUTS = [((4096, 128), "float32")]


def kernel(**inputs):
    import numpy as _np
    import concourse.bacc as _bacc
    from concourse import mybir as _mybir
    from concourse.bass_utils import run_bass_kernel_spmd as _run

    nc = _bacc.Bacc("TRN2", target_bir_lowering=False, num_devices=1)
    arrays, args = {}, []
    for name in _INS:
        a = _np.ascontiguousarray(inputs[name])
        arrays[f"in_{name}_dram"] = a
        args.append(nc.dram_tensor(f"in_{name}_dram", a.shape, _mybir.dt.from_np(a.dtype), kind="ExternalInput").ap())
    for i, (shape, dtype) in enumerate(_OUTS):
        dt = _mybir.dt.from_np(_np.dtype(dtype))
        args.append(nc.dram_tensor(f"out_{i}_dram", shape, dt, kind="ExternalOutput").ap())
    gnn_stack(nc, *args)
    r = _run(nc, [arrays], core_ids=[0])
    return r.results[0]["out_0_dram"]
```

```python
from contextlib import ExitStack

import concourse.bass as bass
from concourse import mybir

F32 = mybir.dt.float32
BF16 = mybir.dt.bfloat16
F16 = mybir.dt.float16
FP8 = mybir.dt.float8e4
U8 = mybir.dt.uint8
ALU = mybir.AluOpType
ACT = mybir.ActivationFunctionType
AX = mybir.AxisListType

P = 128
CH = 512
COS_EPS = 1e-7
NO_NEIGHBOUR = 1e-30
TINY_NORM = 1e-13
XS = 2.0 ** 12
LN_EPS = 1e-5
EPS = 1e-15
MAXNORM = 0.999
HS = 2.0 ** 14
X_MAX = 12.0
R_FLOOR = 1e-15
ATANH_MAX = 0.9999899864196777
EDGE8 = 64.0
EDGE_PE = 2.0
CREDIT = 2


class Chain:

    def __init__(self, eng, sem):
        self.eng, self.sem, self.n = eng, sem, 0

    def mark(self, ins):
        ins.then_inc(self.sem, 1)
        self.n = self.n + 1
        return self.n

    def wait(self, n):
        self.eng.wait_ge(self.sem, n)

    def link(self, ins):
        self.wait(self.mark(ins))


def loop(eng, start, end, chains, body):
    at = [ch.n for ch, _ in chains]
    with eng.Fori(start, end) as i:
        for (ch, steps), n0 in zip(chains, at):
            ch.n = n0 + (i - start) * steps
        want = [ch.n for ch, _ in chains]
        body(i)
    for (ch, steps), n0 in zip(chains, at):
        ch.n = n0 + (end - start) * steps


def gnn_stack(nc, x, adj, beta, W1, b1, W2, b2, W3, b3, hW, hb, att_wl, att_wr, att_b,
              W, B, mu, sigma, out, LAYERS=4):
    import math

    N, D = x.shape
    F1 = W1.shape[1]
    NT = N // P
    NCH = N // CH
    KT = CH // P
    NP = NT // 2
    STG = 2
    NPC = NT // STG
    AUG = 12
    ATANH2_MAX = math.log((1.0 + ATANH_MAX) / (1.0 - ATANH_MAX))
    W_FLOOR = 1.0 + 2.0 ** -23
    assert D == P and F1 == W2.shape[1] and W3.shape[0] == F1

    ctx = ExitStack()
    with ctx:
        def sb(name, shape, dt=F32):
            return ctx.enter_context(nc.sbuf_tensor(name, shape, dt))

        def sem(name):
            return ctx.enter_context(nc.semaphore(name))

        def dram(name, shape, dt=F32):
            return nc.dram_tensor(name, shape, dt, kind="Internal").ap()

        adjT = sb("adjT", [P, NT, N], FP8)
        adjU = adjT[:, :, :].bitcast(U8)
        A = sb("A", [P, NT, D])
        T = sb("T", [P, N])
        arena = sb("arena", [P, 42 * 256])
        ident = sb("ident", [P, P])
        identb = sb("identb", [P, P], BF16)
        DT = 20
        not_i = sb("not_i", [P, P], BF16)
        ones = sb("ones", [P, P])
        NS = 33
        scal = sb("scal", [P, NS, NT])
        par = sb("par", [P, 16])
        PS = ctx.enter_context(nc.psum_tensor("PS", [P, 8, 512], F32))
        PSrow = PS[:, :, :].rearrange("p b (k f) -> p (b k) f", f=P)

        used = {}

        def S(name):
            name = {"rho": "c1", "erho": "c2", "z": "u"}.get(name, name)
            if name not in used:
                used[name] = len(used)
                assert len(used) <= NS, name
            return scal[:, used[name], :]

        def area(start, size, dt=F32):
            return arena[:, start:start + size] if dt == F32 else arena[:, start:start + size].bitcast(dt)

        KW = 256
        R = area(0, 16 * KW).rearrange("p (t f) -> p t f", f=D)
        TMP = area(16 * KW, 16 * KW).rearrange("p (t f) -> p t f", f=D)
        X2 = area(32 * KW, 10 * KW)
        csum = X2[:, 2048:2048 + P]
        X2L = X2[:, 1024:]
        Wb, hbB, wlB, wrB, srow_sb, WT = (X2L[:, k * P:(k + 1) * P] for k in range(6))
        vcols = X2L[:, 6 * P:6 * P + 3]
        wv = X2L[:, 6 * P + 4:6 * P + 7]
        stage = [area(4 * KW * b, 4 * KW) for b in range(2)]
        stage4 = [s.rearrange("p (k x) -> p k x", k=KT) for s in stage]
        stage_hi = [s.bitcast(BF16).rearrange("p (k x two) -> p k x two", k=KT, two=2) for s in stage]
        NR = 4
        rbuf = [area((8 + 4 * b) * KW, 4 * KW) for b in range(NR)]
        ebuf = [area((24 + 4 * b) * KW, 4 * KW) for b in range(2)]
        acc0 = area(32 * KW, 4 * KW)
        rho_b = [area((36 + 4 * b) * KW, 2 * KW) for b in range(2)]
        osb = area(38 * KW, 2 * KW)
        mid = area(40 * KW, 2 * KW)
        That = T[:, :].bitcast(F16)
        hi, lo = That[:, 0:N], That[:, N:2 * N]
        hs1 = [area(KW * 4 * b, KW * 4, BF16)[:, 0:NT * 3 * F1].rearrange("p (t f) -> p t f", f=3 * F1)
               for b in range(2)]
        agg_sb = [area((8 + 2 * b) * KW, 2 * KW) for b in range(2)]
        h_sb = [area((12 + 2 * b) * KW, 2 * KW) for b in range(2)]
        stack = area(32 * KW, 2 * KW)
        w_small = area(34 * KW, 2 * KW)
        NB = 4
        wh = [PS[:, 2 * b:2 * b + 2, :].rearrange("p b f -> p (b f)") for b in range(NB)]
        lnw = [area(4 * b * KW, 4 * KW) for b in range(NB)]
        isq = [area((16 + 4 * b) * KW, 4 * KW) for b in range(NB)]
        fac = [area((32 + 4 * b) * KW, 4 * KW) for b in range(2)]
        augS = A[:, 0:16, :].rearrange("p t f -> p (t f)").bitcast(BF16)
        augM = A[:, 16:32, :].rearrange("p t f -> p (t f)").bitcast(BF16)
        def aug_ps(k):
            return PS[:, 4 * k:4 * k + 4, :].bitcast(BF16).rearrange("p b f -> p (b f)")[0:AUG, 0:N]

        augrows = [area((32 + k) * KW, NT * AUG // 2, BF16).rearrange("p (t a) -> p t a", a=AUG) for k in range(2)]
        NW = 4
        sig = [area(2 * b * KW, 2 * KW) for b in range(NW)]
        wbuf = [area((8 + 4 * b) * KW, 4 * KW) for b in range(NW)]
        acc2 = [area((24 + 8 * b) * KW, 4 * KW) for b in range(2)]
        osb2 = area(28 * KW, 2 * KW)
        srow = [area((40 - 10 * b) * KW, 2 * KW) for b in range(2)]
        Trow = T[:, :].rearrange("p (t f) -> p t f", f=D)
        fin = [A[:, 16 * b:16 * (b + 1), :].rearrange("p t f -> p (t f)") for b in range(2)]
        hs3 = [area(8 * KW * s, 8 * KW, F16).rearrange("p (t f) -> p t f", f=D) for s in range(2)]
        W3s, B3s, hscale, absw = (X2[:, k * P:(k + 1) * P] for k in range(4))
        hscale_c = X2[:, 4 * P:4 * P + 1]

        numT_d = dram("numT", [P, N])
        row_d = dram("row_scalar", [NT, P])
        x_d = dram("x_spill", [P, NT * D])
        h_d = dram("h_spill", [P, NT * D])
        f_d = dram("factor", [N, N])
        f_tiles = f_d.rearrange("(g j p) (c x) -> g c p j x", j=4, p=P, x=CH)
        f_pairs = f_d.rearrange("(g j p) (c x) -> g c p j x", j=2, p=P, x=CH)

        s = {n: sem(n) for n in (
            "x_loaded", "par_loaded", "const_ready", "const_done",
            "act_asked", "act_answered", "dve_step", "act_step", "pe_step",
            "pe_asked", "pe_answered", "columns_ready", "columns_copied", "row_copied", "low_ready", "part_ready", "ln_ready",
            "proj_ready", "proj_copied", "extra_ready", "aug_copied", "hr_asked", "hr_ready", "hr_stored",
            "weights1_loaded", "weights2_loaded", "weights3_loaded", "mt_loaded0", "mt_loaded1", "m_ready", "dma_asked", "dma_answered",
            "piece_in0", "piece_in1", "tp_ready", "tp_free",
            "cos_sum_ready", "cos_free", "guard_ready", "exp_ready", "masked_ready", "masked_used",
            "masked_added", "z_ready", "z_free", "out_bank_free", "osb_ready", "osb_stored",
            "rho_in0", "rho_in1", "z_loaded",
            "agg_ready", "agg_copied", "mixed_ready", "mixed_copied", "t20_ready", "split_ready", "mix_free",
            "dist_ready", "guarded_w_ready", "lnw_ready", "lnw1_ready", "expo_ready", "isq_ready", "sn_ready",
            "ln1p_ready", "artanh_ready", "factor_ready", "factor_stored0", "factor_stored1",
            "rows_in", "srow_in", "factor_in0", "factor_in1", 
            "sig_ready", "tile_weighed", "tf_ready", "c_ready", "c_used", "c_added",
            "u_ready", "u_free", "h_read", "o2_copied", "o2_stored", "o2_bank_free",
            "mask_ready", "agg3_ready", "agg3_free", "out_stored", "spilled")}

        xv = x.rearrange("(t p) f -> p t f", p=P)
        adj_v = adj.rearrange("(c k i) (q x) -> c q i k x", k=KT, i=P, x=STG * P)

        def row(v):
            return v.rearrange("(a n) -> a n", a=1)

        NQ = NT // 4
        NF = NCH * (NCH + 1) // 2
        NFP = 2 * NF

        def fin_reader(c, q, back):
            k = c * NQ + q - back
            uppers = sum(1 for i in range(k + 1) if i % NQ <= i // NQ)
            if k % NQ <= k // NQ:
                return "tile_weighed", 4 * (k + 1) + NW
            return "tf_ready", 2 * (k + 1 - uppers)

        BETA, NABS, ATTB, MU, SIG, Y2, GY, S0, T0, T1, B1C, B2C, B3C, T2, NEG1, BETAS = range(16)

        n_answers = {"scores": 7}

        block = ctx.enter_context(nc.Block())

        @block.sync
        def _(sp):
            asked = [0]

            def serve(fn, n=1):
                asked[0] += 1
                sp.wait_ge(s["dma_asked"], asked[0])
                fn().then_inc(s["dma_answered"], 16)

            sp.dma_start(A[:, :, :], xv).then_inc(s["x_loaded"], 16)
            for col, v in ((BETA, beta), (ATTB, att_b), (MU, mu), (SIG, sigma)):
                sp.dma_start(par[:, col:col + 1], v.partition_broadcast(P)).then_inc(s["par_loaded"], 16)
            for col, v, n in ((B1C, b1, F1), (B2C, b2, F1), (B3C, b3, D)):
                sp.dma_start(par[0:n, col:col + 1], v.rearrange("(n a) -> n a", a=1)).then_inc(s["par_loaded"], 16)

            rows_flat = row_d.rearrange("t p -> (t p)")

            def pieces(cc, first, qs=range(NPC)):
                for q in qs:
                    g = cc * NPC + q
                    sp.wait_ge(s["tp_ready"], g + 1)
                    sp.dma_start(stage4[q % 2], adj_v[bass.ds(cc, 1), q].rearrange("a i k x -> (a i) k x")
                                 if not first else adj_v[0, q]).then_inc(s[f"piece_in{q % 2}"], 16)

            def rho_load(c):
                if c >= 2:
                    sp.wait_ge(s["guard_ready"], (c - 1) * NP)
                sp.dma_start(rho_b[c % 2], rows_flat[c * CH:(c + 1) * CH].partition_broadcast(P))\
                    .then_inc(s[f"rho_in{c % 2}"], 16)

            def store_out(c):
                sp.wait_ge(s["osb_ready"], c + 1)
                sp.dma_start(numT_d[:, bass.ds(c * CH, CH)], osb).then_inc(s["osb_stored"], 16)

            pieces(0, True, range(2))
            serve(lambda: sp.dma_start(row_d, mid[0:NT, 0:P]))
            pieces(0, True, range(2, NPC))
            sp.wait_ge(s["dma_answered"], 16)
            rho_load(0)
            rho_load(1)
            for c in range(NCH - 1):
                pieces(c + 1, False)
                if c + 2 < NCH:
                    rho_load(c + 2)
                store_out(c)
            store_out(NCH - 1)
            sp.wait_ge(s["osb_stored"], 16 * NCH + 16)
            sp.dma_start(T[:, :], numT_d).then_inc(s["z_loaded"], 16)
            if LAYERS > 1:
                sp.wait_ge(s["z_free"], NCH + 1)
                sp.dma_start(w_small[:, 0:F1], W1).then_inc(s["weights1_loaded"], 16)
                for l, (w, f) in enumerate(((W2, F1), (W3, D))):
                    for part in range(3):
                        sp.dma_start(stack[part * F1:(part + 1) * F1, 64 + l * 64:64 + l * 64 + f], w)\
                            .then_inc(s["weights1_loaded"], 16)
            if LAYERS > 2:
                sp.dma_start(Wb, hW).then_inc(s["weights2_loaded"], 16)
                for k, (v, rows) in enumerate(((hb, hbB), (att_wl, wlB), (att_wr, wrB))):
                    sp.dma_start(rows, v.partition_broadcast(P)).then_inc(s["weights2_loaded"], 16)
                    sp.dma_start(vcols[:, k:k + 1], v.rearrange("(n a) -> n a", a=1))\
                        .then_inc(s["weights2_loaded"], 16)
                serve(lambda: sp.dma_start(x_d, A[:, :, :].rearrange("p t f -> p (t f)")))
                sp.wait_ge(s["hr_ready"], 1)
                sp.dma_start(h_d, A[:, :, :].rearrange("p t f -> p (t f)")).then_inc(s["hr_stored"], 16)
                serve(lambda: sp.dma_start(row_d, srow_sb[0:NT, :]))
                sp.wait_ge(s["dma_answered"], 16 * asked[0])
                sp.wait_ge(s["hr_stored"], 16)

                def store2(c):
                    sp.wait_ge(s["o2_copied"], c + 1)
                    sp.dma_start(numT_d[:, bass.ds(c * CH, CH)], osb2).then_inc(s["o2_stored"], 16)

                def load_srow(c):
                    sp.dma_start(srow[c % 2], rows_flat[c * CH:(c + 1) * CH].partition_broadcast(P))\
                        .then_inc(s["srow_in"], 16)

                def load_quad(c, q):
                    if (c, q) >= (0, 2):
                        who, count = fin_reader(c, q, 2)
                        sp.wait_ge(s[who], count)
                    src = f_tiles[q, c] if q <= c else f_tiles[c, q]
                    sp.dma_start(fin[q % 2].rearrange("p (j x) -> p j x", x=CH), src)\
                        .then_inc(s[f"factor_in{q % 2}"], 16)

                load_srow(0)
                n = 0
                for c in range(NCH):
                    for g in range(2 * (c + 1)):
                        if n == NFP - 2:
                            sp.wait_ge(s["dist_ready"], NFP)
                            for b in range(2):
                                sp.wait_ge(s[f"factor_stored{b}"], 16 * 2 + 16)
                            load_quad(0, 0)
                            load_quad(0, 1)
                            sp.dma_start(T[:, :], h_d).then_inc(s["rows_in"], 16)
                        sp.wait_ge(s["factor_ready"], n + 1 + NB)
                        sp.dma_start(f_pairs[g, c], fac[n % 2].rearrange("p (j x) -> p j x", x=CH))\
                            .then_inc(s[f"factor_stored{n % 2}"], 16)
                        n += 1
                for b in range(2):
                    sp.wait_ge(s[f"factor_stored{b}"], 16 * (n // 2) + 16)
                for c in range(NCH):
                    for q in range(NQ):
                        if (c, q) >= (0, 2):
                            load_quad(c, q)
                        if q == 3 and c >= 1:
                            store2(c - 1)
                        if q == 3 and c + 1 < NCH:
                            if c >= 1:
                                sp.wait_ge(s["tile_weighed"], c * NT + NW)
                            load_srow(c + 1)
                Aflat = A[:, :, :].rearrange("p t f -> p (t f)")
                sp.wait_ge(s["o2_stored"], 16 * (NCH // 2) + 16)
                sp.wait_ge(s["tile_weighed"], NCH * NT - 4 + NW)
                sp.dma_start(Aflat[:, 0:N // 2], numT_d[:, 0:N // 2]).then_inc(s["mt_loaded0"], 16)
                store2(NCH - 1)
                sp.wait_ge(s["o2_stored"], 16 * NCH + 16)
                sp.dma_start(Aflat[:, N // 2:], numT_d[:, N // 2:]).then_inc(s["mt_loaded1"], 16)
                if LAYERS > 3:
                    sp.wait_ge(s["u_free"], NCH + 1)
                    sp.dma_start(W3s, W).then_inc(s["weights3_loaded"], 16)
                    sp.dma_start(B3s, B.partition_broadcast(P)).then_inc(s["weights3_loaded"], 16)
                serve(lambda: sp.dma_start(T[:, :], x_d))
            asked[0] += 1
            sp.wait_ge(s["dma_asked"], asked[0])
            sp.dma_start(out.rearrange("(t p) f -> p t f", p=P), A[:, :, :]).then_inc(s["out_stored"], 16)
            sp.wait_ge(s["out_stored"], 16)

        @block.gpsimd
        def _(pool):
            def step(n, ins):
                ins.then_inc(s["const_ready"], 1)
                pool.wait_ge(s["const_ready"], n)

            step(1, pool.memset(ident[:, :], 0.0))
            step(2, pool.memset(not_i[:, :], 1.0))
            step(3, pool.memset(ones[:, :], 1.0))
            step(4, pool.affine_select(out=ident[:, :], in_=ident[:, :], compare_op=ALU.not_equal, fill=1.0,
                                       base=0, pattern=[[-1, P]], channel_multiplier=1))
            step(5, pool.affine_select(out=not_i[:, :], in_=not_i[:, :], compare_op=ALU.not_equal, fill=0.0,
                                       base=0, pattern=[[-1, P]], channel_multiplier=1))
            pool.tensor_copy(identb[:, :], ident[:, :]).then_inc(s["const_done"], 1)

            def add(n, buf):
                pool.wait_ge(s["masked_ready"], n + 1)
                pool.wait_ge(s["masked_added"], n + CREDIT)
                pool.tensor_tensor(acc0, acc0, ebuf[buf], ALU.add).then_inc(s["masked_added"], 1)

            def chunk(c):
                pool.wait_ge(s["z_ready"], c + 1)
                pool.wait_ge(s["masked_ready"], c * NP + 1)
                pool.tensor_tensor(acc0, ebuf[0], ones[:, 0:1].to_broadcast([P, 2 * CH]), ALU.mult).then_inc(s["masked_added"], 1)
                add(c * NP + 1, 1)

                def pairs(m):
                    add(c * NP + 2 * m, 0)
                    add(c * NP + 2 * m + 1, 1)
                loop(pool, 1, NP // 2, [], pairs)

            pool.sem_inc(s["masked_added"], CREDIT)
            loop(pool, 0, NCH, [], chunk)

            if LAYERS > 2:
                pool.wait_ge(s["hr_asked"], 1)
                pool.wait_ge(s["dma_answered"], 32)
                pool.tensor_tensor(A[:, :, :], R, S("hr").unsqueeze(2).to_broadcast([P, NT, D]), ALU.mult)\
                    .then_inc(s["hr_ready"], 1)

                def exponents(m):
                    for b in range(NB):
                        pool.wait_ge(s["lnw1_ready"], NB * m + b + 1)
                        pool.tensor_tensor(isq[b], isq[b], lnw[b], ALU.add).then_inc(s["expo_ready"], 1)
                loop(pool, 0, NFP // NB, [], exponents)

                def add2(n, buf, acc):
                    pool.wait_ge(s["c_ready"], n + 1)
                    pool.wait_ge(s["c_added"], n + NW)
                    pool.tensor_tensor(acc, acc, wbuf[buf], ALU.add).then_inc(s["c_added"], 1)

                def chunk2(c, par_):
                    acc = acc2[par_]
                    pool.wait_ge(s["u_ready"], c + 1)
                    pool.wait_ge(s["c_ready"], c * NP + 1)
                    pool.tensor_tensor(acc, wbuf[0], ones[:, 0:1].to_broadcast([P, 2 * CH]), ALU.mult)\
                        .then_inc(s["c_added"], 1)
                    for b in range(1, NW):
                        add2(c * NP + b, b, acc)

                    def pairs(m):
                        for b in range(NW):
                            add2(c * NP + NW * m + b, b, acc)
                    loop(pool, 1, NP // NW, [], pairs)

                pool.sem_inc(s["c_added"], NW)

                def two_chunks(m):
                    chunk2(2 * m, 0)
                    chunk2(2 * m + 1, 1)
                loop(pool, 0, NCH // 2, [], two_chunks)

        @block.tensor
        def _(pe):
            asked = [0]
            copies = [0]

            def ask_wait():
                asked[0] += 1
                pe.wait_ge(s["pe_asked"], asked[0])

            def transposes(src, dst=None):
                for t in range(NT):
                    last = nc.tensor.transpose(PSrow[:, t, :], src(t), ident[:, :])
                return last

            columns = [0]

            def to_columns(src):
                for t in range(NT):
                    ins = nc.tensor.transpose(PSrow[:, t, :], src(t), ident[:, :])
                    if t % (NT // 2) == NT // 2 - 1:
                        ins.then_inc(s["columns_ready"], 1)
                columns[0] += 2

            def project(w):
                for t in range(NT):
                    if t % (NT // 2) == 0:
                        pe.wait_ge(s["columns_copied"], columns[0] - 1 + t // (NT // 2))
                    ins = nc.tensor.matmul(PSrow[:, t, :], tile_T(t), w, start=True, stop=True)
                    if t % (NT // 2) == NT // 2 - 1:
                        ins.then_inc(s["proj_ready"], 1)

            def tile_T(t):
                return T[:, t * P:(t + 1) * P]

            pe.sem_inc(s["tp_ready"], CREDIT)
            pe.sem_inc(s["masked_used"], CREDIT)
            pe.sem_inc(s["z_ready"], 1)
            pe.wait_ge(s["const_done"], 1)
            ask_wait()
            nc.tensor.transpose(PS[0:NT, 7, 0:P], S("rho"), ident[:, :]).then_inc(s["pe_answered"], 1)
            ask_wait()
            pe.wait_ge(s["row_copied"], 1)
            to_columns(lambda t: TMP[:, t, :])
            pe.wait_ge(s["low_ready"], 2)

            def build(c, jp):
                tp = PS[:, 4 + jp % 2, :].bitcast(BF16).rearrange("p (j x) -> p j x", j=2)
                pe.wait_ge(s[f"piece_in{jp % 2}"], 16 * (c * (NPC // 2) + jp // 2 + 1))
                pe.wait_ge(s["tp_free"], c * NP + jp + 1)
                for jj in range(2):
                    for k in range(KT):
                        last = nc.tensor.transpose(tp[:, jj, k * P:(k + 1) * P],
                                                   stage_hi[jp % 2][:, k, jj * P:(jj + 1) * P, 1],
                                                   identb[:, :])
                last.then_inc(s["tp_ready"], 1)

            def cosines(c, jp):
                n = c * NP + jp
                pe.wait_ge(s["cos_free"], n + 1)
                for jj in range(2):
                    J = 2 * jp + jj
                    for k, (a, b) in enumerate(((hi, hi), (hi, lo), (lo, hi))):
                        last = nc.tensor.matmul(PS[:, 2 * (jp % 2) + jj, :], a[:, J * P:(J + 1) * P],
                                                b[:, bass.ds(c * CH, CH)], start=(k == 0), stop=(k == 2))
                last.then_inc(s["cos_sum_ready"], 1)

            def chunk0(c, more):
                for jp in range(NP):
                    if jp + 2 < NP:
                        cosines(c, jp + 2)
                    elif more:
                        cosines(c + 1, jp + 2 - NP)
                    if jp == 0:
                        pe.wait_ge(s["out_bank_free"], c + 1)
                    pe.wait_ge(s["masked_ready"], c * NP + jp + 1)
                    for jj in range(2):
                        J = 2 * jp + jj
                        last = nc.tensor.matmul(PS[:, 6, :], A[:, J, :], ebuf[jp % 2][:, jj * CH:(jj + 1) * CH],
                                                start=(J == 0), stop=(J == NT - 1))
                    last.then_inc(s["masked_used"], 1)
                    if more:
                        build(c + 1, jp)
                pe.wait_ge(s["masked_added"], (c + 1) * NP + CREDIT)
                pe.wait_ge(s["z_free"], c + 1)
                for k in range(KT):
                    for half in range(2):
                        last = nc.tensor.matmul(PS[:, 7, k:k + 1], acc0[:, half * CH + k * P:half * CH + (k + 1) * P],
                                                ones[:, 0:1], start=(half == 0), stop=(half == 1))
                last.then_inc(s["z_ready"], 1)

            for jp in range(NP):
                build(0, jp)
            cosines(0, 0)
            cosines(0, 1)
            with pe.Fori(0, NCH - 1) as c:
                chunk0(c, True)
            chunk0(NCH - 1, False)

            ask_wait()
            for t in range(NT):
                last = nc.tensor.matmul(PS[:, 0, 0:P], ones[:, :], A[:, t, :], start=(t == 0), stop=(t == NT - 1))
            last.then_inc(s["pe_answered"], 1)
            ask_wait()
            pe.wait_ge(s["z_loaded"], 16)
            transposes(tile_T).then_inc(s["pe_answered"], 1)

            if LAYERS > 1:
                ask_wait()
                to_columns(lambda t: A[:, t, :])
                pe.wait_ge(s["weights1_loaded"], 16 * 7)
                for t in range(NT):
                    if t % (NT // 2) == 0:
                        pe.wait_ge(s["columns_copied"], columns[0] - 1 + t // (NT // 2))
                    last = nc.tensor.matmul(PS[:, t // 4, (t % 4) * F1:(t % 4 + 1) * F1], tile_T(t), w_small[:, 0:F1],
                                            start=True, stop=True)
                last.then_inc(s["pe_answered"], 1)
                pe.sem_inc(s["t20_ready"], CREDIT)
                for l in range(3):
                    F = D if l == 2 else F1
                    wl = stack[0:3 * F1, (0, 64, 128)[l]:(0, 64, 128)[l] + F]
                    hs = hs1[l % 2]

                    def agg(c, half):
                        pe.wait_ge(s["agg_copied"], l * NCH + c + 1)
                        for J in range(NT):
                            last = nc.tensor.matmul(PS[0:3 * F1, half, :], hs[:, J, :],
                                                    adjT[:, J, c * CH:(c + 1) * CH],
                                                    start=(J == 0), stop=(J == NT - 1))
                        last.then_inc(s["agg_ready"], 1)

                    def mix(c, half):
                        pe.wait_ge(s["agg_copied"], l * NCH + c + 1 + CREDIT)
                        pe.wait_ge(s["mixed_copied"], l * NCH + c + 1)
                        nc.tensor.matmul(PS[0:F, 2 + half, :], wl, agg_sb[half][0:3 * F1, :],
                                         start=True, stop=True).then_inc(s["mixed_ready"], 1)

                    def to_rows(c, half):
                        if l == 2:
                            return
                        pe.wait_ge(s["mixed_copied"], l * NCH + c + 1 + CREDIT)
                        pe.wait_ge(s["split_ready"], l * NCH + c + 1)
                        for k in range(KT):
                            last = nc.tensor.transpose(PS[:, 4 + half, k * F1:(k + 1) * F1],
                                                       h_sb[half][0:F1, k * P:(k + 1) * P], ident[0:F1, 0:F1])
                        last.then_inc(s["t20_ready"], 1)

                    pe.wait_ge(s["split_ready"], CREDIT + l * NCH)
                    agg(0, 0)
                    for c in range(1, NCH):
                        agg(c, c % 2)
                        if c >= 2:
                            to_rows(c - 2, c % 2)
                        mix(c - 1, (c - 1) % 2)
                    to_rows(NCH - 2, 0)
                    mix(NCH - 1, 1)
                    to_rows(NCH - 1, 1)
                ask_wait()
                transposes(tile_T).then_inc(s["pe_answered"], 1)

            if LAYERS > 2:
                ask_wait()
                nc.tensor.transpose(PS[:, 0, 0:P], Wb, ident[:, :])
                nc.tensor.matmul(PS[:, 1, 0:3], Wb, vcols, start=True, stop=True).then_inc(s["pe_answered"], 1)
                ask_wait()
                to_columns(lambda t: A[:, t, :])
                project(WT)
                pe.wait_ge(s["proj_copied"], 1)
                for t in range(NT):
                    last = nc.tensor.matmul(PS[:, 0, 3 * t:3 * t + 3], tile_T(t), wv, start=True, stop=True)
                last.then_inc(s["extra_ready"], 1)
                ask_wait()
                pe.wait_ge(s["proj_copied"], 2)
                to_columns(lambda t: TMP[:, t, :])
                ask_wait()
                pe.wait_ge(s["columns_copied"], columns[0])
                nc.tensor.transpose(PS[0:NT, 7, 0:P], S("sc_i"), ident[:, :]).then_inc(s["pe_answered"], 1)
                ask_wait()
                pe.wait_ge(s["row_copied"], 2)
                for aug in range(2):
                    for t in range(NT):
                        last = nc.tensor.transpose(aug_ps(aug)[:, t * P:(t + 1) * P],
                                                   augrows[aug][:, t, :], identb[:, :])
                    last.then_inc(s["pe_answered"], 1)
                pe.wait_ge(s["aug_copied"], 2)
                n = 0
                for c in range(NCH):
                    for g in range(2 * (c + 1)):
                        if n >= NB:
                            pe.wait_ge(s["artanh_ready"], n - NB + 1)
                        for jj in range(2):
                            J = 2 * g + jj
                            o = PS[:, 2 * (n % NB) + jj, :]
                            nc.tensor.matmul(o, T[:, J * P:(J + 1) * P], T[:, c * CH:(c + 1) * CH],
                                             start=True, stop=False)
                            last = nc.tensor.matmul(o, augS[0:AUG, J * P:(J + 1) * P], augM[0:AUG, c * CH:(c + 1) * CH],
                                                    start=False, stop=True)
                        last.then_inc(s["dist_ready"], 1)
                        n += 1

                pe.sem_inc(s["c_used"], NW)
                pe.sem_inc(s["u_ready"], 2)
                low = []

                def mirror(c, jp):
                    q, half = jp // 2, jp % 2
                    if half == 0:
                        pe.wait_ge(s[f"factor_in{q % 2}"], 16 * (c * NQ // 2 + q // 2 + 1))
                    if len(low) >= 2:
                        pe.wait_ge(s["tile_weighed"], 2 * low[-2] + 2 + NW)
                    for jj in range(2):
                        for k in range(KT):
                            last = nc.tensor.transpose(
                                PS[:, 2 * (jp % 2) + jj, k * P:(k + 1) * P],
                                fin[q % 2][:, k * CH + (2 * half + jj) * P:k * CH + (2 * half + jj + 1) * P],
                                ident[:, :])
                    last.then_inc(s["tf_ready"], 1)
                    low.append(c * NP + jp)

                def u_sums(c):
                    pe.wait_ge(s["c_added"], (c + 1) * NP + NW)
                    pe.wait_ge(s["u_free"], c + 1)
                    for k in range(KT):
                        for half in range(2):
                            last = nc.tensor.matmul(PS[:, 7, k:k + 1],
                                                    acc2[c % 2][:, half * CH + k * P:half * CH + (k + 1) * P],
                                                    ones[:, 0:1], start=(half == 0), stop=(half == 1))
                    last.then_inc(s["u_ready"], 1)

                pe.wait_ge(s["rows_in"], 16)
                pe.wait_ge(s["artanh_ready"], NFP)
                for c in range(NCH):
                    for jp in range(NP):
                        if jp % 2 == 0 and jp + 2 < NP and (jp + 2) // 2 > c:
                            mirror(c, jp + 2)
                            mirror(c, jp + 3)
                        if jp == 0:
                            pe.wait_ge(s["o2_bank_free"], c + 1)
                        pe.wait_ge(s["c_ready"], c * NP + jp + 1)
                        for jj in range(2):
                            J = 2 * jp + jj
                            last = nc.tensor.matmul(PS[:, 5 + c % 2, :], Trow[:, J, :],
                                                    wbuf[jp % NW][:, jj * CH:(jj + 1) * CH],
                                                    start=(J == 0), stop=(J == NT - 1))
                        last.then_inc(s["c_used"], 1)
                        if c >= 1 and jp == 2:
                            u_sums(c - 1)
                u_sums(NCH - 1)
                pe.wait_ge(s["tile_weighed"], NCH * NT + NW)
                pe.wait_ge(s["o2_copied"], NCH)
                pe.wait_ge(s["u_free"], NCH + 1)
                for t in range(NT):
                    if t % (NT // 2) == 0:
                        pe.wait_ge(s[f"mt_loaded{t // (NT // 2)}"], 16)
                    ins = nc.tensor.transpose(PSrow[:, t, :], A[:, t, :], ident[:, :])
                    if t % (NT // 2) == NT // 2 - 1:
                        ins.then_inc(s["m_ready"], 1)

            if LAYERS > 3:
                ask_wait()
                nc.tensor.matmul(PS[:, 0, 0:P], ones[:, :], absw, start=True, stop=True).then_inc(s["pe_answered"], 1)
                ask_wait()
                nc.tensor.transpose(PS[:, 1, 0:P], hscale, ident[:, :]).then_inc(s["pe_answered"], 1)
                ask_wait()
                to_columns(lambda t: A[:, t, :])
                project(W3s)
                pe.wait_ge(s["mask_ready"], 1)
                pe.wait_ge(s["agg3_free"], 1)
                for g in range(NCH):
                    pe.wait_ge(s["part_ready"], g + 1)
                    for part in range(2):
                        for J in range(g * KT, (g + 1) * KT):
                            last = nc.tensor.matmul(PS[:, 0, :], hs3[part][:, J, :], adjT[:, J, 0:CH],
                                                    start=(J == 0 and part == 0), stop=(J == NT - 1 and part == 1))
                last.then_inc(s["agg3_ready"], 1)

                def agg3(c, half):
                    pe.wait_ge(s["agg3_free"], c + 1)
                    pe.wait_ge(s["mask_ready"], c + 1)
                    for part in range(2):
                        for J in range(NT):
                            last = nc.tensor.matmul(PS[:, half, :], hs3[part][:, J, :],
                                                    adjT[:, J, c * CH:(c + 1) * CH],
                                                    start=(J == 0 and part == 0), stop=(J == NT - 1 and part == 1))
                    last.then_inc(s["agg3_ready"], 1)

                for c in range(1, NCH):
                    agg3(c, c % 2)
                ask_wait()
                transposes(tile_T).then_inc(s["pe_answered"], 1)

        @block.scalar
        def _(act):
            asked = [0]
            steps = Chain(act, s["act_step"])

            def fn(out_, in_, func, **kw):
                asked[0] += 1
                act.wait_ge(s["act_asked"], asked[0])
                nc.scalar.activation(out_, in_, func, **kw).then_inc(s["act_answered"], 1)

            def share(make):
                asked[0] += 1
                act.wait_ge(s["act_asked"], asked[0])
                for t in range(DT, NT):
                    last = make(t)
                last.then_inc(s["act_answered"], 1)

            def col(name, t):
                return S(name)[:, t:t + 1]

            def squares(name, src):
                share(lambda t: nc.scalar.activation(TMP[:, t, :], src[:, t, :], ACT.Square,
                                                     accum_out=col(name, t)))

            def scaled(dst, src, name):
                share(lambda t: nc.scalar.activation(dst[:, t, :], src[:, t, :], ACT.Copy, scale=col(name, t)))

            def normalise():
                share(lambda t: nc.scalar.activation(A[:, t, :], R[:, t, :], ACT.Identity,
                                                     scale=col("rstd", t), bias=col("shift", t)))

            halves = [0]

            def columns_copy():
                for h in range(2):
                    halves[0] += 1
                    act.wait_ge(s["columns_ready"], halves[0])
                    nc.scalar.copy(T[:, h * (N // 2):(h + 1) * (N // 2)],
                                   PS[:, 4 * h:4 * h + 4, :].rearrange("p b f -> p (b f)"))\
                        .then_inc(s["columns_copied"], 1)

            def sqrt(name):
                fn(S("y0"), S(name), ACT.Sqrt)

            sqrt("ss")
            act.wait_ge(s["pe_answered"], 1)
            nc.scalar.copy(mid[0:NT, 0:P], PS[0:NT, 7, 0:P]).then_inc(s["row_copied"], 1)
            for h in range(2):
                halves[0] += 1
                act.wait_ge(s["columns_ready"], halves[0])
                nc.scalar.activation(hi[:, h * (N // 2):(h + 1) * (N // 2)],
                                     PS[:, 4 * h:4 * h + 4, :].rearrange("p b f -> p (b f)"), ACT.Copy, scale=XS)\
                    .then_inc(s["columns_copied"], 1)

            def guard_ln(n, cp, jp, b):
                if not (isinstance(n, int) and n < NR):
                    act.wait_ge(s["exp_ready"], n + 1 - NR + CREDIT)
                for jj in range(2):
                    nc.scalar.activation(rbuf[b][:, jj * CH:(jj + 1) * CH], rho_b[cp], ACT.Ln,
                                         scale=S("erho")[:, bass.ds(2 * jp + jj, 1)], bias=1.0)\
                        .then_inc(s["ln_ready"], 1)

            def guard_exp(n, b):
                act.wait_ge(s["ln_ready"], 2 * n + 2)
                nc.scalar.activation(rbuf[b], rbuf[b], ACT.Exp, scale=-1.0).then_inc(s["guard_ready"], 1)

            def exps(n, b):
                act.wait_ge(s["cos_free"], n + 1 + CREDIT)
                act.wait_ge(s["masked_used"], n + 1)
                act.wait_ge(s["masked_added"], n + 1)
                nc.scalar.activation(ebuf[b % 2], rbuf[b], ACT.Exp, scale=par[:, BETAS:BETAS + 1],
                                     bias=par[:, NABS:NABS + 1]).then_inc(s["exp_ready"], 1)

            def copy_out(c):
                act.wait_ge(s["masked_used"], (c + 1) * NP + CREDIT)
                act.wait_ge(s["osb_stored"], 16 * c + 16)
                nc.scalar.copy(osb, PS[:, 6, :]).then_inc(s["osb_ready"], 1)
                act.wait_ge(s["osb_ready"], c + 1)
                act.sem_inc(s["out_bank_free"], 1)

            def chunk0(k, cp, first=False, last=False):
                c = 2 * k + cp

                def turn(jp, b):
                    n = c * NP + jp
                    exps(n, b)
                    peeled = isinstance(jp, int)
                    if not (last and peeled and jp + 2 >= NP):
                        guard_exp(n + 2, (b + 2) % NR)
                    if not (peeled and jp + 3 >= NP):
                        guard_ln(n + 3, cp, jp + 3, (b + 3) % NR)
                    elif not last:
                        if jp + 3 == NP:
                            act.wait_ge(s[f"rho_in{1 - cp}"], 16 * (k + 1 + cp))
                        guard_ln(n + 3, 1 - cp, jp + 3 - NP, (b + 3) % NR)

                for b in range(NR):
                    turn(b, b)
                    if b == 0 and not first:
                        copy_out(c - 1)

                def turns(m):
                    for b in range(NR):
                        turn(NR * m + b, b)
                loop(act, 1, NP // NR - 1, [], turns)
                for b in range(NR):
                    turn(NP - NR + b, b)

            act.sem_inc(s["out_bank_free"], 1)
            act.sem_inc(s["osb_stored"], 16)
            act.sem_inc(s["exp_ready"], CREDIT)
            act.wait_ge(s["const_done"], 1)
            nc.scalar.preload_act_table_set("natural_log_exp_and_others")
            act.wait_ge(s["rho_in0"], 16)
            for n in range(2):
                guard_ln(n, 0, n, n)
                guard_exp(n, n)
            guard_ln(2, 0, 2, 2)
            chunk0(0, 0, first=True)
            chunk0(0, 1)
            with act.Fori(1, NCH // 2 - 1) as k:
                chunk0(k, 0)
                chunk0(k, 1)
            chunk0(NCH // 2 - 1, 0)
            chunk0(NCH // 2 - 1, 1, last=True)
            copy_out(NCH - 1)
            sqrt("var")
            normalise()
            if LAYERS > 1:
                columns_copy()
                act.sem_inc(s["agg_copied"], CREDIT)
                act.sem_inc(s["mixed_copied"], CREDIT)
                for l in range(3):
                    if l == 2 and LAYERS > 2:
                        sqrt("ss")
                        fn(S("y2"), S("y1"), ACT.Tanh)
                    F = D if l == 2 else F1
                    bias = par[0:F, (B1C, B2C, B3C)[l]:(B1C, B2C, B3C)[l] + 1]

                    def agg_copy(c, half):
                        act.wait_ge(s["agg_ready"], l * NCH + c + 1)
                        nc.scalar.copy(agg_sb[half][0:3 * F1, :], PS[0:3 * F1, half, :])\
                            .then_inc(s["agg_copied"], 1)

                    def relu(c, half):
                        act.wait_ge(s["mixed_ready"], l * NCH + c + 1)
                        if l < 2:
                            act.wait_ge(s["t20_ready"], l * NCH + c + 1)
                            dst = h_sb[half][0:F, :]
                        else:
                            dst = T[:, bass.ds(c * CH, CH)]
                        nc.scalar.activation(dst, PS[0:F, 2 + half, :], ACT.Relu, bias=bias)\
                            .then_inc(s["mixed_copied"], 1)

                    agg_copy(0, 0)
                    with act.Fori(0, NCH // 2 - 1) as m:
                        agg_copy(2 * m + 1, 1)
                        relu(2 * m, 0)
                        agg_copy(2 * m + 2, 0)
                        relu(2 * m + 1, 1)
                    agg_copy(NCH - 1, 1)
                    relu(NCH - 2, 0)
                    relu(NCH - 1, 1)
                sqrt("var")
                normalise()
            if LAYERS > 2:
                columns_copy()
                sqrt("ss")
                fn(S("y1"), S("y0"), ACT.Ln, bias=1.0)
                fn(S("y2"), S("y0"), ACT.Ln, scale=-1.0, bias=1.0)
                for h in range(2):
                    act.wait_ge(s["proj_ready"], h + 1)
                    nc.scalar.copy(R[:, 16 * h:16 * (h + 1), :], PSrow[:, 16 * h:16 * (h + 1), :])\
                        .then_inc(s["proj_copied"], 1)
                sqrt("ss")
                fn(S("y0"), S("y1"), ACT.Tanh)
                scaled(R, R, "c1")
                squares("ss", R)
                sqrt("ss")
                fn(S("y1"), S("y0"), ACT.Ln, bias=1.0)
                fn(S("y2"), S("y0"), ACT.Ln, scale=-1.0, bias=1.0)
                squares("x2", R)
                columns_copy()
                act.wait_ge(s["pe_answered"], n_answers["scores"])
                nc.scalar.copy(srow_sb[0:NT, :], PS[0:NT, 7, 0:P]).then_inc(s["row_copied"], 1)
                act.wait_ge(s["hr_stored"], 16)
                act.wait_ge(s["pe_answered"], n_answers["scores"] + 1)
                nc.scalar.copy(augS[0:AUG, :], aug_ps(0)).then_inc(s["aug_copied"], 1)

                def ln_w(n, b):
                    act.wait_ge(s["guarded_w_ready"], n + 1)
                    act.wait_ge(s["factor_ready"], n + 1)
                    nc.scalar.activation(lnw[b], wh[b], ACT.Ln, scale=-2.0).then_inc(s["lnw_ready"], 1)

                def ln_w1(n, b):
                    nc.scalar.activation(isq[b], wh[b], ACT.Ln, scale=-2.0, bias=par[:, NEG1:NEG1 + 1])\
                        .then_inc(s["lnw1_ready"], 1)

                def inverse_root(n, b):
                    act.wait_ge(s["expo_ready"], n + 1)
                    nc.scalar.activation(isq[b], isq[b], ACT.Exp, scale=-0.5).then_inc(s["isq_ready"], 1)

                def ln_1p(n, b):
                    act.wait_ge(s["sn_ready"], n + 1)
                    nc.scalar.activation(wh[b], wh[b], ACT.Ln, scale=-2.0, bias=1.0).then_inc(s["ln1p_ready"], 1)

                def turn(n, b, ahead=2):
                    if ahead == 2:
                        ln_w(n + 2, (b + 2) % NB)
                    ln_1p(n, b)
                    if ahead == 2:
                        ln_w1(n + 2, (b + 2) % NB)
                    if ahead >= 1:
                        inverse_root(n + 1, (b + 1) % NB)

                act.sem_inc(s["o2_stored"], 16)
                act.sem_inc(s["o2_bank_free"], 2)
                nc.scalar.preload_act_table_set("natural_log_exp_and_others")
                for n in range(2):
                    ln_w(n, n)
                    ln_w1(n, n)
                inverse_root(0, 0)

                def turns(m):
                    for b in range(NB):
                        turn(NB * m + b, b)
                loop(act, 0, NFP // NB - 1, [], turns)
                for b in range(NB):
                    turn(NFP - NB + b, b, min(2, NB - 1 - b))

                def sigmoids(c, m):
                    for b in range(NW):
                        J = NW * m + b
                        act.wait_ge(s["tile_weighed"], c * NT + J + 1)
                        nc.scalar.activation(sig[b], srow[c % 2], ACT.Sigmoid,
                                             bias=S("sc_j")[:, bass.ds(J, 1)]).then_inc(s["sig_ready"], 1)

                def copy2(c):
                    act.wait_ge(s["c_used"], (c + 1) * NP + NW)
                    act.wait_ge(s["o2_stored"], 16 * c + 16)
                    nc.scalar.copy(osb2, PS[:, 5 + c % 2, :]).then_inc(s["o2_copied"], 1)
                    act.wait_ge(s["o2_copied"], c + 1)
                    act.sem_inc(s["o2_bank_free"], 1)

                nc.scalar.preload_act_table_set("sigmoid_and_others")
                act.wait_ge(s["factor_ready"], NFP + NB)
                for c in range(NCH):
                    act.wait_ge(s["srow_in"], 16 * (c + 1))
                    sigmoids(c, 0)
                    sigmoids(c, 1)
                    if c >= 1:
                        copy2(c - 1)
                    with act.Fori(2, NT // NW) as m:
                        sigmoids(c, m)
                copy2(NCH - 1)
                scaled(A, Trow, "g")
                squares("ss", A)
                sqrt("ss")
                fn(S("y0"), S("y1"), ACT.Tanh)
                scaled(R, Trow, "c1")
                squares("ss", R)
                sqrt("ss")
                fn(S("y1"), S("y0"), ACT.Ln, bias=1.0)
                fn(S("y2"), S("y0"), ACT.Ln, scale=-1.0, bias=1.0)
                squares("ss", R)
                sqrt("ss")
                fn(S("y0"), S("y1"), ACT.Tanh)
                sqrt("var")
                normalise()
            if LAYERS > 3:
                columns_copy()
                fn(par[:, T1:T1 + 1], par[:, T0:T0 + 1], ACT.Square)
                fn(par[:, S0:S0 + 1], par[:, T2:T2 + 1], ACT.Exp)

                def out3(c, half):
                    act.wait_ge(s["agg3_ready"], c + 1)
                    nc.scalar.activation(T[:, bass.ds(c * CH, CH)], PS[:, half, :], ACT.Copy, scale=hscale_c)\
                        .then_inc(s["agg3_free"], 1)

                act.sem_inc(s["agg3_free"], CREDIT)
                with act.Fori(0, NCH // 2) as m:
                    out3(2 * m, 0)
                    out3(2 * m + 1, 1)
                sqrt("var")
                normalise()

        @block.vector
        def _(dve):
            steps = Chain(dve, s["dve_step"])
            link = steps.link
            V = nc.vector
            n_act, n_pe, n_dma = [0], [0], [0]

            def bc(sc):
                return sc.unsqueeze(2).to_broadcast([P, NT, D])

            def bf(v):
                return v.unsqueeze(1).to_broadcast([P, NT, D])

            def act_do():
                n_act[0] += 1
                dve.sem_inc(s["act_asked"], 1)
                dve.wait_ge(s["act_answered"], n_act[0])

            def pe_ask():
                dve.sem_inc(s["pe_asked"], 1)

            def pe_answer():
                n_pe[0] += 1
                dve.wait_ge(s["pe_answered"], n_pe[0])

            def pe_do():
                pe_ask()
                pe_answer()

            def dma_do(wait=True):
                n_dma[0] += 1
                dve.sem_inc(s["dma_asked"], 1)
                if wait:
                    dve.wait_ge(s["dma_answered"], 16 * n_dma[0])

            def tt(o, a, b, op):
                link(V.tensor_tensor(o, a, b, op))

            def ts(o, a, s1, op0, s2=None, op1=ALU.bypass):
                link(V.tensor_scalar(o, a, s1, s2, op0, op1))

            def stt(o, a, sc, b, op0, op1):
                link(V.scalar_tensor_tensor(out=o, in0=a, scalar=sc, in1=b, op0=op0, op1=op1))

            def rec(o, a):
                link(V.reciprocal(o, a))

            def col(name, t):
                return S(name)[:, t:t + 1]

            def dots(name, a, b, n=NT, waits=None, scratch=TMP):
                for t in range(n):
                    if waits is not None and t % (NT // 2) == 0:
                        dve.wait_ge(waits, t // (NT // 2) + 1)
                    ins = V.tensor_tensor_reduce(scratch[:, t, :], a(t), b(t), 1.0, 0.0, ALU.mult, ALU.add,
                                                 accum_out=col(name, t))
                link(ins)

            def act_join():
                n_act[0] += 1
                dve.wait_ge(s["act_answered"], n_act[0])

            def squares(name, src, first=None):
                dve.sem_inc(s["act_asked"], 1)
                if first is not None:
                    first()
                dots(name, lambda t: src[:, t, :], lambda t: src[:, t, :], DT)
                act_join()

            def scaled(dst, src, name):
                dve.sem_inc(s["act_asked"], 1)
                tt(dst[:, 0:DT, :], src[:, 0:DT, :], S(name)[:, 0:DT].unsqueeze(2).to_broadcast([P, DT, D]), ALU.mult)
                act_join()

            def by_tiles(dst, a, name, b, n=NT):
                for t in range(n):
                    ins = V.scalar_tensor_tensor(out=dst(t), in0=a(t), scalar=col(name, t), in1=b(t),
                                                 op0=ALU.mult, op1=ALU.add)
                link(ins)

            def tiles(m):
                return lambda t: m[:, t, :]

            def sqrt(dst, name):
                act_do()
                rec(S("y1"), S("y0"))
                tt(S("y1"), S("y1"), S(name), ALU.mult)
                tt(S("y0"), S("y0"), S("y1"), ALU.add)
                ts(dst, S("y0"), 0.5, ALU.mult)

            def layer_norm():
                st = TMP.rearrange("p t f -> p (t f)")[:, 0:6 * NT].rearrange("p (t k) -> p t k", k=6)
                for t in range(NT):
                    ins = V.bn_stats(st[:, t, :], R[:, t, :])
                link(ins)
                tt(S("mean"), st[:, :, 1], st[:, :, 4], ALU.add)
                ts(S("mean"), S("mean"), 0.5, ALU.mult)
                tt(S("y1"), st[:, :, 1], S("mean"), ALU.subtract)
                tt(S("y1"), S("y1"), S("y1"), ALU.mult)
                tt(S("var"), st[:, :, 2], st[:, :, 5], ALU.add)
                stt(S("var"), S("var"), 1.0 / D, S("y1"), ALU.mult, ALU.add)
                ts(S("var"), S("var"), LN_EPS, ALU.add)
                sqrt(S("rstd"), "var")
                rec(S("rstd"), S("rstd"))
                stt(S("shift"), S("mean"), -1.0, S("rstd"), ALU.mult, ALU.mult)
                dve.sem_inc(s["act_asked"], 1)
                for t in range(DT):
                    ins = V.tensor_scalar(A[:, t, :], R[:, t, :], col("rstd", t), col("shift", t), ALU.mult, ALU.add)
                link(ins)
                act_join()

            def split3(dst, src, rest):
                link(V.tensor_copy(dst[0], src))
                tt(rest, src, dst[0], ALU.subtract)
                link(V.tensor_copy(dst[1], rest))
                tt(rest, rest, dst[1], ALU.subtract)
                link(V.tensor_copy(dst[2], rest))

            dve.wait_ge(s["x_loaded"], 16)
            dots("ss", tiles(A), tiles(A))
            ts(S("ss"), S("ss"), TINY_NORM ** 2, ALU.max)
            sqrt(S("rho"), "ss")
            rec(S("rho"), S("rho"))
            ts(S("erho"), S("rho"), COS_EPS, ALU.mult)
            tt(TMP, A[:, :, :], bc(S("rho")), ALU.mult)
            dve.wait_ge(s["par_loaded"], 16 * 7)
            ts(par[:, T0:T0 + 1], par[:, BETA:BETA + 1], -1.0, ALU.mult)
            tt(par[:, NABS:NABS + 1], par[:, T0:T0 + 1], par[:, BETA:BETA + 1], ALU.min)
            ts(par[:, BETAS:BETAS + 1], par[:, BETA:BETA + 1], 1.0 / (XS * XS), ALU.mult)
            dve.wait_ge(s["const_done"], 1)
            pe_do()
            dve.wait_ge(s["row_copied"], 1)
            dma_do(False)
            pe_ask()
            for h in range(2):
                dve.wait_ge(s["columns_copied"], h + 1)
                cols = slice(h * (N // 2), (h + 1) * (N // 2))
                V.scalar_tensor_tensor(out=lo[:, cols], in0=PS[:, 4 * h:4 * h + 4, :].rearrange("p b f -> p (b f)"),
                                       scalar=XS, in1=hi[:, cols], op0=ALU.mult, op1=ALU.subtract)\
                    .then_inc(s["low_ready"], 1)

            def evacuate(c, jp, par_):
                n = c * NP + jp
                dve.wait_ge(s["tp_ready"], n + 1 + CREDIT)
                V.tensor_scalar(adjU[:, bass.ds(2 * jp, 2), bass.ds(c * CH, CH)],
                                PS[:, 4 + par_, :].bitcast(BF16).rearrange("p (j x) -> p j x", j=2),
                                EDGE8, None, ALU.mult).then_inc(s["tp_free"], 1)

            def product(c, jp, b):
                n = c * NP + jp
                dve.wait_ge(s["cos_sum_ready"], n + 1)
                dve.wait_ge(s["guard_ready"], n + 1)
                V.tensor_tensor(rbuf[b], PS[:, 2 * (b % 2):2 * (b % 2) + 2, :].rearrange("p b f -> p (b f)"),
                                rbuf[b], ALU.mult).then_inc(s["cos_free"], 1)

            def mask(c, jp, par_):
                dve.wait_ge(s["exp_ready"], c * NP + jp + 1 + CREDIT)
                e = ebuf[par_].rearrange("p (j x) -> p j x", j=2)
                V.tensor_tensor(e, e, adjU[:, bass.ds(2 * jp, 2), bass.ds(c * CH, CH)], ALU.mult)\
                    .then_inc(s["masked_ready"], 1)

            def take_z(c):
                dve.wait_ge(s["z_ready"], c + 2)
                V.tensor_copy(S("z")[:, bass.ds(c * KT, KT)], PS[:, 7, 0:KT]).then_inc(s["z_free"], 1)

            def chunk0(c, first=False, last=False):
                dve.wait_ge(s["tp_free"], (c + 1) * NP - 1 + CREDIT)

                def turn(jp, b, evac=True, ahead=True):
                    if ahead:
                        product(c, jp + 1, (b + 1) % NR)
                    mask(c, jp, b % 2)
                    if not last and evac:
                        evacuate(c + 1, jp - 1, 1 - b % 2)

                turn(0, 0, False)
                if not first:
                    evacuate(c, NP - 1, 1)
                turn(1, 1)
                if not first:
                    dve.wait_ge(s["tp_free"], (c + 1) * NP + CREDIT)
                    take_z(c - 1)
                turn(2, 2)
                turn(3, 3)

                def turns(m):
                    for b in range(NR):
                        turn(NR * m + b, b)
                loop(dve, 1, NP // NR - 1, [], turns)
                for b in range(NR):
                    turn(NP - NR + b, b, ahead=not (last and b == NR - 1))

            dve.sem_inc(s["tp_free"], CREDIT)
            dve.sem_inc(s["cos_free"], CREDIT)
            dve.sem_inc(s["z_free"], 1)
            with dve.Fori(0, NP // 2) as m:
                for h in range(2):
                    evacuate(0, 2 * m + h, h)
            product(0, 0, 0)
            chunk0(0, first=True)
            with dve.Fori(1, NCH - 1) as c:
                chunk0(c)
            chunk0(NCH - 1, last=True)
            take_z(NCH - 1)
            dve.wait_ge(s["z_free"], NCH + 1)
            pe_do()
            ts(csum, PS[:, 0, 0:P], EDGE8 * NO_NEIGHBOUR, ALU.mult)
            pe_do()
            ts(S("z"), S("z"), EDGE8 * NO_NEIGHBOUR * N, ALU.add)
            rec(S("z"), S("z"))
            tt(R, PSrow, bf(csum), ALU.add)
            by_tiles(tiles(R), tiles(R), "z", tiles(A))
            layer_norm()

            def clip_norm(dst, name):
                ts(S(name), S(name), EPS * EPS, ALU.max)
                sqrt(dst, name)

            def radius(dst, n):
                rec(dst, n)
                ts(dst, dst, MAXNORM, ALU.mult, 1.0, ALU.min)

            def artanh(dst, n):
                ts(S("y0"), n, ATANH_MAX, ALU.min)
                act_do()
                act_do()
                tt(S("y1"), S("y1"), S("y2"), ALU.subtract)
                ts(dst, S("y1"), 0.5, ALU.mult)

            def add_weights(x2, xy, y2, c1, c2):
                tt(S("y1"), x2, y2, ALU.mult)
                stt(S("y1"), xy, 2.0, S("y1"), ALU.mult, ALU.add)
                ts(S("y1"), S("y1"), 1.0, ALU.add, EPS, ALU.max)
                rec(S("y1"), S("y1"))
                stt(S("y2"), xy, 2.0, y2, ALU.mult, ALU.add)
                stt(c1, S("y2"), 1.0, S("y1"), ALU.add, ALU.mult)
                ts(S("y2"), x2, -1.0, ALU.mult, 1.0, ALU.add)
                tt(c2, S("y2"), S("y1"), ALU.mult)

            def bias_point():
                dve.wait_ge(s["weights2_loaded"], 16 * 7)
                link(V.memset(par[:, NEG1:NEG1 + 1], -1.0))
                for k, (c_, v) in enumerate(((T0, hbB), (T1, wlB), (T2, wrB))):
                    ins = V.tensor_tensor_reduce(TMP[:, k, :], hbB, v, 1.0, 0.0, ALU.mult, ALU.add,
                                                 accum_out=par[:, c_:c_ + 1])
                link(ins)
                tt(S("ss"), par[:, T0:T0 + 1].to_broadcast([P, NT]), par[:, T0:T0 + 1].to_broadcast([P, NT]), ALU.max)
                clip_norm(S("nb"), "ss")
                link(V.tensor_copy(S("y1"), S("nb")))
                act_do()
                ts(S("n"), S("y2"), EPS, ALU.max)
                radius(S("f"), S("n"))
                tt(S("n"), S("n"), S("f"), ALU.mult)
                rec(S("gb"), S("nb"))
                tt(S("gb"), S("gb"), S("n"), ALU.mult)
                tt(S("yy"), S("n"), S("n"), ALU.mult)

            if LAYERS > 1:
                pe_ask()
                pe_answer()
                v = PS[:, :, 0:4 * F1].rearrange("p b (k f) -> p b k f", f=F1)
                rest = TMP.rearrange("p t f -> p (t f)")[:, 0:NT * F1].rearrange("p (b k f) -> p b k f", k=4, f=F1)
                hv = hs1[0].rearrange("p (b k) f -> p b k f", k=4)
                split3([hv[:, :, :, q * F1:(q + 1) * F1] for q in range(3)], v, rest)
                tt(stack[0:3 * F1, 0:F1], ident[0:3 * F1, 0:F1], ident[0:3 * F1, F1:2 * F1], ALU.add)
                tt(stack[0:3 * F1, 0:F1], stack[0:3 * F1, 0:F1], ident[0:3 * F1, 2 * F1:3 * F1], ALU.add)
                ts(stack[0:3 * F1, 0:2 * P], stack[0:3 * F1, 0:2 * P], 1.0 / EDGE_PE, ALU.mult)
                dve.sem_inc(s["split_ready"], CREDIT)
                restc = [area((16 + b) * KW, KT * F1).rearrange("p (k f) -> p k f", f=F1) for b in range(2)]
                for l in range(2):
                    nxt = hs1[(l + 1) % 2]

                    def split(c, half):
                        dve.wait_ge(s["t20_ready"], l * NCH + c + 1 + CREDIT)
                        v = PS[:, 4 + half, 0:KT * F1].rearrange("p (k f) -> p k f", f=F1)
                        split3([nxt[:, bass.ds(c * KT, KT), q * F1:(q + 1) * F1] for q in range(3)], v, restc[half])
                        dve.sem_inc(s["split_ready"], 1)

                    def two(m):
                        split(2 * m, 0)
                        split(2 * m + 1, 1)
                    loop(dve, 0, NCH // 2, [(steps, 10)], two)
                if LAYERS > 2:
                    bias_point()
                dve.wait_ge(s["mixed_copied"], 3 * NCH + CREDIT)
                pe_do()
                tt(R, PSrow, A[:, :, :], ALU.add)
                if LAYERS > 2:
                    pe_ask()
                stt(R, R, 0.0, A[:, :, :], ALU.max, ALU.add)
                layer_norm()

            def scale_weights3():
                dve.wait_ge(s["weights3_loaded"], 32)
                stt(absw, W3s, -1.0, W3s, ALU.mult, ALU.max)
                pe_do()
                stt(absw, B3s, -1.0, B3s, ALU.mult, ALU.max)
                stt(hscale, PS[:, 0, 0:P], X_MAX, absw, ALU.mult, ALU.add)
                ts(hscale, hscale, 1.0 / HS, ALU.mult, NO_NEIGHBOUR, ALU.max)
                rec(hscale, hscale)
                pe_ask()
                tt(W3s, W3s, hscale, ALU.mult)
                tt(B3s, B3s, hscale, ALU.mult)
                pe_answer()
                rec(hscale_c, PS[:, 1, 0:1])

            if LAYERS > 2:
                dma_do(False)
                pe_answer()
                link(V.tensor_copy(WT, PS[:, 0, 0:P]))
                link(V.tensor_copy(wv, PS[:, 1, 0:3]))
                pe_ask()
                dots("ss", tiles(A), tiles(A))
                clip_norm(S("n"), "ss")
                radius(S("f"), S("n"))
                tt(S("n"), S("n"), S("f"), ALU.mult)
                artanh(S("at"), S("n"))
                dots("x2", tiles(R), tiles(R), waits=s["proj_copied"])
                tt(S("ss"), S("x2"), S("f"), ALU.mult)
                tt(S("ss"), S("ss"), S("f"), ALU.mult)
                clip_norm(S("m"), "ss")
                rec(S("y1"), S("n"))
                tt(S("y1"), S("y1"), S("m"), ALU.mult)
                tt(S("y1"), S("y1"), S("at"), ALU.mult)
                act_do()
                rec(S("g"), S("m"))
                tt(S("g"), S("g"), S("f"), ALU.mult)
                tt(S("g"), S("g"), S("y0"), ALU.mult)
                ts(S("n"), S("y0"), EPS, ALU.max)
                radius(S("f"), S("n"))
                tt(S("g"), S("g"), S("f"), ALU.mult)
                tt(S("x2"), S("x2"), S("g"), ALU.mult)
                tt(S("x2"), S("x2"), S("g"), ALU.mult)
                dve.wait_ge(s["extra_ready"], 1)
                xv3 = PS[:, 0, 0:3 * NT].rearrange("p (t k) -> p k t", k=3)
                for k, name in enumerate(("xb", "xl", "xr")):
                    ins = V.tensor_copy(S(name), xv3[:, k, :])
                link(ins)
                tt(S("xy"), S("xb"), S("g"), ALU.mult)
                tt(S("xy"), S("xy"), S("gb"), ALU.mult)
                add_weights(S("x2"), S("xy"), S("yy"), S("c1"), S("c2"))
                tt(S("c1"), S("c1"), S("g"), ALU.mult)
                tt(S("c2"), S("c2"), S("gb"), ALU.mult)
                scaled(R, R, "c1")
                by_tiles(tiles(R), lambda t: hbB, "c2", tiles(R))
                squares("ss", R)
                clip_norm(S("n"), "ss")
                radius(S("f"), S("n"))
                tt(R, R, bc(S("f")), ALU.mult)
                tt(S("n"), S("n"), S("f"), ALU.mult)
                artanh(S("at"), S("n"))
                squares("x2", R)
                ts(S("hr"), S("x2"), 1.0, ALU.add)
                rec(S("hr"), S("hr"))
                dve.sem_inc(s["hr_asked"], 1)
                ts(S("b"), S("x2"), -1.0, ALU.mult, 1.0, ALU.add)
                rec(S("ib"), S("b"))
                tt(TMP, R, bc(S("ib")), ALU.mult)
                pe_ask()
                tt(S("kap"), S("x2"), S("ib"), ALU.mult)
                ts(S("ub"), S("x2"), 1.0, ALU.add)
                tt(S("ub"), S("ub"), S("ib"), ALU.mult)
                ts(S("ub"), S("ub"), 0.5 / EDGE8, ALU.mult)
                rec(S("g"), S("n"))
                tt(S("g"), S("g"), S("at"), ALU.mult)
                tt(S("g"), S("g"), S("f"), ALU.mult)
                for name, xs, c_ in (("sc_i", "xl", T1), ("sc_j", "xr", T2)):
                    tt(S(name), S("c1"), S(xs), ALU.mult)
                    stt(S(name), S("c2"), par[:, c_:c_ + 1], S(name), ALU.mult, ALU.add)
                    tt(S(name), S(name), S("g"), ALU.mult)
                ts(S("sc_j"), S("sc_j"), par[:, ATTB:ATTB + 1], ALU.add)
                pe_do()
                tS, tM = augrows
                rest = X2L[:, 7 * P + 64:7 * P + 64 + NT]
                half = X2L[:, 7 * P + 96:7 * P + 96 + 3 * NT // 2].bitcast(BF16).rearrange("p (t k) -> p t k", k=3)
                for k, name in enumerate(("ib", "kap")):
                    o = 6 * k
                    split3([tS[:, :, o], tS[:, :, o + 3], tS[:, :, o + 5]], S(name), rest)
                    for q, at in enumerate((0, 3, 5)):
                        ins = V.tensor_scalar(half[:, :, q], tS[:, :, o + at], -0.5, None, ALU.mult)
                    for to, at in ((1, 0), (2, 0), (4, 3)):
                        ins = V.tensor_copy(tS[:, :, o + to], tS[:, :, o + at])
                    link(ins)
                    V.tensor_copy(tM[:, :, o:o + 3], half)
                    V.tensor_copy(tM[:, :, o + 3:o + 5], half[:, :, 0:2])
                    link(V.tensor_copy(tM[:, :, o + 5], half[:, :, 0]))
                dve.wait_ge(s["row_copied"], 2)
                dma_do(False)
                pe_ask()
                pe_answer()
                pe_answer()
                dve.wait_ge(s["hr_stored"], 16)
                V.tensor_copy(augM[0:AUG, :], aug_ps(1)).then_inc(s["aug_copied"], 1)

                def guard(n, b):
                    dve.wait_ge(s["dist_ready"], n + 1)
                    V.tensor_scalar(wh[b], wh[b], -0.5 * W_FLOOR, None, ALU.min).then_inc(s["guarded_w_ready"], 1)

                def norm(n, b):
                    dve.wait_ge(s["isq_ready"], n + 1)
                    V.scalar_tensor_tensor(out=wh[b], in0=wh[b], scalar=0.5, in1=isq[b],
                                           op0=ALU.add, op1=ALU.mult).then_inc(s["sn_ready"], 1)

                def artanh2(n, b):
                    dve.wait_ge(s["ln1p_ready"], n + 1)
                    V.scalar_tensor_tensor(out=lnw[b], in0=wh[b], scalar=2.0, in1=lnw[b],
                                           op0=ALU.mult, op1=ALU.add).then_inc(s["artanh_ready"], 1)

                def product(m, b):
                    dve.wait_ge(s["artanh_ready"], NB * m + b + 1)
                    dve.wait_ge(s[f"factor_stored{b % 2}"], 16 * (2 * m + b // 2) + 16)
                    V.scalar_tensor_tensor(out=fac[b % 2], in0=lnw[b], scalar=ATANH2_MAX, in1=isq[b],
                                           op0=ALU.min, op1=ALU.mult).then_inc(s["factor_ready"], 1)

                def turns(m, first=False, last=False):
                    for b in range(NB):
                        n = NB * m + b
                        back = not (first and b == 0)
                        if back:
                            artanh2(n - 1, (b - 1) % NB)
                        if not (last and b >= NB - 2):
                            guard(n + 2, (b + 2) % NB)
                        norm(n, b)
                        if back:
                            product(m - 1 if b == 0 else m, (b - 1) % NB)

                for b in range(2):
                    dve.sem_inc(s[f"factor_stored{b}"], 16)
                dve.sem_inc(s["factor_ready"], NB)
                guard(0, 0)
                guard(1, 1)
                dve.wait_ge(s["dma_answered"], 16 * n_dma[0])
                turns(0, first=True)
                loop(dve, 1, NFP // NB - 1, [], turns)
                turns(NFP // NB - 1, last=True)
                artanh2(NFP - 1, NB - 1)
                product(NFP // NB - 1, NB - 1)

                dve.sem_inc(s["tile_weighed"], NW)
                dve.sem_inc(s["u_free"], 1)

                def weigh(c, q, b, factor_of, ready=None):
                    n = c * NP + 2 * q
                    for h in range(2):
                        if ready is not None:
                            dve.wait_ge(s["tf_ready"], ready + h)
                        dve.wait_ge(s["c_used"], n + h + 1)
                        dve.wait_ge(s["c_added"], n + h + 1)
                        for jj in range(2):
                            dve.wait_ge(s["sig_ready"], 2 * (n + h) + jj + 1)
                            V.scalar_tensor_tensor(out=wbuf[2 * b + h][:, jj * CH:(jj + 1) * CH], in0=sig[2 * h + jj],
                                                   scalar=S("ub")[:, bass.ds(4 * q + 2 * h + jj, 1)],
                                                   in1=factor_of(h, jj), op0=ALU.mult, op1=ALU.mult)\
                                .then_inc(s["tile_weighed"], 1)
                    for h in range(2):
                        dve.wait_ge(s["tile_weighed"], 2 * (n + h) + 2 + NW)
                        w = wbuf[2 * b + h].rearrange("p (j x) -> p j x", j=2)
                        V.tensor_tensor(w, w, adjU[:, bass.ds(4 * q + 2 * h, 2), c * CH:(c + 1) * CH], ALU.mult)\
                            .then_inc(s["c_ready"], 1)

                def take_u(c):
                    dve.wait_ge(s["u_ready"], c + 3)
                    V.tensor_copy(S("u")[:, c * KT:(c + 1) * KT], PS[:, 7, 0:KT]).then_inc(s["u_free"], 1)

                for c in range(NCH):
                    def upper(q, b):
                        dve.wait_ge(s[f"factor_in{b}"], 16 * (c * NQ // 2 + 1) + 8 * (q - b))
                        weigh(c, q, b, lambda h, jj: fin[b][:, (2 * h + jj) * CH:(2 * h + jj + 1) * CH])

                    before = sum(2 * (NQ - 1 - k) for k in range(c))

                    def lower(q, b):
                        weigh(c, q, b, lambda h, jj: PS[:, 2 * h + jj, :], before + 2 * (q - c - 1) + 1)

                    def two(m):
                        upper(2 * m, 0)
                        upper(2 * m + 1, 1)

                    def two_lower(m):
                        lower(2 * m, 0)
                        lower(2 * m + 1, 1)
                    if c >= 1:
                        loop(dve, 0, (c + 1) // 2, [], two)
                    if c % 2 == 0:
                        upper(c, 0)
                        lower(c + 1, 1)
                    if c >= 1:
                        take_u(c - 1)
                    if c // 2 + 1 < NQ // 2:
                        loop(dve, c // 2 + 1, NQ // 2, [], two_lower)
                take_u(NCH - 1)
                dve.wait_ge(s["u_free"], NCH + 1)
                ts(S("ib"), S("x2"), 1.0, ALU.add)
                dots("xy", tiles(Trow), tiles(PSrow), waits=s["m_ready"])
                tt(S("xy"), S("xy"), S("ib"), ALU.mult)
                stt(S("g"), S("xy"), 2.0, S("u"), ALU.mult, ALU.subtract)
                tt(S("g"), S("g"), S("ib"), ALU.mult)
                scaled(A, Trow, "g")
                by_tiles(tiles(A), tiles(PSrow), "b", tiles(A))
                squares("ss", A, lambda: dots("xy", tiles(Trow), tiles(A), scratch=R))
                link(V.tensor_copy(S("at"), S("ss")))
                clip_norm(S("n"), "ss")
                ts(S("y2"), S("b"), EPS, ALU.max)
                rec(S("y2"), S("y2"))
                tt(S("y1"), S("y2"), S("n"), ALU.mult)
                act_do()
                rec(S("gb"), S("n"))
                tt(S("gb"), S("gb"), S("y0"), ALU.mult)
                tt(S("yy"), S("gb"), S("gb"), ALU.mult)
                tt(S("yy"), S("yy"), S("at"), ALU.mult)
                tt(S("xy"), S("xy"), S("ib"), ALU.mult)
                tt(S("xy"), S("xy"), S("gb"), ALU.mult)
                add_weights(S("x2"), S("xy"), S("yy"), S("c1"), S("c2"))
                tt(S("c2"), S("c2"), S("gb"), ALU.mult)
                tt(S("c1"), S("c1"), S("ib"), ALU.mult)
                scaled(R, Trow, "c1")
                dma_do(False)
                by_tiles(tiles(R), tiles(A), "c2", tiles(R))
                squares("ss", R)
                clip_norm(S("n"), "ss")
                radius(S("f"), S("n"))
                tt(S("m"), S("n"), S("f"), ALU.mult)
                ts(S("m"), S("m"), EPS, ALU.max)
                artanh(S("at"), S("m"))
                rec(S("g"), S("m"))
                tt(S("g"), S("g"), S("at"), ALU.mult)
                tt(S("g"), S("g"), S("f"), ALU.mult)
                ts(R, R, 0.0, ALU.max)
                squares("ss", R)
                tt(S("ss"), S("ss"), S("g"), ALU.mult)
                tt(S("ss"), S("ss"), S("g"), ALU.mult)
                clip_norm(S("n"), "ss")
                link(V.tensor_copy(S("y1"), S("n")))
                act_do()
                rec(S("y1"), S("n"))
                tt(S("g"), S("g"), S("y1"), ALU.mult)
                tt(S("g"), S("g"), S("y0"), ALU.mult)
                ts(S("n"), S("y0"), EPS, ALU.max)
                radius(S("f"), S("n"))
                tt(S("g"), S("g"), S("f"), ALU.mult)
                if LAYERS > 3:
                    scale_weights3()
                dve.wait_ge(s["dma_answered"], 16 * n_dma[0])
                by_tiles(tiles(R), tiles(R), "g", tiles(Trow))
                layer_norm()

            if LAYERS > 3:
                def masks(c):
                    m = adjU[:, :, bass.ds(c * CH, CH)]
                    link(V.tensor_scalar(m, m, 0.5 * EDGE8, EDGE8, ALU.is_lt, ALU.mult))
                    for k in range(KT):
                        d = adjU[:, bass.ds(c * KT + k, 1), bass.ds(c * CH + k * P, P)]
                        ins = V.tensor_tensor(d, d, not_i[:, :].unsqueeze(1), ALU.mult)
                    ins.then_inc(s["mask_ready"], 1)

                pe_ask()
                masks(0)
                restf = X2[:, 5 * P:9 * P].rearrange("p (k f) -> p k f", f=P)
                Bb = B3s.unsqueeze(1).to_broadcast([P, KT, D])

                def split_h(g):
                    tt(restf, PSrow[:, g * KT:(g + 1) * KT, :], Bb, ALU.add)
                    upper, lower = (hs3[q][:, g * KT:(g + 1) * KT, :] for q in range(2))
                    link(V.tensor_copy(upper, restf))
                    tt(lower, restf, upper, ALU.subtract)
                for g in range(NCH):
                    if g % (NCH // 2) == 0:
                        dve.wait_ge(s["proj_ready"], 3 + g // (NCH // 2))
                    split_h(g)
                    dve.sem_inc(s["part_ready"], 1)

                link(V.memset(par[:, T2:T2 + 1], R_FLOOR))
                rec(par[:, T2:T2 + 1], par[:, T2:T2 + 1])
                rec(par[:, T1:T1 + 1], par[:, MU:MU + 1])
                tt(par[:, T0:T0 + 1], par[:, T2:T2 + 1], par[:, T1:T1 + 1], ALU.subtract)
                act_do()
                tt(par[:, T2:T2 + 1], par[:, SIG:SIG + 1], par[:, SIG:SIG + 1], ALU.mult)
                ts(par[:, T2:T2 + 1], par[:, T2:T2 + 1], -2.0, ALU.mult)
                rec(par[:, T2:T2 + 1], par[:, T2:T2 + 1])
                tt(par[:, T2:T2 + 1], par[:, T2:T2 + 1], par[:, T1:T1 + 1], ALU.mult)
                act_do()

                loop(dve, 1, NCH, [(steps, 1)], masks)
                dve.wait_ge(s["agg3_free"], NCH + CREDIT)
                pe_do()
                ts(par[:, S0:S0 + 1], par[:, S0:S0 + 1], 1.0 / EDGE_PE, ALU.mult)
                stt(R, PSrow, par[:, S0:S0 + 1], A[:, :, :], ALU.mult, ALU.add)
                layer_norm()
            dma_do(False)


_INS = ["x", "adj", "L0_gnn_beta", "L1_gnn_W1", "L1_gnn_b1", "L1_gnn_W2", "L1_gnn_b2", "L1_gnn_W3", "L1_gnn_b3",
        "L2_gnn_W", "L2_gnn_b", "L2_gnn_att_wl", "L2_gnn_att_wr", "L2_gnn_att_b",
        "L3_gnn_W", "L3_gnn_B", "L3_gnn_mu", "L3_gnn_sigma"]
_OUTS = [((4096, 128), "float32")]


def kernel(**inputs):
    import numpy as _np
    import concourse.bacc as _bacc
    from concourse import mybir as _mybir
    from concourse.bass_utils import run_bass_kernel_spmd as _run

    nc = _bacc.Bacc("TRN2", target_bir_lowering=False, num_devices=1)
    arrays, args = {}, []
    for name in _INS:
        a = _np.ascontiguousarray(inputs[name])
        arrays[f"in_{name}_dram"] = a
        args.append(nc.dram_tensor(f"in_{name}_dram", a.shape, _mybir.dt.from_np(a.dtype), kind="ExternalInput").ap())
    for i, (shape, dtype) in enumerate(_OUTS):
        dt = _mybir.dt.from_np(_np.dtype(dtype))
        args.append(nc.dram_tensor(f"out_{i}_dram", shape, dt, kind="ExternalOutput").ap())
    gnn_stack(nc, *args)
    r = _run(nc, [arrays], core_ids=[0])
    return r.results[0]["out_0_dram"]
```
